# Optimizing a Trainium2 kernel written in Bass

```python
import numpy as np
import jax
import jax.numpy as jnp

def _softmax(x, axis=-1):
    return jax.nn.softmax(x, axis=axis)

def _gelu(x):
    return jax.nn.gelu(x, approximate=True)

def _silu(x):
    return jax.nn.silu(x)

def _sigmoid(x):
    return jax.nn.sigmoid(x)

def _layernorm(x, axis=-1, eps=1e-05):
    m = jnp.mean(x, axis=axis, keepdims=True)
    v = jnp.var(x, axis=axis, keepdims=True)
    return (x - m) / jnp.sqrt(v + eps)

def _scatter_add(tgt, idx, src, axis=0):
    return tgt.at[idx].add(src)

def _segment_sum(src, seg, n):
    return jax.ops.segment_sum(src, seg, n)
kernel_name = 'mk_seq_preln_d1_jaxref_r4_0dbe1c'

def setup_inputs(seed: int=0):
    np.random.seed(seed)
    _w = jnp.asarray

    def _L0_attn_setup():
        import jax, jax.numpy as jnp
        import numpy as np
        import math
        D_MODEL = 256
        NUM_HEADS = 16
        HEAD = D_MODEL // NUM_HEADS
        EPS = 1e-05

        def _layernorm(x, w, b):
            mean = jnp.mean(x, axis=-1, keepdims=True)
            var = jnp.var(x, axis=-1, keepdims=True)
            return (x - mean) * w / jnp.sqrt(var + EPS) + b
        key = jax.random.key(seed)
        ks = jax.random.split(key, 5)
        x = jax.random.normal(ks[0], (2, 512, D_MODEL), dtype=jnp.float32)
        wq = jax.random.uniform(ks[1], (NUM_HEADS, D_MODEL, HEAD), dtype=jnp.float32) * 0.02
        wk = jax.random.uniform(ks[2], (NUM_HEADS, D_MODEL, HEAD), dtype=jnp.float32) * 0.02
        wv = jax.random.uniform(ks[3], (NUM_HEADS, D_MODEL, HEAD), dtype=jnp.float32) * 0.02
        wo = jax.random.uniform(ks[4], (D_MODEL, D_MODEL), dtype=jnp.float32) * 0.02
        ln_w = jnp.ones((D_MODEL,), dtype=jnp.float32)
        ln_b = jnp.zeros((D_MODEL,), dtype=jnp.float32)
        return {'x': x, 'ln_w': ln_w, 'ln_b': ln_b, 'wq': wq, 'wk': wk, 'wv': wv, 'wo': wo}
    _L0_attn_in = _L0_attn_setup()

    def _L0_ffn_setup():
        import jax, jax.numpy as jnp
        import numpy as np
        B, T, E, C, H, G = (2, 512, 8, 256, 512, 16)
        key = jax.random.key(seed)
        ks = jax.random.split(key, 7)
        return {'hidden_states': jax.random.normal(ks[0], (B, T, C), jnp.float32), 'w_red': jax.random.normal(ks[1], (C, G), jnp.float32) * 0.02, 'wg': jax.random.normal(ks[2], (E, G), jnp.float32), 'W1': jax.random.normal(ks[3], (E, C, H), jnp.float32) * 0.02, 'b1': jax.random.normal(ks[4], (E, H), jnp.float32) * 0.02, 'W2': jax.random.normal(ks[5], (E, H, C), jnp.float32) * 0.02, 'b2': jax.random.normal(ks[6], (E, C), jnp.float32) * 0.02}
    _L0_ffn_in = _L0_ffn_setup()
    _d = {'L0_attn_x': _L0_attn_in['x'], 'L0_attn_ln_w': _L0_attn_in['ln_w'], 'L0_attn_ln_b': _L0_attn_in['ln_b'], 'L0_attn_wq': _L0_attn_in['wq'], 'L0_attn_wk': _L0_attn_in['wk'], 'L0_attn_wv': _L0_attn_in['wv'], 'L0_attn_wo': _L0_attn_in['wo'], 'L0_ffn_w_red': _L0_ffn_in['w_red'], 'L0_ffn_wg': _L0_ffn_in['wg'], 'L0_ffn_W1': _L0_ffn_in['W1'], 'L0_ffn_b1': _L0_ffn_in['b1'], 'L0_ffn_W2': _L0_ffn_in['W2'], 'L0_ffn_b2': _L0_ffn_in['b2']}
    _x0 = _d['L0_attn_x']
    _d['L0_attn_x'] = jax.random.normal(jax.random.fold_in(jax.random.key(seed), 1), (8, 1024, 256), dtype=_x0.dtype)
    del _x0
    return _d

def reference(L0_attn_x, L0_attn_ln_w, L0_attn_ln_b, L0_attn_wq, L0_attn_wk, L0_attn_wv, L0_attn_wo, L0_ffn_w_red, L0_ffn_wg, L0_ffn_W1, L0_ffn_b1, L0_ffn_W2, L0_ffn_b2):

    def _L0_attn_ref(x, ln_w, ln_b, wq, wk, wv, wo):
        import jax, jax.numpy as jnp
        import numpy as np
        import math
        D_MODEL = 256
        NUM_HEADS = 16
        HEAD = D_MODEL // NUM_HEADS
        EPS = 1e-05

        def _layernorm(x, w, b):
            mean = jnp.mean(x, axis=-1, keepdims=True)
            var = jnp.var(x, axis=-1, keepdims=True)
            return (x - mean) * w / jnp.sqrt(var + EPS) + b
        y = _layernorm(x, ln_w, ln_b)
        seq_len = y.shape[-2]
        q = jnp.einsum('bsd,hde->bhse', y, wq)
        k = jnp.einsum('bsd,hde->bhse', y, wk)
        v = jnp.einsum('bsd,hde->bhse', y, wv)
        scores = jnp.einsum('bhse,bhte->bhst', q, k) / math.sqrt(HEAD)
        causal = jnp.triu(jnp.full((seq_len, seq_len), -jnp.inf, dtype=scores.dtype), k=1)
        scores = scores + causal
        weights = jax.nn.softmax(scores, axis=-1)
        attn = jnp.einsum('bhst,bhte->bshe', weights, v)
        attn = attn.reshape(*attn.shape[:-2], -1)
        out = attn @ wo
        return out + x

    def _L0_ffn_ref(hidden_states, w_red, wg, W1, b1, W2, b2):
        import jax, jax.numpy as jnp
        import numpy as np
        B, T, E, C, H, G = (2, 512, 8, 256, 512, 16)
        b, t, c = hidden_states.shape
        x = hidden_states.reshape(-1, c)
        x_red = x @ w_red
        wg_n = wg / jnp.maximum(jnp.linalg.norm(wg, axis=1, keepdims=True), 0.0001)
        logits = x_red @ wg_n.T
        gates = jax.nn.softmax(logits, axis=1)
        scores = jnp.max(gates, axis=1)
        idx = jnp.argmax(gates, axis=1)
        h = jnp.einsum('nc,ech->neh', x, W1) + b1[None]
        h = jnp.take_along_axis(h, idx[:, None, None], axis=1)[:, 0, :]
        h = jax.nn.gelu(h, approximate=False)
        o = jnp.einsum('nh,ehc->nec', h, W2) + b2[None]
        o = jnp.take_along_axis(o, idx[:, None, None], axis=1)[:, 0, :]
        o = o * scores[:, None]
        return o.reshape(b, t, c)
    x = L0_attn_x
    x = x + _L0_attn_ref(_layernorm(x, axis=-1), L0_attn_ln_w, L0_attn_ln_b, L0_attn_wq, L0_attn_wk, L0_attn_wv, L0_attn_wo)
    x = x + _L0_ffn_ref(_layernorm(x, axis=-1), L0_ffn_w_red, L0_ffn_wg, L0_ffn_W1, L0_ffn_b1, L0_ffn_W2, L0_ffn_b2)
    return x

_drawn_inputs = setup_inputs


def setup_inputs(seed=0):
    import zlib

    import numpy as np

    out = dict(_drawn_inputs(seed))
    spreads = {'L0_attn_ln_w': (1.0, 0.6), 'L0_attn_ln_b': (0.0, 0.404)}
    factors = {'L0_attn_wq': 8.0,
     'L0_attn_wk': 8.0,
     'L0_attn_wv': 8.0,
     'L0_attn_wo': 8.0,
     'L0_ffn_w_red': 7.83,
     'L0_ffn_wg': 7.818,
     'L0_ffn_W1': 7.767,
     'L0_ffn_b1': 64.0,
     'L0_ffn_W2': 7.547,
     'L0_ffn_b2': 200.0}
    for name, (base, spread) in spreads.items():
        noise = np.random.default_rng([zlib.crc32(name.encode()), seed]).standard_normal(out[name].shape)
        drawn = base * np.exp(spread * noise) if base else spread * noise
        out[name] = jnp.asarray(drawn.astype(out[name].dtype))
    for name, factor in factors.items():
        out[name] = (out[name] * factor).astype(out[name].dtype)
    return out
```

```python
from contextlib import ExitStack

import concourse.bass as bass
from concourse import mybir

P = 128
F32 = mybir.dt.float32
BF16 = mybir.dt.bfloat16
I32 = mybir.dt.int32
U32 = mybir.dt.uint32
ALU = mybir.AluOpType
ACT = mybir.ActivationFunctionType
X = mybir.AxisListType.X

B, S, D = 8, 1024, 256
H, HD = 16, 16
NTOK = B * S
DK = D // P
E, FF, RED = 8, 512, 16
FK = FF // P
EPS = 1e-5

CH = 512
CT = CH // P
NCH = NTOK // CH

PARTS = 3
GH = 4
GROUPS = B * H // GH
PAIRS = GROUPS // 2
ST = S // P
VW = 32
Q_ROWS = [(0, 3), (1, 2), (2, 1)]
KROWS = 6 * HD
MROWS = KROWS + PARTS
MASK = -1e30

REGION = NTOK + P
ROWW = D + 4
TILES = NTOK // P + E
NOWHERE = NTOK + P


def lin(i, u, n, k, q=0):
    return i * (n * k) + (u * k + q)


def wait(eng, sem, value):
    if isinstance(value, int) and value <= 0:
        return
    eng.wait_ge(sem, value)


def wait_alone(eng, sem, value, passed):
    wait(eng, sem, value)
    if not isinstance(value, int):
        eng.sem_inc(passed, 1)


def build(nc, x, ln_w, ln_b, wq, wk, wv, wo, w_red, wg, W1, b1, W2, b2, out):
    qparts = nc.dram_tensor("qparts", (PARTS, PAIRS, P, S), BF16, kind="Internal").ap()
    kparts = nc.dram_tensor("kparts", (PARTS, PAIRS, P, S), BF16, kind="Internal").ap()
    vrows = nc.dram_tensor("vrows", (PAIRS, S, H // 2 * VW), F32, kind="Internal").ap()
    xz_dram = nc.dram_tensor("xz_dram", (NCH, CH, D), F32, kind="Internal").ap()
    attn_dram = nc.dram_tensor("attn_dram", (PAIRS, S, P), F32, kind="Internal").ap()
    dealt = nc.dram_tensor("dealt", (E * REGION + P, ROWW), F32, kind="Internal").ap()

    with ExitStack() as ctx:
        def sb(name, shape, dt=F32):
            return ctx.enter_context(nc.sbuf_tensor(name, shape, dt))

        def sem(name):
            return ctx.enter_context(nc.semaphore(name))

        psum = ctx.enter_context(nc.psum_tensor("psum", [P, 8, 512], F32))
        c = dict(
            ident=sb("ident", [P, P]), identb=sb("identb", [P, P], BF16),
            mask=sb("mask", [P, P], BF16), below=sb("below", [P, P], BF16), ones=sb("ones", [P, P], BF16),
            lnw=sb("lnw", [P, DK]), lnb=sb("lnb", [P, DK]), minus_half=sb("minus_half", [P, CT]),
            counts=sb("counts", [P, E]), wr=sb("wr", [P, DK, E]), wo=sb("wo_sb", [P, DK, D]),
        )
        w1 = sb("w1_sb", [P, E * DK * FF])
        w2 = sb("w2_sb", [P, E * FK * D])
        tile_row = sb("tile_row", [1, TILES], I32)
        tile_expert = sb("tile_expert", [1, TILES], I32)
        s_weights, s_wo = sem("s_weights"), sem("s_wo")
        projections(nc, psum, c, s_wo, x, ln_w, ln_b, wq, wk, wv, wo, w_red, wg,
                    qparts, kparts, vrows, xz_dram)
        attention(nc, psum, c, qparts, kparts, vrows, attn_dram, W1, W2, w1, w2, s_weights)
        routing(nc, psum, c, s_wo, attn_dram, xz_dram, dealt, tile_row, tile_expert)
        mlp(nc, psum, c["ident"], s_weights, w1, w2, tile_row, tile_expert, b1, b2, dealt, out)


def projections(nc, psum, c, s_wo, x, ln_w, ln_b, wq, wk, wv, wo, w_red, wg,
                qparts, kparts, vrows, xz_dram):
    with ExitStack() as ctx:
        def sb(name, shape, dt=F32):
            return ctx.enter_context(nc.sbuf_tensor(name, shape, dt))

        def sem(name):
            return ctx.enter_context(nc.semaphore(name))

        ident, identb, mask, below, ones = c["ident"], c["identb"], c["mask"], c["below"], c["ones"]
        lnw, lnb, minus_half = c["lnw"], c["lnb"], c["minus_half"]
        wqkv = sb("wqkv", [P, 3, DK, D])
        xt = sb("xt", [P, 2, CT, D])
        z = sb("z", [P, 2, CT, D])
        yn = sb("yn", [P, 2, CT, D])
        xz = sb("xz", [P, 2, CT, D])
        yT = sb("yT", [P, 2, DK, CH])
        parts = sb("parts", [P, 2, 4, PARTS, CH], BF16)
        rest = sb("rest", [P, 4, CH])
        vsb = sb("vsb", [P, 2, CT, H, VW])
        stats = sb("stats", [P, CT, 6])
        mv = sb("mv", [P, 2, 2, CT, 2])
        ve = sb("ve", [P, 2, 2, CT])
        rstd = sb("rstd", [P, 2, 2, CT])
        wgs = sb("wgs", [E, RED])
        wgq = sb("wgq", [E, RED])
        wgn = sb("wgn", [E, 4])
        wgT = sb("wgT", [RED, E])
        wred = sb("wred", [P, DK, RED])
        wredT = sb("wredT", [RED, DK, P])

        s_const, s_cst2, s_load, s_w = sem("s_const"), sem("s_cst2"), sem("s_load"), sem("s_w")
        s_router, s_rc, s_rp = sem("s_router"), sem("s_rc"), sem("s_rp")
        s_vinit = sem("s_vinit")
        x_in = [sem(f"x_in{u}") for u in range(2)]
        var_ready, rstd_ready, ve_ready = sem("var_ready"), sem("rstd_ready"), sem("ve_ready")
        stats_ready, z_ready, yn_ready = sem("stats_ready"), sem("z_ready"), sem("yn_ready")
        xz_ready = sem("xz_ready")
        xz_out = [sem(f"xz_out{u}") for u in range(2)]
        turned, yT_ready = sem("turned"), sem("yT_ready")
        qk_ready, v_ready = sem("qk_ready"), sem("v_ready")
        part1, rest_ready, part2, part3 = sem("part1"), sem("rest_ready"), sem("part2"), sem("part3")
        v_copied = sem("v_copied")
        parts_out = [sem(f"parts_out{u}") for u in range(2)]
        v_out = [sem(f"v_out{u}") for u in range(2)]

        block = ctx.enter_context(nc.Block())
        N2 = NCH // 2

        @block.sync
        def _(sp):
            def load_x(i, u):
                sp.dma_start(xt[:, u], x[bass.ds(lin(i, u, 2, 1), 1)].rearrange("o (t p) d -> p (o t) d", p=P)
                             ).then_inc(x_in[u], 16)

            def chunk(i, u, last=False):
                wait(sp, xz_ready, lin(i, u, 2, 1, 1))
                sp.dma_start(xz_dram[bass.ds(lin(i, u, 2, 1), 1)].rearrange("o (t p) d -> p (o t) d", p=P),
                             xz[:, u]).then_inc(xz_out[u], 16)
                if not last:
                    load_x(i + 1, u)
                for m in range(4):
                    wait(sp, part3, lin(i, u, 2, 4, m + 1))
                    dst = (qparts if m < 2 else kparts)[:, bass.ds(i + (m % 2) * B, 1), :, u * CH:(u + 1) * CH]
                    sp.dma_start(dst.rearrange("a o p n -> p (o a) n"), parts[:, u, m]).then_inc(parts_out[u], 16)
                wait(sp, v_copied, lin(i, u, 2, 2, 2))
                for half in range(2):
                    dst = vrows[bass.ds(i + half * B, 1), u * CH:(u + 1) * CH]
                    sp.dma_start(dst.rearrange("o (t p) n -> p (o t) n", p=P),
                                 vsb[:, u, :, half * 8:half * 8 + 8, :].rearrange("p t h w -> p t (h w)")
                                 ).then_inc(v_out[u], 16)

            load_x(0, 0)
            load_x(0, 1)
            for u in range(2):
                chunk(0, u)
            with sp.Fori(1, N2 - 1) as i:
                for u in range(2):
                    chunk(i, u)
            for u in range(2):
                chunk(N2 - 1, u, last=True)
            for u in range(2):
                sp.wait_ge(xz_out[u], 16 * N2)
                sp.wait_ge(parts_out[u], 64 * N2)
                sp.wait_ge(v_out[u], 32 * N2)

        @block.gpsimd
        def _(pool):
            passed = sem("pool_passed1")
            pool.memset(ident[:, :], 0.0).then_inc(s_const, 1)
            pool.memset(minus_half[:, :], -0.5).then_inc(s_const, 1)
            pool.memset(mask[:, :], 0.0).then_inc(s_const, 1)
            pool.memset(ones[:, :], 1.0).then_inc(s_const, 1)
            pool.memset(c["counts"][:, :], 0.0).then_inc(s_const, 1)
            pool.wait_ge(s_const, 5)
            pool.affine_select(out=ident[:, :], in_=ident[:, :], compare_op=ALU.not_equal, fill=1.0, base=0,
                               pattern=[[-1, P]], channel_multiplier=1).then_inc(s_const, 1)
            pool.affine_select(out=mask[:, :], in_=mask[:, :], compare_op=ALU.is_ge, fill=MASK, base=0,
                               pattern=[[-1, P]], channel_multiplier=1).then_inc(s_const, 1)
            pool.affine_select(out=below[:, :], in_=ones[:, :], compare_op=ALU.is_gt, fill=0.0, base=0,
                               pattern=[[1, P]], channel_multiplier=-1).then_inc(s_const, 1)
            pool.memset(vsb[:, :, :, :, HD:VW], 0.0).then_inc(s_vinit, 1)
            pool.wait_ge(s_const, 8)
            pool.tensor_copy(identb[:, :], ident[:, :]).then_inc(s_const, 1)
            pool.wait_ge(s_vinit, 1)
            pool.memset(vsb[:, :, :, :, HD:HD + 1], 1.0).then_inc(s_vinit, 1)
            pool.wait_ge(s_rc, 1)
            pool.tensor_tensor(wgn[:, 1:2], wgn[:, 0:1], wgn[:, 3:4], ALU.pow).then_inc(s_rp, 1)

            def chunk(i, u):
                for norm in range(2):
                    wait_alone(pool, var_ready, lin(i, u, 2, 2, norm + 1), passed)
                    pool.tensor_scalar(ve[:, u, norm], mv[:, u, norm, :, 1], EPS, None, ALU.add).then_inc(ve_ready, 1)
                    wait(pool, ve_ready, lin(i, u, 2, 2, norm + 1))
                    pool.tensor_tensor(rstd[:, u, norm], ve[:, u, norm], minus_half[:, :], ALU.pow).then_inc(rstd_ready, 1)
                wait(pool, xz_out[u], lin(i, 0, 1, 16))
                wait(pool, z_ready, lin(i, u, 2, 1, 1))
                pool.tensor_tensor(xz[:, u], xt[:, u], z[:, u], ALU.add).then_inc(xz_ready, 1)

            for u in range(2):
                chunk(0, u)
            with pool.Fori(1, N2) as i:
                for u in range(2):
                    chunk(i, u)

        @block.vector
        def _(dve):
            passed = sem("dve_passed4")
            dve.memset(wgn[:, 3:4], 0.5).then_inc(s_cst2, 1)
            dve.wait_ge(s_cst2, 1)
            dve.wait_ge(s_router, 32)
            dve.tensor_tensor_reduce(wgq[:, :], wgs[:, :], wgs[:, :], 1.0, 0.0, ALU.mult, ALU.add,
                                     wgn[:, 0:1]).then_inc(s_rc, 1)
            dve.wait_ge(s_rp, 1)
            dve.tensor_scalar(wgn[:, 2:3], wgn[:, 1:2], 1e-4, None, ALU.max).then_inc(s_rc, 1)
            dve.wait_ge(s_rc, 2)
            dve.reciprocal(wgn[:, 0:1], wgn[:, 2:3]).then_inc(s_rc, 1)
            dve.wait_ge(s_rc, 3)
            dve.tensor_scalar(wgq[:, :], wgs[:, :], wgn[:, 0:1], None, ALU.mult).then_inc(s_rc, 1)
            dve.wait_ge(s_rp, 2)
            dve.tensor_copy(wgT[:, :], psum[0:RED, 0, 0:E]).then_inc(s_rc, 1)
            dve.tensor_copy(wredT[:, :, :], psum[0:RED, 1, 0:DK * P].rearrange("r (k p) -> r k p", k=DK)
                            ).then_inc(s_rc, 1)
            dve.wait_ge(s_rp, 3)
            dve.tensor_copy(c["wr"][:, :, :], psum[:, 2, 0:DK * E].rearrange("p (k e) -> p k e", k=DK)
                            ).then_inc(s_rc, 1)

            def norms(i, u):
                wait(dve, x_in[u], lin(i, 0, 1, 16, 16))
                wait(dve, xz_ready, lin(i, u, 2, 1, -1))
                for norm, (src, dst) in enumerate(((xt, z), (z, yn))):
                    for t in range(CT):
                        last = dve.bn_stats(stats[:, t], src[:, u, t])
                    last.then_inc(stats_ready, 1)
                    wait_alone(dve, stats_ready, lin(i, u, 2, 2, norm + 1), passed)
                    for t in range(CT):
                        last = dve.bn_aggr(mv[:, u, norm, t], stats[:, t])
                    last.then_inc(var_ready, 1)
                    wait(dve, rstd_ready, lin(i, u, 2, 2, norm + 1))
                    if norm:
                        wait(dve, turned, lin(i, u, 2, 1, -1))
                    for t in range(CT):
                        last = dve.tensor_scalar(dst[:, u, t], src[:, u, t], mv[:, u, norm, t, 0:1],
                                                 rstd[:, u, norm, t:t + 1], ALU.subtract, ALU.mult)
                    if norm == 0:
                        last.then_inc(z_ready, 1)
                        wait(dve, z_ready, lin(i, u, 2, 1, 1))
                    else:
                        last.then_inc(yn_ready, 1)

            def split(i, u):
                def second(m):
                    wait(dve, part1, lin(i, u, 2, 4, m + 1))
                    dve.tensor_tensor(rest[:, m], psum[:, m], parts[:, u, m, 0], ALU.subtract).then_inc(rest_ready, 1)

                def third(m):
                    wait(dve, part2, lin(i, u, 2, 4, m + 1))
                    dve.tensor_tensor(parts[:, u, m, 2], rest[:, m], parts[:, u, m, 1], ALU.subtract).then_inc(part3, 1)

                second(0)
                second(1)
                third(0)
                second(2)
                third(1)
                second(3)
                third(2)
                third(3)
                for half in range(2):
                    wait(dve, v_ready, lin(i, u, 2, 2, half + 1))
                    if half == 0:
                        wait(dve, v_out[u], lin(i, 0, 1, 32))
                    dve.tensor_copy(vsb[:, u, 2 * half:2 * half + 2, :, 0:HD],
                                    psum[:, 4 + half].rearrange("p (t h d) -> p t h d", t=2, d=HD)
                                    ).then_inc(v_copied, 1)

            norms(0, 0)
            dve.wait_ge(s_vinit, 2)
            norms(0, 1)
            split(0, 0)
            with dve.Fori(1, N2) as i:
                norms(i, 0)
                split(i - 1, 1)
                norms(i, 1)
                split(i, 0)
            split(N2 - 1, 1)

        @block.scalar
        def _(act):
            act.dma_start(wgs[:, :], wg).then_inc(s_router, 16)
            act.dma_start(wred[:, :, :], w_red.rearrange("(k p) r -> p k r", p=P)).then_inc(s_router, 16)
            act.dma_start(lnw[:, :], ln_w.rearrange("(k p) -> p k", p=P), allow_slow_non_contiguous=True).then_inc(s_load, 16)
            act.dma_start(lnb[:, :], ln_b.rearrange("(k p) -> p k", p=P), allow_slow_non_contiguous=True).then_inc(s_load, 16)
            for n, w in enumerate((wq, wk, wv)):
                for k in range(DK):
                    act.dma_start(wqkv[:, n, k].rearrange("p (h e) -> p h e", h=H),
                                  w[:, k * P:(k + 1) * P, :].rearrange("h p e -> p h e")).then_inc(s_w, 16)
            act.dma_start(c["wo"][:, :, :], wo.rearrange("(k p) d -> p k d", p=P)).then_inc(s_wo, 16)

            def evacuate(i, u):
                wait(act, turned, lin(i, u, 2, 1, 1))
                for k in range(DK):
                    last = act.activation(yT[:, u, k], psum[:, 6 + k], ACT.Identity, bias=lnb[:, k:k + 1],
                                          scale=lnw[:, k:k + 1])
                last.then_inc(yT_ready, 1)

            def split(i, u):
                def first(m):
                    wait(act, qk_ready, lin(i, u, 2, 4, m + 1))
                    act.activation(parts[:, u, m, 0], psum[:, m], ACT.Copy).then_inc(part1, 1)

                def second(m):
                    wait(act, rest_ready, lin(i, u, 2, 4, m + 1))
                    act.activation(parts[:, u, m, 1], rest[:, m], ACT.Copy).then_inc(part2, 1)

                wait(act, parts_out[u], lin(i, 0, 1, 64))
                first(0)
                first(1)
                second(0)
                first(2)
                second(1)
                first(3)
                second(2)
                second(3)

            act.wait_ge(s_load, 32)
            evacuate(0, 0)
            split(0, 0)
            evacuate(0, 1)
            with act.Fori(1, N2) as i:
                split(i - 1, 1)
                evacuate(i, 0)
                split(i, 0)
                evacuate(i, 1)
            split(N2 - 1, 1)

        @block.tensor
        def _(pe):
            pe.wait_ge(s_const, 9)
            pe.wait_ge(s_rc, 4)
            pe.wait_ge(s_router, 32)
            pe.transpose(psum[0:RED, 0, 0:E], wgq[:, :], ident[0:E, 0:E])
            for k in range(DK):
                last = pe.transpose(psum[0:RED, 1, k * P:(k + 1) * P], wred[:, k], ident[:, :])
            last.then_inc(s_rp, 1)
            pe.wait_ge(s_rc, 6)
            for k in range(DK):
                last = pe.matmul(psum[:, 2, k * E:(k + 1) * E], wredT[:, k], wgT[:, :], start=True, stop=True)
            last.then_inc(s_rp, 1)
            pe.wait_ge(s_rc, 7)

            def turn(i, u):
                wait(pe, yn_ready, lin(i, u, 2, 1, 1))
                wait(pe, yT_ready, lin(i, u, 2, 1))
                for k in range(DK):
                    for t in range(CT):
                        last = pe.transpose(psum[:, 6 + k, t * P:(t + 1) * P], yn[:, u, t, k * P:(k + 1) * P],
                                            ident[:, :])
                last.then_inc(turned, 1)

            def project(i, u):
                wait(pe, yT_ready, lin(i, u, 2, 1, 1))
                for m in range(4):
                    wait(pe, rest_ready, lin(i, u, 2, 4, m - 3))
                    for k in range(DK):
                        last = pe.matmul(psum[:, m], wqkv[:, m // 2, k, (m % 2) * P:(m % 2 + 1) * P],
                                         yT[:, u, k], start=(k == 0), stop=(k == DK - 1))
                    last.then_inc(qk_ready, 1)
                for t in range(CT):
                    if t % 2 == 0:
                        wait(pe, v_copied, lin(i, u, 2, 2, t // 2 - 1))
                    for k in range(DK):
                        last = pe.matmul(psum[:, 4 + t // 2, (t % 2) * D:(t % 2 + 1) * D],
                                         yT[:, u, k, t * P:(t + 1) * P], wqkv[:, 2, k],
                                         start=(k == 0), stop=(k == DK - 1))
                    if t % 2:
                        last.then_inc(v_ready, 1)

            turn(0, 0)
            pe.wait_ge(s_w, 96)
            project(0, 0)
            turn(0, 1)
            with pe.Fori(1, N2) as i:
                project(i - 1, 1)
                turn(i, 0)
                project(i, 0)
                turn(i, 1)
            project(N2 - 1, 1)


UNITS = [(0, j) for j in range(4)] + [(1, j) for j in range(8)]
ITEMS = [(0, 0, 4), (1, 0, 4)] + [(i, h, 2) for i in (2, 3) for h in (0, 2)] + [
    (i, h, 1) for i in range(4, 8) for h in range(4)]
SHARE = [3, 3, 3, 3, 3, 2, 2, 3]
assert sum(SHARE) == len(ITEMS)
NU, NI = len(UNITS), len(ITEMS)
GU = 4
NG = GROUPS // GU


def columns(c, j):
    return CH - max(0, j - 4 * c) * P


def attention(nc, psum, c, qparts, kparts, vrows, attn_dram, W1, W2, w1, w2, s_weights):
    with ExitStack() as ctx:
        def sb(name, shape, dt=F32):
            return ctx.enter_context(nc.sbuf_tensor(name, shape, dt))

        def sem(name):
            return ctx.enter_context(nc.semaphore(name))

        ident, identb, mask = c["ident"], c["identb"], c["mask"]
        qst = sb("qst", [P, GU, GH, S], BF16)
        kst = sb("kst", [P, GU, GH, S], BF16)
        vst = sb("vst", [P, 2, ST, GH * VW])
        pT = sb("pT", [P, 3, GH, CH])
        oT = sb("oT", [P, 2, CH])
        mneg = sb("mneg", [P, 2, GH * ST])
        mparts = sb("mparts", [GH * ST, 2, PARTS, P], BF16)
        mrest = sb("mrest", [GH * ST, P])
        rsum = sb("rsum", [P, 2, CT, GH])
        attn = sb("attn", [P, 2, ST, P])

        s_ones = sem("s_ones")
        stack_in = [sem(f"stack_in{g}") for g in range(GU)]
        v_in = [sem(f"v_in{g}") for g in range(2)]
        m_in = sem("m_in")
        attn_out = [sem(f"attn_out{g}") for g in range(2)]
        smax_ready, max_done = sem("smax_ready"), sem("max_done")
        m_turned, m_split, m_chain = sem("m_turned"), sem("m_split"), sem("m_chain")
        st_ready, exp_done, masked, pv_done = sem("st_ready"), sem("exp_done"), sem("masked"), sem("pv_done")
        oT_ready, o_turned, normed, rsum_ready = sem("oT_ready"), sem("o_turned"), sem("normed"), sem("rsum_ready")

        block = ctx.enter_context(nc.Block())

        def over_groups(eng, group):
            for g in range(GU):
                group(0, g)
            with eng.Fori(1, NG - 1) as i:
                for g in range(GU):
                    group(i, g)
            for g in range(GU):
                group(NG - 1, g, last=(g == GU - 1))

        @block.sync
        def _(sp):
            def load_stack(i, g):
                i, g = i + g // GU, g % GU
                pair, h0 = lin(i, g // 2, 2, 1), (g % 2) * GH * HD
                heads = slice(h0, h0 + GH * HD)
                row = 0
                for part, times in Q_ROWS:
                    for k in range(times):
                        src = qparts[part, bass.ds(pair, 1), heads].rearrange("o (h e) n -> e (o h) n", e=HD)
                        sp.dma_start(qst[row + k * HD:row + (k + 1) * HD, g], src).then_inc(stack_in[g], 16)
                        src = kparts[k, bass.ds(pair, 1), heads].rearrange("o (h e) n -> e (o h) n", e=HD)
                        sp.dma_start(kst[row + k * HD:row + (k + 1) * HD, g], src).then_inc(stack_in[g], 16)
                    row += times * HD

            def load_v(i, g):
                i, g = i + g // GU, g % GU
                src = vrows[bass.ds(lin(i, g // 2, 2, 1), 1), :, (g % 2) * GH * VW:(g % 2 + 1) * GH * VW]
                sp.dma_start(vst[:, g % 2], src.rearrange("o (t p) n -> p (o t) n", p=P)).then_inc(v_in[g % 2], 16)

            def load_max(i, g):
                wait(sp, m_split, lin(i, g, GU, 1, 1))
                i, g = i + g // GU, g % GU
                for part in range(PARTS):
                    row = KROWS + part
                    sp.dma_start(qst[row:row + 1, g].rearrange("o h (t n) -> o (h t) n", n=P),
                                 mparts[:, g % 2, part]).then_inc(m_in, 16)

            def store(i, g):
                wait(sp, normed, lin(i, g, GU, 2))
                pair = lin(i, g // 2, 2, 1, -1)
                buf = (g // 2 + 1) % 2
                sp.dma_start(attn_dram[bass.ds(pair, 1)].rearrange("o (t p) n -> p (o t) n", p=P),
                             attn[:, buf]).then_inc(attn_out[buf], 16)

            def group(i, g, last=False):
                wait(sp, pv_done, lin(i, g, GU, NU))
                if not last:
                    load_v(i, g + 1)
                if not (isinstance(i, int) and i * GU + g + 2 >= GROUPS):
                    load_stack(i, g + 2)
                if g % 2 == 0 and not (isinstance(i, int) and i * GU + g == 0):
                    store(i, g)
                if not last:
                    load_max(i, g + 1)

            sp.wait_ge(s_ones, 1)
            load_stack(0, 0)
            load_v(0, 0)
            load_stack(0, 1)
            load_max(0, 0)
            over_groups(sp, group)
            store(NG, 0)
            for buf in range(2):
                sp.wait_ge(attn_out[buf], 16 * NG)

        @block.gpsimd
        def _(pool):
            passed = sem("pool_passed7")
            pool.memset(kst[96:MROWS], 1.0).then_inc(s_ones, 1)

            def group(i, g, last=False):
                diagonal = 0
                for n, (half, j) in enumerate(UNITS):
                    if j < 4 * half:
                        continue
                    wait_alone(pool, exp_done, lin(i, g, GU, NU * GH, (n + 1) * GH), passed)
                    part = pT[:, n % 3, :, 0:P]
                    pool.affine_select(out=part, in_=part, compare_op=ALU.is_ge, fill=0.0, base=0,
                                       pattern=[[0, GH], [1, P]], channel_multiplier=-1).then_inc(masked, 1)
                    diagonal += 1

            over_groups(pool, group)

        @block.scalar
        def _(act):
            def evacuate(i, g, half):
                wait(act, pv_done, lin(i, g, GU, NU, 4 + 8 * half))
                wait(act, o_turned, lin(i, g, GU, 2, half - 1))
                act.activation(oT[:, half], psum[:, 6], ACT.Copy).then_inc(oT_ready, 1)

            def group(i, g, last=False):
                for n, (half, j) in enumerate(UNITS):
                    cols = columns(half, j)
                    wait(act, pv_done, lin(i, g, GU, NU, n - 2))
                    for h in range(GH):
                        wait(act, st_ready, lin(i, g, GU, NU * GH, n * GH + h + 1))
                        act.activation(pT[:, n % 3, h, 0:cols], psum[:, 4 + h % 2, 0:cols], ACT.Exp,
                                       scale=HD ** -0.5).then_inc(exp_done, 1)
                    if n == 0 and not (isinstance(i, int) and i * GU + g == 0):
                        evacuate(i, g - 1, 1)
                    if n == 4:
                        evacuate(i, g, 0)

            act.dma_start(w1[:, :].rearrange("p (e k f) -> p e k f", e=E, k=DK),
                          W1.rearrange("e (k p) f -> p e k f", p=P)).then_inc(s_weights, 16)
            act.dma_start(w2[:, :].rearrange("p (e k f) -> p e k f", e=E, k=FK),
                          W2.rearrange("e (k p) f -> p e k f", p=P)).then_inc(s_weights, 16)
            over_groups(act, group)
            evacuate(NG - 1, GU - 1, 1)

        @block.vector
        def _(dve):
            def largest(i, g, k):
                tile, h0, n = ITEMS[k]
                cols = (tile + 1) * P
                buf = 2 * (k % 2)
                wait(dve, smax_ready, lin(i, g, GU, NI, k + 1))
                if tile < 2:
                    src = psum[:, buf:buf + 2].rearrange("p b n -> p (b n)")[:, 0:n * cols].rearrange(
                        "p (h n) -> p h n", h=n)
                elif tile < 4:
                    src = psum[:, buf:buf + 2, 0:cols]
                else:
                    src = psum[:, buf:buf + 2].rearrange("p b n -> p (b n)")[:, 0:cols]
                dst = mneg[:, g % 2].rearrange("p (h t) -> p h t", t=ST)[:, h0:h0 + n, tile]
                dve.tensor_reduce(dst, src, X, ALU.max, negate=True).then_inc(max_done, 1)

            def split_max(i, g):
                wait(dve, m_turned, lin(i, g, GU, 1, 1))
                wait(dve, m_in, lin(i, g, GU, 16 * PARTS, -16 * PARTS))
                turned = psum[0:GH * ST, 7, 0:P]
                p1, p2, p3 = (mparts[:, g % 2, k] for k in range(PARTS))
                dve.tensor_copy(p1, turned).then_inc(m_chain, 1)
                wait(dve, m_chain, lin(i, g, GU, 3, 1))
                dve.tensor_tensor(mrest[:, :], turned, p1, ALU.subtract).then_inc(m_chain, 1)
                wait(dve, m_chain, lin(i, g, GU, 3, 2))
                dve.tensor_copy(p2, mrest[:, :]).then_inc(m_chain, 1)
                wait(dve, m_chain, lin(i, g, GU, 3, 3))
                dve.tensor_tensor(p3, mrest[:, :], p2, ALU.subtract).then_inc(m_split, 1)

            def normalise(i, g, half):
                wait(dve, o_turned, lin(i, g, GU, 2, half + 1))
                g4 = g % GU
                if half == 0 and g4 % 2 == 0:
                    wait(dve, attn_out[(g4 // 2) % 2], lin(i, 0, 1, 16))
                src = psum[:, 7].rearrange("p (t h w) -> p t h w", t=CT, w=VW)
                dve.reciprocal(rsum[:, half], src[:, :, :, HD]).then_inc(rsum_ready, 1)
                wait(dve, rsum_ready, lin(i, g, GU, 2, half + 1))
                dst = attn[:, (g4 // 2) % 2, half * CT:(half + 1) * CT, (g4 % 2) * GH * HD:(g4 % 2 + 1) * GH * HD]
                dve.tensor_tensor(dst.rearrange("p t (h d) -> p t h d", h=GH), src[:, :, :, 0:HD],
                                  rsum[:, half].rearrange("p t (h o) -> p t h o", o=1).broadcast_to([P, CT, GH, HD]),
                                  ALU.mult).then_inc(normed, 1)

            def group(i, g, last=False):
                k = 0
                for n in range(NU):
                    if not last and n < len(SHARE):
                        for _ in range(SHARE[n]):
                            largest(i, g + 1, k)
                            k += 1
                    if n == 2 and not (isinstance(i, int) and i * GU + g == 0):
                        normalise(i, g - 1, 1)
                    if n == 6:
                        normalise(i, g, 0)
                    if n == 8 and not last:
                        split_max(i, g + 1)

            for k in range(NI):
                largest(0, 0, k)
            split_max(0, 0)
            over_groups(dve, group)
            normalise(NG - 1, GU - 1, 1)

        @block.tensor
        def _(pe):
            def first_pass(i, g, k):
                tile, h0, n = ITEMS[k]
                b = g % GU
                if k == 0:
                    wait(pe, stack_in[b], lin(i + g // GU, 0, 1, 12 * 16, 12 * 16))
                wait(pe, max_done, lin(i, g, GU, NI, k - 1))
                cols = (tile + 1) * P
                buf = psum[:, 2 * (k % 2):2 * (k % 2) + 2].rearrange("p b n -> p (b n)")
                for a in range(n):
                    h = h0 + a
                    at = a * cols if tile < 2 else a * 512
                    q = qst[0:KROWS, b, h, tile * P:(tile + 1) * P]
                    for t0 in range(0, cols, 512):
                        t1 = min(cols, t0 + 512)
                        pe.matmul(buf[:, at + t0:at + t1], q, kst[0:KROWS, b, h, t0:t1], start=True,
                                  stop=(t1 < cols), skip_group_check=True)
                    mm = pe.matmul(buf[:, at + cols - P:at + cols], identb[:, :], mask[:, :], start=False, stop=True,
                                   skip_group_check=True)
                mm.then_inc(smax_ready, 1)

            def turn_max(i, g):
                wait(pe, normed, lin(i, g, GU, 2, -1))
                wait(pe, max_done, lin(i, g, GU, NI, NI))
                pe.transpose(psum[0:GH * ST, 7, 0:P], mneg[:, g % 2], ident[:, :]).then_inc(m_turned, 1)

            def scores(i, g, n):
                half, j = UNITS[n]
                cols = columns(half, j)
                if n == 0:
                    wait(pe, m_in, lin(i, g, GU, 16 * PARTS, 16 * PARTS))
                for h in range(GH):
                    wait(pe, exp_done, lin(i, g, GU, NU * GH, n * GH + h - 1))
                    pe.matmul(psum[:, 4 + h % 2, 0:cols], kst[0:MROWS, g, h, j * P:(j + 1) * P],
                              qst[0:MROWS, g, h, (half + 1) * CH - cols:(half + 1) * CH],
                              start=True, stop=True).then_inc(st_ready, 1)

            def weigh(i, g, n):
                half, j = UNITS[n]
                cols = columns(half, j)
                if n == 0:
                    wait(pe, v_in[g % 2], lin(i, g // 2, 2, 16, 16))
                if j == 0:
                    wait(pe, oT_ready, lin(i, g, GU, 2, half))
                if j >= 4 * half:
                    wait(pe, masked, lin(i, g, GU, 8, j + 1))
                else:
                    wait(pe, exp_done, lin(i, g, GU, NU * GH, (n + 1) * GH))
                for h in range(GH):
                    mm = pe.matmul(psum[32 * h:32 * h + 32, 6, CH - cols:CH], vst[:, g % 2, j, h * VW:(h + 1) * VW],
                                   pT[:, n % 3, h, 0:cols], start=(j == 0), stop=(j == 4 * half + 3),
                                   skip_group_check=True)
                mm.then_inc(pv_done, 1)

            def turn_out(i, g, half):
                wait(pe, oT_ready, lin(i, g, GU, 2, half + 1))
                if half == 0 or (isinstance(i, int) and i * GU + g == GROUPS - 1):
                    wait(pe, normed, lin(i, g, GU, 2, half))
                else:
                    wait(pe, m_split, lin(i, g, GU, 1, 2))
                for t in range(CT):
                    mm = pe.transpose(psum[:, 7, t * P:(t + 1) * P], oT[:, half, t * P:(t + 1) * P], ident[:, :])
                mm.then_inc(o_turned, 1)

            def group(i, g, last=False):
                k = 0
                for n in range(NU):
                    scores(i, g, n)
                    if not last and n < len(SHARE):
                        for _ in range(SHARE[n]):
                            first_pass(i, g + 1, k)
                            k += 1
                    if n == 2 and not (isinstance(i, int) and i * GU + g == 0):
                        turn_out(i, g - 1, 1)
                    if n == 6:
                        turn_out(i, g, 0)
                    if n == 8 and not last:
                        turn_max(i, g + 1)
                    if n > 0:
                        weigh(i, g, n - 1)
                weigh(i, g, NU - 1)

            for k in range(NI):
                first_pass(0, 0, k)
            turn_max(0, 0)
            over_groups(pe, group)
            turn_out(NG - 1, GU - 1, 1)


def routing(nc, psum, c, s_wo, attn_dram, xz_dram, dealt, tile_row, tile_expert):
    with ExitStack() as ctx:
        def sb(name, shape, dt=F32):
            return ctx.enter_context(nc.sbuf_tensor(name, shape, dt))

        def sem(name):
            return ctx.enter_context(nc.semaphore(name))

        ident, below, ones, counts = c["ident"], c["below"], c["ones"], c["counts"]
        at = sb("at", [P, 2, 2, CT, P])
        xz = sb("xz_r", [P, 2, CT, D])
        aT = sb("aT", [P, 2, DK, CH])
        rows = sb("rows", [P, 2, CT, ROWW])
        hn = sb("hn", [P, 2, CT, D])
        hT = sb("hT", [P, 2, DK, CH])
        stats = sb("stats_r", [P, CT, 6])
        mv = sb("mv_r", [P, 2, CT, 2])
        ve = sb("ve_r", [P, 2, CT])
        lmax = sb("lmax", [P, CT])
        shifted = sb("shifted", [P, CT, E])
        exps = sb("exps", [P, CT, E])
        expsum = sb("expsum", [P, CT])
        order = sb("order", [P, CT, E])
        first = sb("first", [P, CT, E])
        best = sb("best", [P, CT])
        chosen = sb("chosen", [P, CT, E], BF16)
        place = sb("place", [P, CT, E])
        slot = sb("slot", [P, 2, CT], I32)
        token = sb("token", [P, CT])
        nobody = sb("nobody", [P, ROWW])
        lane8 = sb("lane8", [P, E])
        slot8 = sb("slot8", [P, E], I32)
        start = sb("start", [1, E])
        held = sb("held", [1, E])
        grid = sb("grid", [1, E, NTOK // P])
        over = sb("over", [1, E, NTOK // P])
        ntiles = sb("ntiles", [1, E])
        ones8 = sb("ones8", [1, E])
        upto = sb("upto", [1, E])
        jgrid = sb("jgrid", [1, TILES, E])
        behind = sb("behind", [1, TILES, E])
        gone = sb("gone", [1, TILES, E])
        ej = sb("ej", [1, TILES])
        cj = sb("cj", [1, TILES])
        rj = sb("rj", [1, TILES])
        rk = sb("rk", [1, TILES])

        at_in = [sem(f"at_in{u}") for u in range(2)]
        xz_in = [sem(f"xz_in{u}") for u in range(2)]
        s_init = sem("s_init")
        a_turned, aT_ready, wo_ready, x1_ready = sem("a_turned"), sem("aT_ready"), sem("wo_ready"), sem("x1_ready")
        stats_ready, var_ready, rstd_ready, ve_ready = (
            sem("stats_ready2"), sem("var_ready2"), sem("rstd_ready2"), sem("ve_ready2"))
        h_ready, h_turned, hT_ready = sem("h_ready"), sem("h_turned"), sem("hT_ready")
        logits_ready, shifted_ready, exp_ready = sem("logits_ready"), sem("shifted_ready"), sem("exp_ready")
        chosen_ready, rank_ready, slot_ready = sem("chosen_ready"), sem("rank_ready"), sem("slot_ready")
        step = sem("step")
        sent = [sem(f"sent{u}") for u in range(2)]
        s_tail, s_nobody, s_pad = sem("s_tail"), sem("s_nobody"), sem("s_pad")

        block = ctx.enter_context(nc.Block())
        N2 = NCH // 2

        @block.sync
        def _(sp):
            def load(i, u):
                for half in range(2):
                    sp.dma_start(at[:, u, half], attn_dram[bass.ds(i + half * B, 1), u * CH:(u + 1) * CH].rearrange(
                        "o (t p) n -> p (o t) n", p=P)).then_inc(at_in[u], 16)
                sp.dma_start(xz[:, u], xz_dram[bass.ds(lin(i, u, 2, 1), 1)].rearrange("o (t p) d -> p (o t) d", p=P)
                             ).then_inc(xz_in[u], 16)

            def chunk(i, u):
                wait(sp, a_turned, lin(i, u, 2, 1, -1))
                wait(sp, x1_ready, lin(i, u, 2, 1, -1))
                load(i, u)

            for u in range(2):
                chunk(0, u)
            with sp.Fori(1, N2) as i:
                for u in range(2):
                    chunk(i, u)
            sp.wait_ge(s_init, 10)
            sp.dma_start(dealt[E * REGION:E * REGION + P, :], nobody[:, :]).then_inc(s_nobody, 16)
            sp.wait_ge(s_nobody, 16)

        @block.gpsimd
        def _(pool):
            passed = sem("pool_passed13")
            pool.iota(counts[:, :], pattern=[[REGION, E]], base=0, channel_multiplier=0,
                      allow_small_or_imprecise_dtypes=True).then_inc(s_init, 1)
            pool.iota(start[:, :], pattern=[[REGION, E]], base=0, channel_multiplier=0,
                      allow_small_or_imprecise_dtypes=True).then_inc(s_init, 1)
            pool.iota(order[:, :, :], pattern=[[0, CT], [-1, E]], base=E, channel_multiplier=0,
                      allow_small_or_imprecise_dtypes=True).then_inc(s_init, 1)
            pool.iota(token[:, :], pattern=[[P, CT]], base=0, channel_multiplier=1,
                      allow_small_or_imprecise_dtypes=True).then_inc(s_init, 1)
            pool.iota(lane8[:, :], pattern=[[0, E]], base=0, channel_multiplier=1,
                      allow_small_or_imprecise_dtypes=True).then_inc(s_init, 1)
            pool.iota(grid[:, :, :], pattern=[[0, E], [P, NTOK // P]], base=0, channel_multiplier=0,
                      allow_small_or_imprecise_dtypes=True).then_inc(s_init, 1)
            pool.iota(jgrid[:, :, :], pattern=[[1, TILES], [0, E]], base=0, channel_multiplier=0,
                      allow_small_or_imprecise_dtypes=True).then_inc(s_init, 1)
            pool.memset(ones8[:, :], 1.0).then_inc(s_init, 1)
            pool.memset(nobody[:, :], 0.0).then_inc(s_init, 1)
            pool.wait_ge(s_init, 9)
            pool.memset(nobody[:, D + 1:D + 2], float(NOWHERE)).then_inc(s_init, 1)

            def deviation(i, u):
                wait_alone(pool, var_ready, lin(i, u, 2, 1, 1), passed)
                pool.tensor_scalar(ve[:, u], mv[:, u, :, 1], EPS, None, ALU.add).then_inc(ve_ready, 1)
                wait(pool, ve_ready, lin(i, u, 2, 1, 1))
                pool.tensor_tensor(rows[:, u, :, D + 3], ve[:, u], c["minus_half"][:, :], ALU.pow).then_inc(rstd_ready, 1)

            def deal(i, u):
                wait_alone(pool, slot_ready, lin(i, u, 2, 1, 1), passed)
                for t in range(CT):
                    pool.indirect_dma_start(
                        out=dealt[:, :], out_offset=bass.IndirectOffsetOnAxis(ap=slot[:, u, t:t + 1].bitcast(U32), axis=0),
                        in_=rows[:, u, t], in_offset=None).then_inc(sent[u], 16)

            deviation(0, 0)
            deviation(0, 1)
            deal(0, 0)
            with pool.Fori(1, N2) as i:
                deviation(i, 0)
                deal(i - 1, 1)
                deviation(i, 1)
                deal(i, 0)
            deal(N2 - 1, 1)
            pool.wait_ge(s_tail, 1)
            for e in range(E):
                pool.indirect_dma_start(
                    out=dealt[:, :], out_offset=bass.IndirectOffsetOnAxis(ap=slot8[:, e:e + 1].bitcast(U32), axis=0),
                    in_=nobody[:, :], in_offset=None).then_inc(s_pad, 16)
            for u in range(2):
                pool.wait_ge(sent[u], 16 * CT * N2)
            pool.wait_ge(s_pad, 16 * E)

        @block.scalar
        def _(act):
            def turn_attention(i, u):
                wait(act, a_turned, lin(i, u, 2, 1, 1))
                act.activation(aT[:, u], psum[:, 0:2], ACT.Copy).then_inc(aT_ready, 1)

            def turn_h(i, u):
                wait(act, h_turned, lin(i, u, 2, 1, 1))
                act.activation(hT[:, u], psum[:, 4:6], ACT.Copy).then_inc(hT_ready, 1)

            def gate(i, u):
                wait(act, shifted_ready, lin(i, u, 2, 1, 1))
                act.activation(exps[:, :, :], shifted[:, :, :], ACT.Exp).then_inc(exp_ready, 1)

            turn_attention(0, 0)
            turn_attention(0, 1)
            turn_h(0, 0)
            gate(0, 0)
            with act.Fori(1, N2) as i:
                turn_attention(i, 0)
                turn_h(i - 1, 1)
                gate(i - 1, 1)
                turn_attention(i, 1)
                turn_h(i, 0)
                gate(i, 0)
            turn_h(N2 - 1, 1)
            gate(N2 - 1, 1)

        @block.tensor
        def _(pe):
            pe.wait_ge(s_wo, 16)

            def attended(i, u):
                wait(pe, at_in[u], lin(i, 0, 1, 32, 32))
                wait(pe, aT_ready, lin(i, u, 2, 1))
                for k in range(DK):
                    for t in range(CT):
                        mm = pe.transpose(psum[:, k, t * P:(t + 1) * P], at[:, u, k, t], ident[:, :])
                mm.then_inc(a_turned, 1)
                wait(pe, aT_ready, lin(i, u, 2, 1, 1))
                wait(pe, x1_ready, lin(i, u, 2, 1))
                for t in range(CT):
                    for k in range(DK):
                        mm = pe.matmul(psum[:, 2 + t // 2, (t % 2) * D:(t % 2 + 1) * D], aT[:, u, k, t * P:(t + 1) * P],
                                       c["wo"][:, k], start=(k == 0), stop=(k == DK - 1))
                mm.then_inc(wo_ready, 1)

            def router(i, u):
                wait(pe, h_ready, lin(i, u, 2, 1, 1))
                wait(pe, hT_ready, lin(i, u, 2, 1))
                for k in range(DK):
                    for t in range(CT):
                        mm = pe.transpose(psum[:, 4 + k, t * P:(t + 1) * P], hn[:, u, t, k * P:(k + 1) * P], ident[:, :])
                mm.then_inc(h_turned, 1)
                wait(pe, hT_ready, lin(i, u, 2, 1, 1))
                wait(pe, shifted_ready, lin(i, u, 2, 1))
                for t in range(CT):
                    for k in range(DK):
                        mm = pe.matmul(psum[:, 6, t * E:(t + 1) * E], hT[:, u, k, t * P:(t + 1) * P], c["wr"][:, k],
                                       start=(k == 0), stop=(k == DK - 1))
                mm.then_inc(logits_ready, 1)

            def rank(i, u):
                wait(pe, chosen_ready, lin(i, u, 2, 1, 1))
                wait(pe, slot_ready, lin(i, u, 2, 1))
                flat = chosen[:, :, :].rearrange("p t e -> p (t e)")
                pe.matmul(psum[:, 7, 0:CT * E], below[:, :], flat, start=True, stop=False, skip_group_check=True)
                for t in range(1, CT):
                    for before in range(t):
                        pe.matmul(psum[:, 7, t * E:(t + 1) * E], ones[:, :], chosen[:, before], start=False,
                                  stop=True, skip_group_check=True)
                for t in range(CT):
                    mm = pe.matmul(psum[:, 7, CT * E:CT * E + E], ones[:, :], chosen[:, t], start=False,
                                   stop=(t == CT - 1), skip_group_check=True)
                mm.then_inc(rank_ready, 1)

            attended(0, 0)
            attended(0, 1)
            router(0, 0)
            rank(0, 0)
            with pe.Fori(1, N2) as i:
                attended(i, 0)
                router(i - 1, 1)
                rank(i - 1, 1)
                attended(i, 1)
                router(i, 0)
                rank(i, 0)
            router(N2 - 1, 1)
            rank(N2 - 1, 1)

        @block.vector
        def _(dve):
            passed = sem("dve_passed16")
            dve.wait_ge(s_init, 10)

            def normed(i, u):
                wait(dve, wo_ready, lin(i, u, 2, 1, 1))
                wait(dve, xz_in[u], lin(i, 0, 1, 16, 16))
                wait(dve, sent[u], lin(i, 0, 1, 16 * CT))
                dve.tensor_tensor(rows[:, u, :, 0:D], psum[:, 2:4].rearrange("p b (t d) -> p (b t) d", d=D), xz[:, u],
                                  ALU.add).then_inc(x1_ready, 1)
                wait(dve, x1_ready, lin(i, u, 2, 1, 1))
                for t in range(CT):
                    last = dve.bn_stats(stats[:, t], rows[:, u, t, 0:D])
                last.then_inc(stats_ready, 1)
                wait_alone(dve, stats_ready, lin(i, u, 2, 1, 1), passed)
                for t in range(CT):
                    last = dve.bn_aggr(mv[:, u, t], stats[:, t])
                last.then_inc(var_ready, 1)
                wait(dve, var_ready, lin(i, u, 2, 1, 1))
                dve.tensor_copy(rows[:, u, :, D + 2], mv[:, u, :, 0])
                wait(dve, rstd_ready, lin(i, u, 2, 1, 1))
                for t in range(CT):
                    last = dve.tensor_scalar(hn[:, u, t], rows[:, u, t, 0:D], mv[:, u, t, 0:1],
                                             rows[:, u, t, D + 3:D + 4], ALU.subtract, ALU.mult)
                last.then_inc(h_ready, 1)

            STEPS = 7

            def choose(i, u):
                n = 0

                def then(ins):
                    nonlocal n
                    n += 1
                    ins.then_inc(step, 1)
                    wait(dve, step, lin(i, u, 2, STEPS, n))

                logits = psum[:, 6, 0:CT * E].rearrange("p (t e) -> p t e", e=E)

                def wide(a):
                    return a.rearrange("p (t o) -> p t o", o=1).broadcast_to([P, CT, E])

                wait(dve, logits_ready, lin(i, u, 2, 1, 1))
                then(dve.tensor_reduce(lmax[:, :], logits, X, ALU.max))
                dve.tensor_tensor(shifted[:, :, :], logits, wide(lmax[:, :]), ALU.subtract).then_inc(shifted_ready, 1)
                wait(dve, shifted_ready, lin(i, u, 2, 1, 1))
                then(dve.scalar_tensor_tensor(out=first[:, :, :], in0=shifted[:, :, :], scalar=0.0, in1=order[:, :, :],
                                              op0=ALU.is_equal, op1=ALU.mult))
                then(dve.tensor_reduce(best[:, :], first[:, :, :], X, ALU.max))
                dve.tensor_tensor(chosen[:, :, :], first[:, :, :], wide(best[:, :]), ALU.is_equal
                                  ).then_inc(chosen_ready, 1)
                wait(dve, exp_ready, lin(i, u, 2, 1, 1))
                then(dve.tensor_reduce(expsum[:, :], exps[:, :, :], X, ALU.add))
                dve.reciprocal(rows[:, u, :, D], expsum[:, :])
                dve.tensor_copy(rows[:, u, :, D + 1], token[:, :])
                wait(dve, rank_ready, lin(i, u, 2, 1, 1))
                then(dve.tensor_tensor(place[:, :, :], psum[:, 7, 0:CT * E].rearrange("p (t e) -> p t e", e=E),
                                       counts[:, :].rearrange("p (o e) -> p o e", o=1).broadcast_to([P, CT, E]),
                                       ALU.add))
                dve.tensor_scalar(token[:, :], token[:, :], float(CH), None, ALU.add)
                then(dve.tensor_tensor(first[:, :, :], place[:, :, :], chosen[:, :, :], ALU.mult))
                dve.tensor_tensor(counts[:, :], psum[:, 7, CT * E:CT * E + E], counts[:, :], ALU.add)
                then(dve.tensor_reduce(best[:, :], first[:, :, :], X, ALU.add))
                dve.tensor_copy(slot[:, u], best[:, :]).then_inc(slot_ready, 1)
                assert n == STEPS

            normed(0, 0)
            normed(0, 1)
            choose(0, 0)
            with dve.Fori(1, N2) as i:
                normed(i, 0)
                choose(i - 1, 1)
                normed(i, 1)
                choose(i, 0)
            choose(N2 - 1, 1)

            done = STEPS * NCH

            def then(ins):
                nonlocal done
                done += 1
                ins.then_inc(step, 1)
                dve.wait_ge(step, done)

            dve.wait_ge(slot_ready, NCH)
            dve.tensor_tensor(slot8[:, :], counts[:, :], lane8[:, :], ALU.add).then_inc(s_tail, 1)
            then(dve.tensor_tensor(held[:, :], counts[0:1, :], start[:, :], ALU.subtract))
            then(dve.tensor_tensor(over[:, :, :], held[:, :].rearrange("p (e o) -> p e o", o=1).broadcast_to(
                [1, E, NTOK // P]), grid[:, :, :], ALU.is_gt))
            then(dve.tensor_reduce(ntiles[:, :], over[:, :, :], X, ALU.add))
            then(dve.tensor_tensor_scan(upto[:, :], ones8[:, :], ntiles[:, :], 0.0, ALU.mult, ALU.add))

            def each(a):
                return a.rearrange("p (o e) -> p o e", o=1).broadcast_to([1, TILES, E])

            then(dve.tensor_tensor(behind[:, :, :], each(upto[:, :]), jgrid[:, :, :], ALU.is_le))
            then(dve.tensor_reduce(ej[:, :], behind[:, :, :], X, ALU.add))
            then(dve.tensor_tensor(gone[:, :, :], behind[:, :, :], each(ntiles[:, :]), ALU.mult))
            then(dve.tensor_reduce(cj[:, :], gone[:, :, :], X, ALU.add))
            then(dve.tensor_tensor(rj[:, :], jgrid[:, :, 0], cj[:, :], ALU.subtract))
            then(dve.tensor_scalar(rj[:, :], rj[:, :], float(P), None, ALU.mult))
            then(dve.tensor_scalar(rk[:, :], ej[:, :], float(REGION), None, ALU.mult))
            then(dve.tensor_tensor(rj[:, :], rj[:, :], rk[:, :], ALU.add))
            then(dve.tensor_scalar(tile_row[:, :], rj[:, :], float(E * REGION), None, ALU.min))
            then(dve.tensor_scalar(tile_expert[:, :], ej[:, :], float(E - 1), None, ALU.min))


def mlp(nc, psum, ident, s_weights, w1, w2, tile_row, tile_expert, b1, b2, dealt, out):
    with ExitStack() as ctx:
        def sb(name, shape, dt=F32):
            return ctx.enter_context(nc.sbuf_tensor(name, shape, dt))

        def sem(name):
            return ctx.enter_context(nc.semaphore(name))

        TU = 4
        NT = TILES // TU
        b1s = sb("b1s", [P, E * FF])
        b2s = sb("b2s", [P, E * D])
        rows = sb("rows_m", [P, TU, ROWW])
        hn = sb("hn_m", [P, 2, D])
        hT = sb("hT_m", [P, 2, DK, P])
        pre = sb("pre", [P, 2, FF])
        act_out = sb("act_out", [P, 2, FF])
        gT = sb("gT", [P, 2, FK, P])
        o1 = sb("o1", [P, 2, D])
        orow = sb("orow", [P, TU, D])
        token = sb("token_m", [P, TU, 1], I32)

        s_bias = sem("s_bias")
        row_in = [sem(f"row_in{u}") for u in range(TU)]
        h_ready, h_turned, hT_ready = sem("h_ready3"), sem("h_turned3"), sem("hT_ready3")
        up_ready, pre_ready, gelu_ready = sem("up_ready"), sem("pre_ready"), sem("gelu_ready")
        g_turned, gT_ready, down_ready = sem("g_turned"), sem("gT_ready"), sem("down_ready")
        o1_ready, orow_ready = sem("o1_ready"), sem("orow_ready")
        sent = [sem(f"sent_m{u}") for u in range(TU)]

        block = ctx.enter_context(nc.Block())

        def over_tiles(eng, tile):
            for u in range(TU):
                tile(0, u)
            with eng.Fori(1, NT - 1) as i:
                for u in range(TU):
                    tile(i, u)
            for u in range(TU):
                tile(NT - 1, u)

        def beyond(i, u):
            return isinstance(i, int) and i * TU + u >= TILES

        def entry(eng, table, i, u, most):
            return eng.value_load(table[0:1, bass.ds(lin(i, u, TU, 1), 1)], min_val=0, max_val=most)

        @block.sync
        def _(sp):
            sp.dma_start(b1s[:, :], b1.rearrange("(o e) f -> o (e f)", o=1).broadcast_to([P, E * FF])).then_inc(s_bias, 16)
            sp.dma_start(b2s[:, :], b2.rearrange("(o e) f -> o (e f)", o=1).broadcast_to([P, E * D])).then_inc(s_bias, 16)

            def tile(i, u):
                wait(sp, orow_ready, lin(i, u, TU, 1, 1 - TU))
                row = entry(sp, tile_row, i, u, E * REGION)
                sp.dma_start(rows[:, u], dealt[bass.ds(row, P), :]).then_inc(row_in[u], 16)

            over_tiles(sp, tile)

        @block.gpsimd
        def _(pool):
            passed = sem("pool_passed19")
            def tile(i, u):
                wait_alone(pool, orow_ready, lin(i, u, TU, 1, 1), passed)
                pool.indirect_dma_start(
                    out=out, out_offset=bass.IndirectOffsetOnAxis(ap=token[:, u].bitcast(U32), axis=0),
                    in_=orow[:, u], in_offset=None, bounds_check=NTOK - 1, oob_is_err=False).then_inc(sent[u], 16)

            over_tiles(pool, tile)
            for u in range(TU):
                pool.wait_ge(sent[u], 16 * NT)

        @block.vector
        def _(dve):
            dve.wait_ge(s_bias, 32)

            def normed(i, u):
                if beyond(i, u):
                    return
                n, u4 = lin(i, u, TU, 1), u % TU
                wait(dve, row_in[u4], lin(i + u // TU, 0, 1, 16, 16))
                wait(dve, h_turned, n - 1)
                dve.tensor_scalar(hn[:, u % 2], rows[:, u4, 0:D], rows[:, u4, D + 2:D + 3], rows[:, u4, D + 3:D + 4],
                                  ALU.subtract, ALU.mult).then_inc(h_ready, 1)

            def bias(i, u):
                if beyond(i, u):
                    return
                n = lin(i, u, TU, 1)
                e = entry(dve, tile_expert, i, u, E - 1)
                wait(dve, up_ready, n + 1)
                wait(dve, gelu_ready, n - 1)
                dve.tensor_tensor(pre[:, u % 2], psum[:, 2 + u % 2], b1s[:, bass.ds(e * FF, FF)], ALU.add
                                  ).then_inc(pre_ready, 1)

            def tile(i, u):
                bias(i, u + 1)
                n = lin(i, u, TU, 1)
                e = entry(dve, tile_expert, i, u, E - 1)
                wait(dve, down_ready, n + 1)
                dve.tensor_tensor(o1[:, u % 2], psum[:, 6 + u % 2, 0:D], b2s[:, bass.ds(e * D, D)], ALU.add
                                  ).then_inc(o1_ready, 1)
                wait(dve, sent[u], lin(i, 0, 1, 16))
                dve.tensor_copy(token[:, u], rows[:, u, D + 1:D + 2])
                wait(dve, o1_ready, n + 1)
                dve.scalar_tensor_tensor(out=orow[:, u], in0=o1[:, u % 2], scalar=rows[:, u, D:D + 1], in1=rows[:, u, 0:D],
                                         op0=ALU.mult, op1=ALU.add).then_inc(orow_ready, 1)
                normed(i, u + 3)

            for u in range(3):
                normed(0, u)
            bias(0, 0)
            over_tiles(dve, tile)

        @block.scalar
        def _(act):
            def turned_h(i, u):
                if beyond(i, u):
                    return
                wait(act, h_turned, lin(i, u, TU, 1, 1))
                act.activation(hT[:, u % 2], psum[:, u % 2, 0:DK * P].rearrange("p (k n) -> p k n", k=DK), ACT.Copy
                               ).then_inc(hT_ready, 1)

            def gelu(i, u):
                if beyond(i, u):
                    return
                wait(act, pre_ready, lin(i, u, TU, 1, 1))
                act.activation(act_out[:, u % 2], pre[:, u % 2], ACT.Gelu).then_inc(gelu_ready, 1)

            def tile(i, u):
                wait(act, g_turned, lin(i, u, TU, 1, 1))
                act.activation(gT[:, u % 2], psum[:, 4 + u % 2].rearrange("p (k n) -> p k n", k=FK), ACT.Copy
                               ).then_inc(gT_ready, 1)
                turned_h(i, u + 2)
                gelu(i, u + 1)

            turned_h(0, 0)
            turned_h(0, 1)
            gelu(0, 0)
            over_tiles(act, tile)

        @block.tensor
        def _(pe):
            def turn_h(i, u):
                if beyond(i, u):
                    return
                n = lin(i, u, TU, 1)
                wait(pe, h_ready, n + 1)
                wait(pe, hT_ready, n - 1)
                for k in range(DK):
                    mm = pe.transpose(psum[:, u % 2, k * P:(k + 1) * P], hn[:, u % 2, k * P:(k + 1) * P], ident[:, :])
                mm.then_inc(h_turned, 1)

            def up(i, u):
                if beyond(i, u):
                    return
                n = lin(i, u, TU, 1)
                e = entry(pe, tile_expert, i, u, E - 1)
                wait(pe, hT_ready, n + 1)
                wait(pe, pre_ready, n - 1)
                for k in range(DK):
                    mm = pe.matmul(psum[:, 2 + u % 2], hT[:, u % 2, k], w1[:, bass.ds(e * (DK * FF) + k * FF, FF)],
                                   start=(k == 0), stop=(k == DK - 1))
                mm.then_inc(up_ready, 1)

            def tile(i, u):
                n = lin(i, u, TU, 1)
                wait(pe, gelu_ready, n + 1)
                wait(pe, gT_ready, n - 1)
                for k in range(FK):
                    mm = pe.transpose(psum[:, 4 + u % 2, k * P:(k + 1) * P], act_out[:, u % 2, k * P:(k + 1) * P],
                                      ident[:, :])
                mm.then_inc(g_turned, 1)
                turn_h(i, u + 2)
                up(i, u + 1)
                e = entry(pe, tile_expert, i, u, E - 1)
                wait(pe, gT_ready, n + 1)
                wait(pe, o1_ready, n - 1)
                for k in range(FK):
                    mm = pe.matmul(psum[:, 6 + u % 2, 0:D], gT[:, u % 2, k], w2[:, bass.ds(e * (FK * D) + k * D, D)],
                                   start=(k == 0), stop=(k == FK - 1))
                mm.then_inc(down_ready, 1)

            pe.wait_ge(s_weights, 32)
            turn_h(0, 0)
            turn_h(0, 1)
            up(0, 0)
            over_tiles(pe, tile)


_INS = ["L0_attn_x", "L0_attn_ln_w", "L0_attn_ln_b", "L0_attn_wq", "L0_attn_wk", "L0_attn_wv", "L0_attn_wo",
        "L0_ffn_w_red", "L0_ffn_wg", "L0_ffn_W1", "L0_ffn_b1", "L0_ffn_W2", "L0_ffn_b2"]


def kernel(**inputs):
    import numpy as np
    import concourse.bacc as bacc
    from concourse.bass_utils import run_bass_kernel_spmd

    nc = bacc.Bacc("TRN2", target_bir_lowering=False, num_devices=1)
    arrays, args = {}, []
    for name in _INS:
        a = np.ascontiguousarray(inputs[name])
        if name == "L0_attn_x":
            a = a.reshape(NCH, CH, D)
        arrays[name + "_in"] = a
        args.append(nc.dram_tensor(name + "_in", a.shape, mybir.dt.from_np(a.dtype), kind="ExternalInput").ap())
    args.append(nc.dram_tensor("out", (NTOK, D), F32, kind="ExternalOutput").ap())
    build(nc, *args)
    r = run_bass_kernel_spmd(nc, [arrays], core_ids=[0])
    return r.results[0]["out"].reshape(B, S, D)
```

```python
from contextlib import ExitStack

import concourse.bass as bass
from concourse import mybir

P = 128
F32 = mybir.dt.float32
BF16 = mybir.dt.bfloat16
I32 = mybir.dt.int32
U32 = mybir.dt.uint32
ALU = mybir.AluOpType
ACT = mybir.ActivationFunctionType
X = mybir.AxisListType.X

B, S, D = 8, 1024, 256
H, HD = 16, 16
NTOK = B * S
DK = D // P
E, FF, RED = 8, 512, 16
FK = FF // P
EPS = 1e-5

CH = 512
CT = CH // P
NCH = NTOK // CH

PARTS = 3
GH = 4
GROUPS = B * H // GH
PAIRS = GROUPS // 2
ST = S // P
VW = 32
Q_ROWS = [(0, 3), (1, 2), (2, 1)]
KROWS = 6 * HD
MROWS = KROWS + PARTS
MASK = -1e30

REGION = NTOK + P
ROWW = D + 4
TILES = NTOK // P + E
NOWHERE = NTOK + P


def lin(i, u, n, k, q=0):
    return i * (n * k) + (u * k + q)


def wait(eng, sem, value):
    if isinstance(value, int) and value <= 0:
        return
    eng.wait_ge(sem, value)


def wait_alone(eng, sem, value, passed):
    wait(eng, sem, value)
    if not isinstance(value, int):
        eng.sem_inc(passed, 1)


def build(nc, x, ln_w, ln_b, wq, wk, wv, wo, w_red, wg, W1, b1, W2, b2, out):
    qparts = nc.dram_tensor("qparts", (PARTS, PAIRS, P, S), BF16, kind="Internal").ap()
    kparts = nc.dram_tensor("kparts", (PARTS, PAIRS, P, S), BF16, kind="Internal").ap()
    vrows = nc.dram_tensor("vrows", (PAIRS, S, H // 2 * VW), F32, kind="Internal").ap()
    xz_dram = nc.dram_tensor("xz_dram", (NCH, CH, D), F32, kind="Internal").ap()
    attn_dram = nc.dram_tensor("attn_dram", (PAIRS, S, P), F32, kind="Internal").ap()
    dealt = nc.dram_tensor("dealt", (E * REGION + P, ROWW), F32, kind="Internal").ap()

    with ExitStack() as ctx:
        def sb(name, shape, dt=F32):
            return ctx.enter_context(nc.sbuf_tensor(name, shape, dt))

        def sem(name):
            return ctx.enter_context(nc.semaphore(name))

        psum = ctx.enter_context(nc.psum_tensor("psum", [P, 8, 512], F32))
        c = dict(
            ident=sb("ident", [P, P]), identb=sb("identb", [P, P], BF16),
            mask=sb("mask", [P, P], BF16), below=sb("below", [P, P], BF16), ones=sb("ones", [P, P], BF16),
            lnw=sb("lnw", [P, DK]), lnb=sb("lnb", [P, DK]), minus_half=sb("minus_half", [P, CT]),
            counts=sb("counts", [P, E]), wr=sb("wr", [P, DK, E]), wo=sb("wo_sb", [P, DK, D]),
        )
        w1 = sb("w1_sb", [P, E * DK * FF])
        w2 = sb("w2_sb", [P, E * FK * D])
        b1s = sb("b1s", [P, E * FK])
        b2s = sb("b2s", [P, E * D])
        tile_row = sb("tile_row", [1, TILES], I32)
        tile_expert = sb("tile_expert", [1, TILES], I32)
        s_weights, s_wo = sem("s_weights"), sem("s_wo")
        projections(nc, psum, c, s_wo, x, ln_w, ln_b, wq, wk, wv, wo, w_red, wg,
                    qparts, kparts, vrows, xz_dram)
        attention(nc, psum, c, qparts, kparts, vrows, attn_dram, (W1, b1, W2, b2), (w1, b1s, w2, b2s), s_weights)
        routing(nc, psum, c, s_wo, attn_dram, xz_dram, dealt, tile_row, tile_expert)
        mlp(nc, psum, c["ident"], s_weights, w1, w2, b1s, b2s, tile_row, tile_expert, dealt, out)


def projections(nc, psum, c, s_wo, x, ln_w, ln_b, wq, wk, wv, wo, w_red, wg,
                qparts, kparts, vrows, xz_dram):
    with ExitStack() as ctx:
        def sb(name, shape, dt=F32):
            return ctx.enter_context(nc.sbuf_tensor(name, shape, dt))

        def sem(name):
            return ctx.enter_context(nc.semaphore(name))

        ident, identb, mask, below, ones = c["ident"], c["identb"], c["mask"], c["below"], c["ones"]
        lnw, lnb, minus_half = c["lnw"], c["lnb"], c["minus_half"]
        wqkv = sb("wqkv", [P, 3, DK, D])
        xt = sb("xt", [P, 2, CT, D])
        z = sb("z", [P, 2, CT, D])
        yn = sb("yn", [P, 2, CT, D])
        xz = sb("xz", [P, 2, CT, D])
        yT = sb("yT", [P, 2, DK, CH])
        parts = sb("parts", [P, 2, 4, PARTS, CH], BF16)
        rest = sb("rest", [P, 4, CH])
        vsb = sb("vsb", [P, 2, CT, H, VW])
        stats = sb("stats", [P, CT, 6])
        mv = sb("mv", [P, 2, 2, CT, 2])
        ve = sb("ve", [P, 2, 2, CT])
        rstd = sb("rstd", [P, 2, 2, CT])
        wgs = sb("wgs", [E, RED])
        wgq = sb("wgq", [E, RED])
        wgn = sb("wgn", [E, 4])
        wgT = sb("wgT", [RED, E])
        wred = sb("wred", [P, DK, RED])
        wredT = sb("wredT", [RED, DK, P])

        s_const, s_cst2, s_load, s_w = sem("s_const"), sem("s_cst2"), sem("s_load"), sem("s_w")
        s_router, s_rc, s_rp = sem("s_router"), sem("s_rc"), sem("s_rp")
        s_vinit = sem("s_vinit")
        x_in = [sem(f"x_in{u}") for u in range(2)]
        var_ready, rstd_ready, ve_ready = sem("var_ready"), sem("rstd_ready"), sem("ve_ready")
        stats_ready, z_ready, yn_ready = sem("stats_ready"), sem("z_ready"), sem("yn_ready")
        xz_ready = sem("xz_ready")
        xz_out = [sem(f"xz_out{u}") for u in range(2)]
        turned, yT_ready = sem("turned"), sem("yT_ready")
        qk_ready, v_ready = sem("qk_ready"), sem("v_ready")
        part1, rest_ready, part2, part3 = sem("part1"), sem("rest_ready"), sem("part2"), sem("part3")
        v_copied = sem("v_copied")
        parts_out = [sem(f"parts_out{u}") for u in range(2)]
        v_out = [sem(f"v_out{u}") for u in range(2)]

        block = ctx.enter_context(nc.Block())
        N2 = NCH // 2

        @block.sync
        def _(sp):
            def load_x(i, u):
                sp.dma_start(xt[:, u], x[bass.ds(lin(i, u, 2, 1), 1)].rearrange("o (t p) d -> p (o t) d", p=P)
                             ).then_inc(x_in[u], 16)

            def chunk(i, u, last=False):
                wait(sp, xz_ready, lin(i, u, 2, 1, 1))
                sp.dma_start(xz_dram[bass.ds(lin(i, u, 2, 1), 1)].rearrange("o (t p) d -> p (o t) d", p=P),
                             xz[:, u]).then_inc(xz_out[u], 16)
                if not last:
                    load_x(i + 1, u)
                for m in range(4):
                    wait(sp, part3, lin(i, u, 2, 4, m + 1))
                    dst = (qparts if m < 2 else kparts)[:, bass.ds(i + (m % 2) * B, 1), :, u * CH:(u + 1) * CH]
                    sp.dma_start(dst.rearrange("a o p n -> p (o a) n"), parts[:, u, m]).then_inc(parts_out[u], 16)
                wait(sp, v_copied, lin(i, u, 2, 2, 2))
                for half in range(2):
                    dst = vrows[bass.ds(i + half * B, 1), u * CH:(u + 1) * CH]
                    sp.dma_start(dst.rearrange("o (t p) n -> p (o t) n", p=P),
                                 vsb[:, u, :, half * 8:half * 8 + 8, :].rearrange("p t h w -> p t (h w)")
                                 ).then_inc(v_out[u], 16)

            load_x(0, 0)
            load_x(0, 1)
            for u in range(2):
                chunk(0, u)
            with sp.Fori(1, N2 - 1) as i:
                for u in range(2):
                    chunk(i, u)
            for u in range(2):
                chunk(N2 - 1, u, last=True)
            for u in range(2):
                sp.wait_ge(xz_out[u], 16 * N2)
                sp.wait_ge(parts_out[u], 64 * N2)
                sp.wait_ge(v_out[u], 32 * N2)

        @block.gpsimd
        def _(pool):
            passed = sem("pool_passed1")
            pool.memset(ident[:, :], 0.0).then_inc(s_const, 1)
            pool.memset(minus_half[:, :], -0.5).then_inc(s_const, 1)
            pool.memset(mask[:, :], 0.0).then_inc(s_const, 1)
            pool.memset(ones[:, :], 1.0).then_inc(s_const, 1)
            pool.memset(c["counts"][:, :], 0.0).then_inc(s_const, 1)
            pool.wait_ge(s_const, 5)
            pool.affine_select(out=ident[:, :], in_=ident[:, :], compare_op=ALU.not_equal, fill=1.0, base=0,
                               pattern=[[-1, P]], channel_multiplier=1).then_inc(s_const, 1)
            pool.affine_select(out=mask[:, :], in_=mask[:, :], compare_op=ALU.is_ge, fill=MASK, base=0,
                               pattern=[[-1, P]], channel_multiplier=1).then_inc(s_const, 1)
            pool.affine_select(out=below[:, :], in_=ones[:, :], compare_op=ALU.is_gt, fill=0.0, base=0,
                               pattern=[[1, P]], channel_multiplier=-1).then_inc(s_const, 1)
            pool.memset(vsb[:, :, :, :, HD:VW], 0.0).then_inc(s_vinit, 1)
            pool.wait_ge(s_const, 8)
            pool.tensor_copy(identb[:, :], ident[:, :]).then_inc(s_const, 1)
            pool.wait_ge(s_vinit, 1)
            pool.memset(vsb[:, :, :, :, HD:HD + 1], 1.0).then_inc(s_vinit, 1)
            pool.wait_ge(s_rc, 1)
            pool.tensor_tensor(wgn[:, 1:2], wgn[:, 0:1], wgn[:, 3:4], ALU.pow).then_inc(s_rp, 1)

            def chunk(i, u):
                for norm in range(2):
                    wait_alone(pool, var_ready, lin(i, u, 2, 2, norm + 1), passed)
                    pool.tensor_scalar(ve[:, u, norm], mv[:, u, norm, :, 1], EPS, None, ALU.add).then_inc(ve_ready, 1)
                    wait(pool, ve_ready, lin(i, u, 2, 2, norm + 1))
                    pool.tensor_tensor(rstd[:, u, norm], ve[:, u, norm], minus_half[:, :], ALU.pow).then_inc(rstd_ready, 1)
                wait(pool, xz_out[u], lin(i, 0, 1, 16))
                wait(pool, z_ready, lin(i, u, 2, 1, 1))
                pool.tensor_tensor(xz[:, u], xt[:, u], z[:, u], ALU.add).then_inc(xz_ready, 1)

            for u in range(2):
                chunk(0, u)
            with pool.Fori(1, N2) as i:
                for u in range(2):
                    chunk(i, u)

        @block.vector
        def _(dve):
            passed = sem("dve_passed4")
            dve.memset(wgn[:, 3:4], 0.5).then_inc(s_cst2, 1)
            dve.wait_ge(s_cst2, 1)
            dve.wait_ge(s_router, 32)
            dve.tensor_tensor_reduce(wgq[:, :], wgs[:, :], wgs[:, :], 1.0, 0.0, ALU.mult, ALU.add,
                                     wgn[:, 0:1]).then_inc(s_rc, 1)
            dve.wait_ge(s_rp, 1)
            dve.tensor_scalar(wgn[:, 2:3], wgn[:, 1:2], 1e-4, None, ALU.max).then_inc(s_rc, 1)
            dve.wait_ge(s_rc, 2)
            dve.reciprocal(wgn[:, 0:1], wgn[:, 2:3]).then_inc(s_rc, 1)
            dve.wait_ge(s_rc, 3)
            dve.tensor_scalar(wgq[:, :], wgs[:, :], wgn[:, 0:1], None, ALU.mult).then_inc(s_rc, 1)
            dve.wait_ge(s_rp, 2)
            dve.tensor_copy(wgT[:, :], psum[0:RED, 0, 0:E]).then_inc(s_rc, 1)
            dve.tensor_copy(wredT[:, :, :], psum[0:RED, 1, 0:DK * P].rearrange("r (k p) -> r k p", k=DK)
                            ).then_inc(s_rc, 1)
            dve.wait_ge(s_rp, 3)
            dve.tensor_copy(c["wr"][:, :, :], psum[:, 2, 0:DK * E].rearrange("p (k e) -> p k e", k=DK)
                            ).then_inc(s_rc, 1)

            def norms(i, u):
                wait(dve, x_in[u], lin(i, 0, 1, 16, 16))
                wait(dve, xz_ready, lin(i, u, 2, 1, -1))
                for norm, (src, dst) in enumerate(((xt, z), (z, yn))):
                    for t in range(CT):
                        last = dve.bn_stats(stats[:, t], src[:, u, t])
                    last.then_inc(stats_ready, 1)
                    wait_alone(dve, stats_ready, lin(i, u, 2, 2, norm + 1), passed)
                    for t in range(CT):
                        last = dve.bn_aggr(mv[:, u, norm, t], stats[:, t])
                    last.then_inc(var_ready, 1)
                    wait(dve, rstd_ready, lin(i, u, 2, 2, norm + 1))
                    if norm:
                        wait(dve, turned, lin(i, u, 2, 1, -1))
                    for t in range(CT):
                        last = dve.tensor_scalar(dst[:, u, t], src[:, u, t], mv[:, u, norm, t, 0:1],
                                                 rstd[:, u, norm, t:t + 1], ALU.subtract, ALU.mult)
                    if norm == 0:
                        last.then_inc(z_ready, 1)
                        wait(dve, z_ready, lin(i, u, 2, 1, 1))
                    else:
                        last.then_inc(yn_ready, 1)

            def split(i, u):
                def second(m):
                    wait(dve, part1, lin(i, u, 2, 4, m + 1))
                    dve.tensor_tensor(rest[:, m], psum[:, m], parts[:, u, m, 0], ALU.subtract).then_inc(rest_ready, 1)

                def third(m):
                    wait(dve, part2, lin(i, u, 2, 4, m + 1))
                    dve.tensor_tensor(parts[:, u, m, 2], rest[:, m], parts[:, u, m, 1], ALU.subtract).then_inc(part3, 1)

                second(0)
                second(1)
                third(0)
                second(2)
                third(1)
                second(3)
                third(2)
                third(3)
                for half in range(2):
                    wait(dve, v_ready, lin(i, u, 2, 2, half + 1))
                    if half == 0:
                        wait(dve, v_out[u], lin(i, 0, 1, 32))
                    dve.tensor_copy(vsb[:, u, 2 * half:2 * half + 2, :, 0:HD],
                                    psum[:, 4 + half].rearrange("p (t h d) -> p t h d", t=2, d=HD)
                                    ).then_inc(v_copied, 1)

            norms(0, 0)
            dve.wait_ge(s_vinit, 2)
            norms(0, 1)
            split(0, 0)
            with dve.Fori(1, N2) as i:
                norms(i, 0)
                split(i - 1, 1)
                norms(i, 1)
                split(i, 0)
            split(N2 - 1, 1)

        @block.scalar
        def _(act):
            act.dma_start(wgs[:, :], wg).then_inc(s_router, 16)
            act.dma_start(wred[:, :, :], w_red.rearrange("(k p) r -> p k r", p=P)).then_inc(s_router, 16)
            act.dma_start(lnw[:, :], ln_w.rearrange("(k p) -> p k", p=P), allow_slow_non_contiguous=True).then_inc(s_load, 16)
            act.dma_start(lnb[:, :], ln_b.rearrange("(k p) -> p k", p=P), allow_slow_non_contiguous=True).then_inc(s_load, 16)
            for n, w in enumerate((wq, wk, wv)):
                for k in range(DK):
                    act.dma_start(wqkv[:, n, k].rearrange("p (h e) -> p h e", h=H),
                                  w[:, k * P:(k + 1) * P, :].rearrange("h p e -> p h e")).then_inc(s_w, 16)
            act.dma_start(c["wo"][:, :, :], wo.rearrange("(k p) d -> p k d", p=P)).then_inc(s_wo, 16)

            def evacuate(i, u):
                wait(act, turned, lin(i, u, 2, 1, 1))
                for k in range(DK):
                    last = act.activation(yT[:, u, k], psum[:, 6 + k], ACT.Identity, bias=lnb[:, k:k + 1],
                                          scale=lnw[:, k:k + 1])
                last.then_inc(yT_ready, 1)

            def split(i, u):
                def first(m):
                    wait(act, qk_ready, lin(i, u, 2, 4, m + 1))
                    act.activation(parts[:, u, m, 0], psum[:, m], ACT.Copy).then_inc(part1, 1)

                def second(m):
                    wait(act, rest_ready, lin(i, u, 2, 4, m + 1))
                    act.activation(parts[:, u, m, 1], rest[:, m], ACT.Copy).then_inc(part2, 1)

                wait(act, parts_out[u], lin(i, 0, 1, 64))
                first(0)
                first(1)
                second(0)
                first(2)
                second(1)
                first(3)
                second(2)
                second(3)

            act.wait_ge(s_load, 32)
            evacuate(0, 0)
            split(0, 0)
            evacuate(0, 1)
            with act.Fori(1, N2) as i:
                split(i - 1, 1)
                evacuate(i, 0)
                split(i, 0)
                evacuate(i, 1)
            split(N2 - 1, 1)

        @block.tensor
        def _(pe):
            pe.wait_ge(s_const, 9)
            pe.wait_ge(s_rc, 4)
            pe.wait_ge(s_router, 32)
            pe.transpose(psum[0:RED, 0, 0:E], wgq[:, :], ident[0:E, 0:E])
            for k in range(DK):
                last = pe.transpose(psum[0:RED, 1, k * P:(k + 1) * P], wred[:, k], ident[:, :])
            last.then_inc(s_rp, 1)
            pe.wait_ge(s_rc, 6)
            for k in range(DK):
                last = pe.matmul(psum[:, 2, k * E:(k + 1) * E], wredT[:, k], wgT[:, :], start=True, stop=True)
            last.then_inc(s_rp, 1)
            pe.wait_ge(s_rc, 7)

            def turn(i, u):
                wait(pe, yn_ready, lin(i, u, 2, 1, 1))
                wait(pe, yT_ready, lin(i, u, 2, 1))
                for k in range(DK):
                    for t in range(CT):
                        last = pe.transpose(psum[:, 6 + k, t * P:(t + 1) * P], yn[:, u, t, k * P:(k + 1) * P],
                                            ident[:, :])
                last.then_inc(turned, 1)

            def project(i, u):
                wait(pe, yT_ready, lin(i, u, 2, 1, 1))
                for m in range(4):
                    wait(pe, rest_ready, lin(i, u, 2, 4, m - 3))
                    for k in range(DK):
                        last = pe.matmul(psum[:, m], wqkv[:, m // 2, k, (m % 2) * P:(m % 2 + 1) * P],
                                         yT[:, u, k], start=(k == 0), stop=(k == DK - 1))
                    last.then_inc(qk_ready, 1)
                for t in range(CT):
                    if t % 2 == 0:
                        wait(pe, v_copied, lin(i, u, 2, 2, t // 2 - 1))
                    for k in range(DK):
                        last = pe.matmul(psum[:, 4 + t // 2, (t % 2) * D:(t % 2 + 1) * D],
                                         yT[:, u, k, t * P:(t + 1) * P], wqkv[:, 2, k],
                                         start=(k == 0), stop=(k == DK - 1))
                    if t % 2:
                        last.then_inc(v_ready, 1)

            turn(0, 0)
            pe.wait_ge(s_w, 96)
            project(0, 0)
            turn(0, 1)
            with pe.Fori(1, N2) as i:
                project(i - 1, 1)
                turn(i, 0)
                project(i, 0)
                turn(i, 1)
            project(N2 - 1, 1)


UNITS = [(0, j) for j in range(4)] + [(1, j) for j in range(8)]
ITEMS = [(0, 0, 4), (1, 0, 4)] + [(i, h, 2) for i in (2, 3) for h in (0, 2)] + [
    (i, h, 1) for i in range(4, 8) for h in range(4)]
ROTATION = [[20, 21], ["m1", "o1"], [], [], [0, 1, 2], [3, 4, 5], ["o0", 6, 7], [8, 9, 10], [11, 12, "m0"],
            [13, 14, 15], [16, 17], [18, 19]]
OWN = 4
ENTRIES = sum(len(r) for r in ROTATION)
FIRST = [0, 1, 2, 3, 4, 5, 6, "m0"] + list(range(7, 20))
assert ENTRIES % 2 == 0
NU = len(UNITS)
SB = 3
GU = 4
NG = GROUPS // GU


def columns(c, j):
    return CH - max(0, j - 4 * c) * P


def attention(nc, psum, c, qparts, kparts, vrows, attn_dram, experts, resident, s_weights):
    with ExitStack() as ctx:
        def sb(name, shape, dt=F32):
            return ctx.enter_context(nc.sbuf_tensor(name, shape, dt))

        def sem(name):
            return ctx.enter_context(nc.semaphore(name))

        ident, identb, mask = c["ident"], c["identb"], c["mask"]
        qst = sb("qst", [P, GU, 2, GH, CH], BF16)
        kst = sb("kst", [P, GU, GH, S], BF16)
        vst = sb("vst", [P, 2, ST, GH * VW])
        pT = sb("pT", [P, 3, GH, CH])
        oT = sb("oT", [P, 2, CH])
        mneg = sb("mneg", [P, 2, 2, GH * CT])
        mparts = sb("mparts", [GH * CT, 2, PARTS, P], BF16)
        mrest = sb("mrest", [GH * CT, P])
        rsum = sb("rsum", [P, 2, CT, GH])
        attn = sb("attn", [P, 2, ST, P])

        s_ones, s_oT = sem("s_ones"), sem("s_oT")
        stack_in = [sem(f"stack_in{g}") for g in range(GU)]
        v_in = [sem(f"v_in{g}") for g in range(2)]
        m_in = [sem(f"m_in{half}") for half in range(2)]
        attn_out = [sem(f"attn_out{g}") for g in range(2)]
        filled, drained = sem("filled"), sem("drained")
        m_split, m_chain = sem("m_split"), sem("m_chain")
        st_ready, exp_done, masked, pv_done = sem("st_ready"), sem("exp_done"), sem("masked"), sem("pv_done")
        oT_ready, rsum_ready = sem("oT_ready"), sem("rsum_ready")


        def at(i, g, pos):
            return lin(i, g, GU, ENTRIES, len(FIRST) + pos + 1)

        def owner(n, entry):
            if entry == "o1":
                return -1
            return 0 if entry == "o0" or n < OWN else 1

        END = len(FIRST) + len([e for n, r in enumerate(ROTATION) for e in r if owner(n, e) < 1])

        def position(entry):
            return sum(ROTATION, []).index(entry)

        block = ctx.enter_context(nc.Block())

        def over_groups(eng, group):
            for g in range(GU):
                group(0, g)
            with eng.Fori(1, NG - 1) as i:
                for g in range(GU):
                    group(i, g)
            for g in range(GU):
                group(NG - 1, g, last=(g == GU - 1))

        @block.sync
        def _(sp):
            def load_stack(i, g):
                i, g = i + g // GU, g % GU
                pair, h0 = lin(i, g // 2, 2, 1), (g % 2) * GH * HD
                heads = slice(h0, h0 + GH * HD)
                row = 0
                for part, times in Q_ROWS:
                    for k in range(times):
                        for half in range(2):
                            src = qparts[part, bass.ds(pair, 1), heads, half * CH:(half + 1) * CH].rearrange(
                                "o (h e) n -> e (o h) n", e=HD)
                            sp.dma_start(qst[row + k * HD:row + (k + 1) * HD, g, half], src).then_inc(stack_in[g], 16)
                        src = kparts[k, bass.ds(pair, 1), heads].rearrange("o (h e) n -> e (o h) n", e=HD)
                        sp.dma_start(kst[row + k * HD:row + (k + 1) * HD, g], src).then_inc(stack_in[g], 16)
                    row += times * HD

            def load_v(i, g):
                i, g = i + g // GU, g % GU
                src = vrows[bass.ds(lin(i, g // 2, 2, 1), 1), :, (g % 2) * GH * VW:(g % 2 + 1) * GH * VW]
                sp.dma_start(vst[:, g % 2], src.rearrange("o (t p) n -> p (o t) n", p=P)).then_inc(v_in[g % 2], 16)

            def load_max(i, g, half):
                wait(sp, m_split, lin(i, g, GU, 2, half + 1))
                for part in range(PARTS):
                    row = KROWS + part
                    sp.dma_start(qst[row:row + 1, g % GU, half].rearrange("o h (t n) -> o (h t) n", n=P),
                                 mparts[:, half, part]).then_inc(m_in[half], 16)

            def store(i, g, count=None):
                wait(sp, drained, at(i, g, position("o1")) if count is None else count)
                pair = lin(i, g // 2, 2, 1, -1)
                buf = (g // 2 + 1) % 2
                sp.dma_start(attn_dram[bass.ds(pair, 1)].rearrange("o (t p) n -> p (o t) n", p=P),
                             attn[:, buf]).then_inc(attn_out[buf], 16)

            def group(i, g, last=False):
                wait(sp, pv_done, lin(i, g, GU, NU))
                if not last:
                    load_v(i, g + 1)
                load_max(i, g, 1)
                if not (isinstance(i, int) and i * GU + g + 2 >= GROUPS):
                    load_stack(i, g + 2)
                if g % 2 == 0 and not (isinstance(i, int) and i * GU + g == 0):
                    store(i, g)
                if not last:
                    load_max(i, g + 1, 0)

            sp.wait_ge(s_ones, 1)
            load_stack(0, 0)
            load_v(0, 0)
            load_stack(0, 1)
            load_max(0, 0, 0)
            over_groups(sp, group)
            store(NG, 0, at(NG - 1, GU - 1, END - len(FIRST)))
            for buf in range(2):
                sp.wait_ge(attn_out[buf], 16 * NG)

        @block.gpsimd
        def _(pool):
            passed = sem("pool_passed7")
            pool.memset(kst[96:MROWS], 1.0).then_inc(s_ones, 1)

            def group(i, g, last=False):
                diagonal = 0
                for n, (half, j) in enumerate(UNITS):
                    if j < 4 * half:
                        continue
                    wait_alone(pool, exp_done, lin(i, g, GU, NU * GH, (n + 1) * GH), passed)
                    part = pT[:, n % 3, :, 0:P]
                    pool.affine_select(out=part, in_=part, compare_op=ALU.is_ge, fill=0.0, base=0,
                                       pattern=[[0, GH], [1, P]], channel_multiplier=-1).then_inc(masked, 1)
                    diagonal += 1

            over_groups(pool, group)

        @block.scalar
        def _(act):
            def evacuate(i, g, half):
                wait(act, pv_done, lin(i, g, GU, NU, 4 + 8 * half))
                act.activation(oT[:, half], psum[:, 7], ACT.Copy).then_inc(oT_ready, 1)

            def group(i, g, last=False):
                for n, (half, j) in enumerate(UNITS):
                    cols = columns(half, j)
                    wait(act, pv_done, lin(i, g, GU, NU, n - 2))
                    for h in range(GH):
                        wait(act, st_ready, lin(i, g, GU, NU * GH, n * GH + h + 1))
                        act.activation(pT[:, n % 3, h, 0:cols], psum[:, 4 + (n * GH + h) % SB, 0:cols], ACT.Exp,
                                       scale=HD ** -0.5).then_inc(exp_done, 1)
                    if n == 0 and not (isinstance(i, int) and i * GU + g == 0):
                        evacuate(i, g - 1, 1)
                    if n == 4:
                        evacuate(i, g, 0)

            (W1, b1, W2, b2), (w1, b1s, w2, b2s) = experts, resident
            act.dma_start(w1[:, :].rearrange("p (e k f) -> p e k f", e=E, k=DK),
                          W1.rearrange("e (k p) f -> p e k f", p=P)).then_inc(s_weights, 16)
            act.dma_start(w2[:, :].rearrange("p (e k f) -> p e k f", e=E, k=FK),
                          W2.rearrange("e (k p) f -> p e k f", p=P)).then_inc(s_weights, 16)
            act.dma_start(b1s[:, :], b1.rearrange("e (k p) -> p (e k)", p=P), allow_slow_non_contiguous=True
                          ).then_inc(s_weights, 16)
            act.dma_start(b2s[:, :], b2.rearrange("(o e) f -> o (e f)", o=1).broadcast_to([P, E * D])
                          ).then_inc(s_weights, 16)
            over_groups(act, group)
            evacuate(NG - 1, GU - 1, 1)

        @block.vector
        def _(dve):
            def largest(g, k, buf, count):
                tile, h0, n = ITEMS[k]
                cols = (tile + 1) * P
                wait(dve, filled, count)
                src = psum[:, 2 * buf:2 * buf + 2]
                flat = src.rearrange("p b n -> p (b n)")
                if tile < 2:
                    src = flat[:, 0:n * cols].rearrange("p (h n) -> p h n", h=n)
                elif tile < 4:
                    src = src[:, :, 0:cols]
                else:
                    src = flat[:, 0:cols]
                dst = mneg[:, g % 2, tile // CT].rearrange("p (h t) -> p h t", t=CT)[:, h0:h0 + n, tile % CT]
                dve.tensor_reduce(dst, src, X, ALU.max, negate=True).then_inc(drained, 1)

            def split_max(i, g, half, buf, count):
                wait(dve, filled, count)
                wait(dve, m_in[half], lin(i, g, GU, 16 * PARTS))
                turned = psum[0:GH * CT, 2 * buf, 0:P]
                p1, p2, p3 = (mparts[:, half, k] for k in range(PARTS))
                dve.tensor_copy(p1, turned).then_inc(m_chain, 1)
                wait(dve, m_chain, lin(i, g, GU, 4, 2 * half + 1))
                dve.tensor_tensor(mrest[:, :], turned, p1, ALU.subtract).then_inc(drained, 1)
                wait(dve, drained, count)
                dve.tensor_copy(p2, mrest[:, :]).then_inc(m_chain, 1)
                wait(dve, m_chain, lin(i, g, GU, 4, 2 * half + 2))
                dve.tensor_tensor(p3, mrest[:, :], p2, ALU.subtract).then_inc(m_split, 1)

            def normalise(i, g, half, buf, count):
                wait(dve, filled, count)
                g4 = g % GU
                if half == 0 and g4 % 2 == 0:
                    wait(dve, attn_out[(g4 // 2) % 2], lin(i, 0, 1, 16))
                src = psum[:, 2 * buf].rearrange("p (t h w) -> p t h w", t=CT, w=VW)
                dve.reciprocal(rsum[:, half], src[:, :, :, HD]).then_inc(rsum_ready, 1)
                wait(dve, rsum_ready, lin(i, g, GU, 2, half + 2))
                dst = attn[:, (g4 // 2) % 2, half * CT:(half + 1) * CT, (g4 % 2) * GH * HD:(g4 % 2 + 1) * GH * HD]
                dve.tensor_tensor(dst.rearrange("p t (h d) -> p t h d", h=GH), src[:, :, :, 0:HD],
                                  rsum[:, half].rearrange("p t (h o) -> p t h o", o=1).broadcast_to([P, CT, GH, HD]),
                                  ALU.mult).then_inc(drained, 1)

            def drain(i, g, entry, buf, count):
                if entry in ("m0", "m1"):
                    split_max(i, g, int(entry[1]), buf, count)
                elif entry in ("o0", "o1"):
                    normalise(i, g, int(entry[1]), buf, count)
                else:
                    largest(g, entry, buf, count)

            def group(i, g, last=False):
                pos = 0
                for n in range(NU):
                    for entry in ROTATION[n]:
                        ahead = owner(n, entry)
                        if not (last and ahead > 0):
                            drain(i, g + ahead, entry, (len(FIRST) + pos) % 2, at(i, g, pos))
                            pos += 1

            dve.memset(oT[:, 1], 1.0).then_inc(s_oT, 1)
            for pos, entry in enumerate(FIRST):
                drain(0, 0, entry, pos % 2, pos + 1)
            over_groups(dve, group)
            normalise(NG - 1, GU - 1, 1, END % 2, at(NG - 1, GU - 1, END - len(FIRST)))

        @block.tensor
        def _(pe):
            def first_pass(g, k, buf):
                tile, h0, n = ITEMS[k]
                b = g % GU
                cols = (tile + 1) * P
                buf = psum[:, 2 * buf:2 * buf + 2].rearrange("p b n -> p (b n)")
                for a in range(n):
                    h = h0 + a
                    at0 = a * cols if tile < 2 else a * 512
                    q = qst[0:KROWS, b, tile // CT, h, (tile % CT) * P:(tile % CT + 1) * P]
                    for t0 in range(0, cols, 512):
                        t1 = min(cols, t0 + 512)
                        pe.matmul(buf[:, at0 + t0:at0 + t1], q, kst[0:KROWS, b, h, t0:t1], start=True,
                                  stop=(t1 < cols), skip_group_check=True)
                    mm = pe.matmul(buf[:, at0 + cols - P:at0 + cols], identb[:, :], mask[:, :], start=False,
                                   stop=True, skip_group_check=True)
                return mm

            def fill(i, g, entry, buf, count):
                small = entry in ("m0", "m1")
                if entry == 0:
                    wait(pe, stack_in[g % GU], lin(i + g // GU, 0, 1, 18 * 16, 18 * 16))
                if entry in ("o0", "o1"):
                    wait(pe, oT_ready, lin(i, g, GU, 2, int(entry[1]) + 1))
                wait(pe, drained, count - (1 if small else 2))
                if small:
                    mm = pe.transpose(psum[0:GH * CT, 2 * buf, 0:P], mneg[:, g % 2, int(entry[1])], ident[:, :])
                elif entry in ("o0", "o1"):
                    for t in range(CT):
                        mm = pe.transpose(psum[:, 2 * buf, t * P:(t + 1) * P], oT[:, int(entry[1]), t * P:(t + 1) * P],
                                          ident[:, :])
                else:
                    mm = first_pass(g, entry, buf)
                mm.then_inc(filled, 1)

            def scores(i, g, n, h):
                half, j = UNITS[n]
                cols = columns(half, j)
                if j == 0 and h == 0:
                    wait(pe, m_in[half], lin(i, g, GU, 16 * PARTS, 16 * PARTS))
                wait(pe, exp_done, lin(i, g, GU, NU * GH, n * GH + h + 1 - SB))
                pe.matmul(psum[:, 4 + (n * GH + h) % SB, 0:cols], kst[0:MROWS, g, h, j * P:(j + 1) * P],
                          qst[0:MROWS, g, half, h, CH - cols:CH],
                          start=True, stop=True).then_inc(st_ready, 1)

            def weigh(i, g, n):
                half, j = UNITS[n]
                cols = columns(half, j)
                if n == 0:
                    wait(pe, v_in[g % 2], lin(i, g // 2, 2, 16, 16))
                if j == 0:
                    wait(pe, oT_ready, lin(i, g, GU, 2, half))
                if j >= 4 * half:
                    wait(pe, masked, lin(i, g, GU, 8, j + 1))
                else:
                    wait(pe, exp_done, lin(i, g, GU, NU * GH, (n + 1) * GH))
                for h in range(GH):
                    mm = pe.matmul(psum[32 * h:32 * h + 32, 7, CH - cols:CH], vst[:, g % 2, j, h * VW:(h + 1) * VW],
                                   pT[:, n % 3, h, 0:cols], start=(j == 0), stop=(j == 4 * half + 3),
                                   skip_group_check=True)
                mm.then_inc(pv_done, 1)

            def group(i, g, last=False):
                pos = 0
                for n in range(NU):
                    left = [e for e in ROTATION[n] if not (last and owner(n, e) > 0)]
                    for h in range(GH):
                        scores(i, g, n, h)
                        if h < len(left):
                            fill(i, g + owner(n, left[h]), left[h], (len(FIRST) + pos) % 2, at(i, g, pos))
                            pos += 1
                    if n > 0:
                        weigh(i, g, n - 1)
                    elif not (isinstance(i, int) and i * GU + g == 0):
                        weigh(i, g - 1, NU - 1)

            pe.wait_ge(s_oT, 1)
            for pos, entry in enumerate(FIRST):
                fill(0, 0, entry, pos % 2, pos + 1)
            over_groups(pe, group)
            weigh(NG - 1, GU - 1, NU - 1)
            fill(NG - 1, GU - 1, "o1", END % 2, at(NG - 1, GU - 1, END - len(FIRST)))


def routing(nc, psum, c, s_wo, attn_dram, xz_dram, dealt, tile_row, tile_expert):
    with ExitStack() as ctx:
        def sb(name, shape, dt=F32):
            return ctx.enter_context(nc.sbuf_tensor(name, shape, dt))

        def sem(name):
            return ctx.enter_context(nc.semaphore(name))

        ident, below, ones, counts = c["ident"], c["below"], c["ones"], c["counts"]
        at = sb("at", [P, 2, 2, CT, P])
        xz = sb("xz_r", [P, 2, CT, D])
        aT = sb("aT", [P, 2, DK, CH])
        rows = sb("rows", [P, 2, CT, ROWW])
        hn = sb("hn", [P, 2, CT, D])
        hT = sb("hT", [P, 2, DK, CH])
        stats = sb("stats_r", [P, CT, 6])
        mv = sb("mv_r", [P, 2, CT, 2])
        ve = sb("ve_r", [P, 2, CT])
        lmax = sb("lmax", [P, CT])
        shifted = sb("shifted", [P, CT, E])
        exps = sb("exps", [P, CT, E])
        expsum = sb("expsum", [P, CT])
        order = sb("order", [P, CT, E])
        first = sb("first", [P, CT, E])
        best = sb("best", [P, CT])
        chosen = sb("chosen", [P, CT, E], BF16)
        place = sb("place", [P, CT, E])
        slot = sb("slot", [P, 2, CT], I32)
        token = sb("token", [P, CT])
        nobody = sb("nobody", [P, ROWW])
        lane8 = sb("lane8", [P, E])
        slot8 = sb("slot8", [P, E], I32)
        start = sb("start", [1, E])
        held = sb("held", [1, E])
        grid = sb("grid", [1, E, NTOK // P])
        over = sb("over", [1, E, NTOK // P])
        ntiles = sb("ntiles", [1, E])
        ones8 = sb("ones8", [1, E])
        upto = sb("upto", [1, E])
        jgrid = sb("jgrid", [1, TILES, E])
        behind = sb("behind", [1, TILES, E])
        gone = sb("gone", [1, TILES, E])
        ej = sb("ej", [1, TILES])
        cj = sb("cj", [1, TILES])
        rj = sb("rj", [1, TILES])
        rk = sb("rk", [1, TILES])

        at_in = [sem(f"at_in{u}") for u in range(2)]
        xz_in = [sem(f"xz_in{u}") for u in range(2)]
        s_init = sem("s_init")
        a_turned, aT_ready, wo_ready, x1_ready = sem("a_turned"), sem("aT_ready"), sem("wo_ready"), sem("x1_ready")
        stats_ready, var_ready, rstd_ready, ve_ready = (
            sem("stats_ready2"), sem("var_ready2"), sem("rstd_ready2"), sem("ve_ready2"))
        h_ready, h_turned, hT_ready = sem("h_ready"), sem("h_turned"), sem("hT_ready")
        logits_ready, shifted_ready, exp_ready = sem("logits_ready"), sem("shifted_ready"), sem("exp_ready")
        chosen_ready, rank_ready, slot_ready = sem("chosen_ready"), sem("rank_ready"), sem("slot_ready")
        step = sem("step")
        sent = [sem(f"sent{u}") for u in range(2)]
        s_tail, s_nobody, s_pad = sem("s_tail"), sem("s_nobody"), sem("s_pad")

        block = ctx.enter_context(nc.Block())
        N2 = NCH // 2

        @block.sync
        def _(sp):
            def load(i, u):
                for half in range(2):
                    sp.dma_start(at[:, u, half], attn_dram[bass.ds(i + half * B, 1), u * CH:(u + 1) * CH].rearrange(
                        "o (t p) n -> p (o t) n", p=P)).then_inc(at_in[u], 16)
                sp.dma_start(xz[:, u], xz_dram[bass.ds(lin(i, u, 2, 1), 1)].rearrange("o (t p) d -> p (o t) d", p=P)
                             ).then_inc(xz_in[u], 16)

            def chunk(i, u):
                wait(sp, a_turned, lin(i, u, 2, 1, -1))
                wait(sp, x1_ready, lin(i, u, 2, 1, -1))
                load(i, u)

            for u in range(2):
                chunk(0, u)
            with sp.Fori(1, N2) as i:
                for u in range(2):
                    chunk(i, u)
            sp.wait_ge(s_init, 10)
            sp.dma_start(dealt[E * REGION:E * REGION + P, :], nobody[:, :]).then_inc(s_nobody, 16)
            sp.wait_ge(s_nobody, 16)

        @block.gpsimd
        def _(pool):
            passed = sem("pool_passed13")
            pool.iota(counts[:, :], pattern=[[REGION, E]], base=0, channel_multiplier=0,
                      allow_small_or_imprecise_dtypes=True).then_inc(s_init, 1)
            pool.iota(start[:, :], pattern=[[REGION, E]], base=0, channel_multiplier=0,
                      allow_small_or_imprecise_dtypes=True).then_inc(s_init, 1)
            pool.iota(order[:, :, :], pattern=[[0, CT], [-1, E]], base=E, channel_multiplier=0,
                      allow_small_or_imprecise_dtypes=True).then_inc(s_init, 1)
            pool.iota(token[:, :], pattern=[[P, CT]], base=0, channel_multiplier=1,
                      allow_small_or_imprecise_dtypes=True).then_inc(s_init, 1)
            pool.iota(lane8[:, :], pattern=[[0, E]], base=0, channel_multiplier=1,
                      allow_small_or_imprecise_dtypes=True).then_inc(s_init, 1)
            pool.iota(grid[:, :, :], pattern=[[0, E], [P, NTOK // P]], base=0, channel_multiplier=0,
                      allow_small_or_imprecise_dtypes=True).then_inc(s_init, 1)
            pool.iota(jgrid[:, :, :], pattern=[[1, TILES], [0, E]], base=0, channel_multiplier=0,
                      allow_small_or_imprecise_dtypes=True).then_inc(s_init, 1)
            pool.memset(ones8[:, :], 1.0).then_inc(s_init, 1)
            pool.memset(nobody[:, :], 0.0).then_inc(s_init, 1)
            pool.wait_ge(s_init, 9)
            pool.memset(nobody[:, D + 1:D + 2], float(NOWHERE)).then_inc(s_init, 1)

            def deviation(i, u):
                wait_alone(pool, var_ready, lin(i, u, 2, 1, 1), passed)
                pool.tensor_scalar(ve[:, u], mv[:, u, :, 1], EPS, None, ALU.add).then_inc(ve_ready, 1)
                wait(pool, ve_ready, lin(i, u, 2, 1, 1))
                pool.tensor_tensor(rows[:, u, :, D + 3], ve[:, u], c["minus_half"][:, :], ALU.pow).then_inc(rstd_ready, 1)

            def deal(i, u):
                wait_alone(pool, slot_ready, lin(i, u, 2, 1, 1), passed)
                for t in range(CT):
                    pool.indirect_dma_start(
                        out=dealt[:, :], out_offset=bass.IndirectOffsetOnAxis(ap=slot[:, u, t:t + 1].bitcast(U32), axis=0),
                        in_=rows[:, u, t], in_offset=None).then_inc(sent[u], 16)

            deviation(0, 0)
            deviation(0, 1)
            deal(0, 0)
            with pool.Fori(1, N2) as i:
                deviation(i, 0)
                deal(i - 1, 1)
                deviation(i, 1)
                deal(i, 0)
            deal(N2 - 1, 1)
            pool.wait_ge(s_tail, 1)
            for e in range(E):
                pool.indirect_dma_start(
                    out=dealt[:, :], out_offset=bass.IndirectOffsetOnAxis(ap=slot8[:, e:e + 1].bitcast(U32), axis=0),
                    in_=nobody[:, :], in_offset=None).then_inc(s_pad, 16)
            for u in range(2):
                pool.wait_ge(sent[u], 16 * CT * N2)
            pool.wait_ge(s_pad, 16 * E)

        @block.scalar
        def _(act):
            def turn_attention(i, u):
                wait(act, a_turned, lin(i, u, 2, 1, 1))
                act.activation(aT[:, u], psum[:, 0:2], ACT.Copy).then_inc(aT_ready, 1)

            def turn_h(i, u):
                wait(act, h_turned, lin(i, u, 2, 1, 1))
                act.activation(hT[:, u], psum[:, 4:6], ACT.Copy).then_inc(hT_ready, 1)

            def gate(i, u):
                wait(act, shifted_ready, lin(i, u, 2, 1, 1))
                act.activation(exps[:, :, :], shifted[:, :, :], ACT.Exp).then_inc(exp_ready, 1)

            turn_attention(0, 0)
            turn_attention(0, 1)
            turn_h(0, 0)
            gate(0, 0)
            with act.Fori(1, N2) as i:
                turn_attention(i, 0)
                turn_h(i - 1, 1)
                gate(i - 1, 1)
                turn_attention(i, 1)
                turn_h(i, 0)
                gate(i, 0)
            turn_h(N2 - 1, 1)
            gate(N2 - 1, 1)

        @block.tensor
        def _(pe):
            pe.wait_ge(s_wo, 16)

            def attended(i, u):
                wait(pe, at_in[u], lin(i, 0, 1, 32, 32))
                wait(pe, aT_ready, lin(i, u, 2, 1))
                for k in range(DK):
                    for t in range(CT):
                        mm = pe.transpose(psum[:, k, t * P:(t + 1) * P], at[:, u, k, t], ident[:, :])
                mm.then_inc(a_turned, 1)
                wait(pe, aT_ready, lin(i, u, 2, 1, 1))
                wait(pe, x1_ready, lin(i, u, 2, 1))
                for t in range(CT):
                    for k in range(DK):
                        mm = pe.matmul(psum[:, 2 + t // 2, (t % 2) * D:(t % 2 + 1) * D], aT[:, u, k, t * P:(t + 1) * P],
                                       c["wo"][:, k], start=(k == 0), stop=(k == DK - 1))
                mm.then_inc(wo_ready, 1)

            def router(i, u):
                wait(pe, h_ready, lin(i, u, 2, 1, 1))
                wait(pe, hT_ready, lin(i, u, 2, 1))
                for k in range(DK):
                    for t in range(CT):
                        mm = pe.transpose(psum[:, 4 + k, t * P:(t + 1) * P], hn[:, u, t, k * P:(k + 1) * P], ident[:, :])
                mm.then_inc(h_turned, 1)
                wait(pe, hT_ready, lin(i, u, 2, 1, 1))
                wait(pe, shifted_ready, lin(i, u, 2, 1))
                for t in range(CT):
                    for k in range(DK):
                        mm = pe.matmul(psum[:, 6, t * E:(t + 1) * E], hT[:, u, k, t * P:(t + 1) * P], c["wr"][:, k],
                                       start=(k == 0), stop=(k == DK - 1))
                mm.then_inc(logits_ready, 1)

            def rank(i, u):
                wait(pe, chosen_ready, lin(i, u, 2, 1, 1))
                wait(pe, slot_ready, lin(i, u, 2, 1))
                flat = chosen[:, :, :].rearrange("p t e -> p (t e)")
                pe.matmul(psum[:, 7, 0:CT * E], below[:, :], flat, start=True, stop=False, skip_group_check=True)
                for t in range(1, CT):
                    for before in range(t):
                        pe.matmul(psum[:, 7, t * E:(t + 1) * E], ones[:, :], chosen[:, before], start=False,
                                  stop=True, skip_group_check=True)
                for t in range(CT):
                    mm = pe.matmul(psum[:, 7, CT * E:CT * E + E], ones[:, :], chosen[:, t], start=False,
                                   stop=(t == CT - 1), skip_group_check=True)
                mm.then_inc(rank_ready, 1)

            attended(0, 0)
            attended(0, 1)
            router(0, 0)
            rank(0, 0)
            with pe.Fori(1, N2) as i:
                attended(i, 0)
                router(i - 1, 1)
                rank(i - 1, 1)
                attended(i, 1)
                router(i, 0)
                rank(i, 0)
            router(N2 - 1, 1)
            rank(N2 - 1, 1)

        @block.vector
        def _(dve):
            passed = sem("dve_passed16")
            dve.wait_ge(s_init, 10)

            def normed(i, u):
                wait(dve, wo_ready, lin(i, u, 2, 1, 1))
                wait(dve, xz_in[u], lin(i, 0, 1, 16, 16))
                wait(dve, sent[u], lin(i, 0, 1, 16 * CT))
                dve.tensor_tensor(rows[:, u, :, 0:D], psum[:, 2:4].rearrange("p b (t d) -> p (b t) d", d=D), xz[:, u],
                                  ALU.add).then_inc(x1_ready, 1)
                wait(dve, x1_ready, lin(i, u, 2, 1, 1))
                for t in range(CT):
                    last = dve.bn_stats(stats[:, t], rows[:, u, t, 0:D])
                last.then_inc(stats_ready, 1)
                wait_alone(dve, stats_ready, lin(i, u, 2, 1, 1), passed)
                for t in range(CT):
                    last = dve.bn_aggr(mv[:, u, t], stats[:, t])
                last.then_inc(var_ready, 1)
                wait(dve, var_ready, lin(i, u, 2, 1, 1))
                dve.tensor_copy(rows[:, u, :, D + 2], mv[:, u, :, 0])
                wait(dve, rstd_ready, lin(i, u, 2, 1, 1))
                for t in range(CT):
                    last = dve.tensor_scalar(hn[:, u, t], rows[:, u, t, 0:D], mv[:, u, t, 0:1],
                                             rows[:, u, t, D + 3:D + 4], ALU.subtract, ALU.mult)
                last.then_inc(h_ready, 1)

            STEPS = 7

            def choose(i, u):
                n = 0

                def then(ins):
                    nonlocal n
                    n += 1
                    ins.then_inc(step, 1)
                    wait(dve, step, lin(i, u, 2, STEPS, n))

                logits = psum[:, 6, 0:CT * E].rearrange("p (t e) -> p t e", e=E)

                def wide(a):
                    return a.rearrange("p (t o) -> p t o", o=1).broadcast_to([P, CT, E])

                wait(dve, logits_ready, lin(i, u, 2, 1, 1))
                then(dve.tensor_reduce(lmax[:, :], logits, X, ALU.max))
                dve.tensor_tensor(shifted[:, :, :], logits, wide(lmax[:, :]), ALU.subtract).then_inc(shifted_ready, 1)
                wait(dve, shifted_ready, lin(i, u, 2, 1, 1))
                then(dve.scalar_tensor_tensor(out=first[:, :, :], in0=shifted[:, :, :], scalar=0.0, in1=order[:, :, :],
                                              op0=ALU.is_equal, op1=ALU.mult))
                then(dve.tensor_reduce(best[:, :], first[:, :, :], X, ALU.max))
                dve.tensor_tensor(chosen[:, :, :], first[:, :, :], wide(best[:, :]), ALU.is_equal
                                  ).then_inc(chosen_ready, 1)
                wait(dve, exp_ready, lin(i, u, 2, 1, 1))
                then(dve.tensor_reduce(expsum[:, :], exps[:, :, :], X, ALU.add))
                dve.reciprocal(rows[:, u, :, D], expsum[:, :])
                dve.tensor_copy(rows[:, u, :, D + 1], token[:, :])
                wait(dve, rank_ready, lin(i, u, 2, 1, 1))
                then(dve.tensor_tensor(place[:, :, :], psum[:, 7, 0:CT * E].rearrange("p (t e) -> p t e", e=E),
                                       counts[:, :].rearrange("p (o e) -> p o e", o=1).broadcast_to([P, CT, E]),
                                       ALU.add))
                dve.tensor_scalar(token[:, :], token[:, :], float(CH), None, ALU.add)
                then(dve.tensor_tensor(first[:, :, :], place[:, :, :], chosen[:, :, :], ALU.mult))
                dve.tensor_tensor(counts[:, :], psum[:, 7, CT * E:CT * E + E], counts[:, :], ALU.add)
                then(dve.tensor_reduce(best[:, :], first[:, :, :], X, ALU.add))
                dve.tensor_copy(slot[:, u], best[:, :]).then_inc(slot_ready, 1)
                assert n == STEPS

            normed(0, 0)
            normed(0, 1)
            choose(0, 0)
            with dve.Fori(1, N2) as i:
                normed(i, 0)
                choose(i - 1, 1)
                normed(i, 1)
                choose(i, 0)
            choose(N2 - 1, 1)

            done = STEPS * NCH

            def then(ins):
                nonlocal done
                done += 1
                ins.then_inc(step, 1)
                dve.wait_ge(step, done)

            dve.wait_ge(slot_ready, NCH)
            dve.tensor_tensor(slot8[:, :], counts[:, :], lane8[:, :], ALU.add).then_inc(s_tail, 1)
            then(dve.tensor_tensor(held[:, :], counts[0:1, :], start[:, :], ALU.subtract))
            then(dve.tensor_tensor(over[:, :, :], held[:, :].rearrange("p (e o) -> p e o", o=1).broadcast_to(
                [1, E, NTOK // P]), grid[:, :, :], ALU.is_gt))
            then(dve.tensor_reduce(ntiles[:, :], over[:, :, :], X, ALU.add))
            then(dve.tensor_tensor_scan(upto[:, :], ones8[:, :], ntiles[:, :], 0.0, ALU.mult, ALU.add))

            def each(a):
                return a.rearrange("p (o e) -> p o e", o=1).broadcast_to([1, TILES, E])

            then(dve.tensor_tensor(behind[:, :, :], each(upto[:, :]), jgrid[:, :, :], ALU.is_le))
            then(dve.tensor_reduce(ej[:, :], behind[:, :, :], X, ALU.add))
            then(dve.tensor_tensor(gone[:, :, :], behind[:, :, :], each(ntiles[:, :]), ALU.mult))
            then(dve.tensor_reduce(cj[:, :], gone[:, :, :], X, ALU.add))
            then(dve.tensor_tensor(rj[:, :], jgrid[:, :, 0], cj[:, :], ALU.subtract))
            then(dve.tensor_scalar(rj[:, :], rj[:, :], float(P), None, ALU.mult))
            then(dve.tensor_scalar(rk[:, :], ej[:, :], float(REGION), None, ALU.mult))
            then(dve.tensor_tensor(rj[:, :], rj[:, :], rk[:, :], ALU.add))
            then(dve.tensor_scalar(tile_row[:, :], rj[:, :], float(E * REGION), None, ALU.min))
            then(dve.tensor_scalar(tile_expert[:, :], ej[:, :], float(E - 1), None, ALU.min))


def mlp(nc, psum, ident, s_weights, w1, w2, b1s, b2s, tile_row, tile_expert, dealt, out):
    with ExitStack() as ctx:
        def sb(name, shape, dt=F32):
            return ctx.enter_context(nc.sbuf_tensor(name, shape, dt))

        def sem(name):
            return ctx.enter_context(nc.semaphore(name))

        TU = 8
        NT = TILES // TU
        rows = sb("rows_m", [P, TU, ROWW])
        hn = sb("hn_m", [P, 2, D])
        hT = sb("hT_m", [P, 2, DK, P])
        w1t = sb("w1t", [P, 2, DK * FF])
        pre = sb("pre", [P, 2, FK, P])
        gT = sb("gT", [P, 2, FK, P])
        o1 = sb("o1", [P, 2, D])
        orow = sb("orow", [P, TU, D])
        token = sb("token_m", [P, TU, 1], I32)

        row_in = [sem(f"row_in{u}") for u in range(TU)]
        h_ready, h_turned, hT_ready = sem("h_ready3"), sem("h_turned3"), sem("hT_ready3")
        up_ready, pre_ready, gelu_ready = sem("up_ready"), sem("pre_ready"), sem("gelu_ready")
        down_ready, w1_ready = sem("down_ready"), sem("w1_ready")
        o1_ready, orow_ready = sem("o1_ready"), sem("orow_ready")
        sent = [sem(f"sent_m{u}") for u in range(TU)]

        block = ctx.enter_context(nc.Block())

        def over_tiles(eng, tile):
            for u in range(TU):
                tile(0, u)
            with eng.Fori(1, NT - 1) as i:
                for u in range(TU):
                    tile(i, u)
            for u in range(TU):
                tile(NT - 1, u)

        def beyond(i, u):
            return isinstance(i, int) and i * TU + u >= TILES

        def entry(eng, table, i, u, most):
            return eng.value_load(table[0:1, bass.ds(lin(i, u, TU, 1), 1)], min_val=0, max_val=most)

        @block.sync
        def _(sp):
            def tile(i, u):
                wait(sp, orow_ready, lin(i, u, TU, 1, 1 - TU))
                row = entry(sp, tile_row, i, u, E * REGION)
                sp.dma_start(rows[:, u], dealt[bass.ds(row, P), :]).then_inc(row_in[u], 16)

            over_tiles(sp, tile)

        @block.gpsimd
        def _(pool):
            passed = sem("pool_passed19")
            def tile(i, u):
                wait_alone(pool, orow_ready, lin(i, u, TU, 1, 1), passed)
                pool.indirect_dma_start(
                    out=out, out_offset=bass.IndirectOffsetOnAxis(ap=token[:, u].bitcast(U32), axis=0),
                    in_=orow[:, u], in_offset=None, bounds_check=NTOK - 1, oob_is_err=False).then_inc(sent[u], 16)

            over_tiles(pool, tile)
            for u in range(TU):
                pool.wait_ge(sent[u], 16 * NT)

        @block.vector
        def _(dve):
            dve.wait_ge(s_weights, 64)

            def normed(i, u):
                if beyond(i, u):
                    return
                n, u4 = lin(i, u, TU, 1), u % TU
                wait(dve, row_in[u4], lin(i + u // TU, 0, 1, 16, 16))
                wait(dve, h_turned, n - 1)
                dve.tensor_scalar(hn[:, u % 2], rows[:, u4, 0:D], rows[:, u4, D + 2:D + 3], rows[:, u4, D + 3:D + 4],
                                  ALU.subtract, ALU.mult).then_inc(h_ready, 1)

            def bias(i, u):
                if beyond(i, u):
                    return
                n = lin(i, u, TU, 1)
                e = entry(dve, tile_expert, i, u, E - 1)
                wait(dve, up_ready, n + 1)
                wait(dve, gelu_ready, n - 1)
                dve.tensor_tensor(pre[:, u % 2], psum[:, 2 + u % 2].rearrange("p (k n) -> p k n", k=FK),
                                  b1s[:, bass.ds(e * FK, FK)].rearrange("p (k o) -> p k o", o=1
                                                                        ).broadcast_to([P, FK, P]), ALU.add
                                  ).then_inc(pre_ready, 1)

            def tile(i, u):
                normed(i, u + 3)
                bias(i, u + 1)
                n = lin(i, u, TU, 1)
                e = entry(dve, tile_expert, i, u, E - 1)
                wait(dve, down_ready, n + 1)
                dve.tensor_tensor(o1[:, u % 2], psum[:, 4 + u % 2, 0:D], b2s[:, bass.ds(e * D, D)], ALU.add
                                  ).then_inc(o1_ready, 1)
                wait(dve, sent[u], lin(i, 0, 1, 16))
                dve.tensor_copy(token[:, u], rows[:, u, D + 1:D + 2])
                wait(dve, o1_ready, n + 1)
                dve.scalar_tensor_tensor(out=orow[:, u], in0=o1[:, u % 2], scalar=rows[:, u, D:D + 1], in1=rows[:, u, 0:D],
                                         op0=ALU.mult, op1=ALU.add).then_inc(orow_ready, 1)

            for u in range(3):
                normed(0, u)
            bias(0, 0)
            over_tiles(dve, tile)

        @block.scalar
        def _(act):
            def turned_h(i, u):
                if beyond(i, u):
                    return
                wait(act, h_turned, lin(i, u, TU, 1, 1))
                act.activation(hT[:, u % 2], psum[:, u % 2, 0:DK * P].rearrange("p (k n) -> p k n", k=DK), ACT.Copy
                               ).then_inc(hT_ready, 1)

            def fetch(i, u):
                if beyond(i, u):
                    return
                e = entry(act, tile_expert, i, u, E - 1)
                wait(act, up_ready, lin(i, u, TU, 1, -1))
                act.activation(w1t[:, u % 2], w1[:, bass.ds(e * (DK * FF), DK * FF)], ACT.Copy).then_inc(w1_ready, 1)

            def gelu(i, u):
                if beyond(i, u):
                    return
                wait(act, pre_ready, lin(i, u, TU, 1, 1))
                wait(act, down_ready, lin(i, u, TU, 1, -1))
                act.activation(gT[:, u % 2], pre[:, u % 2], ACT.Gelu).then_inc(gelu_ready, 1)

            def tile(i, u):
                turned_h(i, u + 2)
                gelu(i, u + 1)
                fetch(i, u + 3)

            act.wait_ge(s_weights, 64)
            fetch(0, 0)
            fetch(0, 1)
            turned_h(0, 0)
            turned_h(0, 1)
            gelu(0, 0)
            fetch(0, 2)
            over_tiles(act, tile)

        @block.tensor
        def _(pe):
            def turn_h(i, u):
                if beyond(i, u):
                    return
                n = lin(i, u, TU, 1)
                wait(pe, h_ready, n + 1)
                wait(pe, hT_ready, n - 1)
                for k in range(DK):
                    mm = pe.transpose(psum[:, u % 2, k * P:(k + 1) * P], hn[:, u % 2, k * P:(k + 1) * P], ident[:, :])
                mm.then_inc(h_turned, 1)

            def up(i, u):
                if beyond(i, u):
                    return
                n = lin(i, u, TU, 1)
                wait(pe, w1_ready, n + 1)
                wait(pe, hT_ready, n + 1)
                wait(pe, pre_ready, n - 1)
                for f in range(FK):
                    for k in range(DK):
                        mm = pe.matmul(psum[:, 2 + u % 2, f * P:(f + 1) * P],
                                       w1t[:, u % 2, k * FF + f * P:k * FF + (f + 1) * P], hT[:, u % 2, k],
                                       start=(k == 0), stop=(k == DK - 1))
                mm.then_inc(up_ready, 1)

            def tile(i, u):
                n = lin(i, u, TU, 1)
                turn_h(i, u + 2)
                up(i, u + 1)
                e = entry(pe, tile_expert, i, u, E - 1)
                wait(pe, gelu_ready, n + 1)
                wait(pe, o1_ready, n - 1)
                for k in range(FK):
                    mm = pe.matmul(psum[:, 4 + u % 2, 0:D], gT[:, u % 2, k], w2[:, bass.ds(e * (FK * D) + k * D, D)],
                                   start=(k == 0), stop=(k == FK - 1))
                mm.then_inc(down_ready, 1)

            pe.wait_ge(s_weights, 64)
            turn_h(0, 0)
            turn_h(0, 1)
            up(0, 0)
            over_tiles(pe, tile)


_INS = ["L0_attn_x", "L0_attn_ln_w", "L0_attn_ln_b", "L0_attn_wq", "L0_attn_wk", "L0_attn_wv", "L0_attn_wo",
        "L0_ffn_w_red", "L0_ffn_wg", "L0_ffn_W1", "L0_ffn_b1", "L0_ffn_W2", "L0_ffn_b2"]


def kernel(**inputs):
    import numpy as np
    import concourse.bacc as bacc
    from concourse.bass_utils import run_bass_kernel_spmd

    nc = bacc.Bacc("TRN2", target_bir_lowering=False, num_devices=1)
    arrays, args = {}, []
    for name in _INS:
        a = np.ascontiguousarray(inputs[name])
        if name == "L0_attn_x":
            a = a.reshape(NCH, CH, D)
        arrays[name + "_in"] = a
        args.append(nc.dram_tensor(name + "_in", a.shape, mybir.dt.from_np(a.dtype), kind="ExternalInput").ap())
    args.append(nc.dram_tensor("out", (NTOK, D), F32, kind="ExternalOutput").ap())
    build(nc, *args)
    r = run_bass_kernel_spmd(nc, [arrays], core_ids=[0])
    return r.results[0]["out"].reshape(B, S, D)
```

```python
from contextlib import ExitStack

import concourse.bass as bass
from concourse import mybir

P = 128
F32 = mybir.dt.float32
BF16 = mybir.dt.bfloat16
I32 = mybir.dt.int32
U32 = mybir.dt.uint32
ALU = mybir.AluOpType
ACT = mybir.ActivationFunctionType
X = mybir.AxisListType.X

B, S, D = 8, 1024, 256
H, HD = 16, 16
NTOK = B * S
DK = D // P
E, FF, RED = 8, 512, 16
FK = FF // P
EPS = 1e-5

CH = 512
CT = CH // P
NCH = NTOK // CH

PARTS = 3
GH = 4
GROUPS = B * H // GH
PAIRS = GROUPS // 2
ST = S // P
VW = 32
Q_ROWS = [(0, 3), (1, 2), (2, 1)]
KROWS = 6 * HD
MROWS = KROWS + PARTS
MASK = -1e30

REGION = NTOK + P
ROWW = D + 4
TILES = NTOK // P + E
WEIGHTS = 16 * (2 * E + 2)
NOWHERE = NTOK + P


def lin(i, u, n, k, q=0):
    return i * (n * k) + (u * k + q)


def wait(eng, sem, value):
    if isinstance(value, int) and value <= 0:
        return
    eng.wait_ge(sem, value)


def wait_alone(eng, sem, value, passed):
    wait(eng, sem, value)
    if not isinstance(value, int):
        eng.sem_inc(passed, 1)


def load_stack(eng, stacks, i, g):
    qparts, kparts, qst, kst, stack_in = stacks
    i, g = i + g // GU, g % GU
    pair, h0 = lin(i, g // 2, 2, 1), (g % 2) * GH * HD
    heads = slice(h0, h0 + GH * HD)
    row = 0
    for part, times in Q_ROWS:
        for k in range(times):
            for half in range(2):
                src = qparts[part, bass.ds(pair, 1), heads, half * CH:(half + 1) * CH].rearrange(
                    "o (h e) n -> e (o h) n", e=HD)
                eng.dma_start(qst[row + k * HD:row + (k + 1) * HD, g, half], src).then_inc(stack_in[g], 16)
            src = kparts[k, bass.ds(pair, 1), heads].rearrange("o (h e) n -> e (o h) n", e=HD)
            eng.dma_start(kst[row + k * HD:row + (k + 1) * HD, g], src).then_inc(stack_in[g], 16)
        row += times * HD


def build(nc, x, ln_w, ln_b, wq, wk, wv, wo, w_red, wg, W1, b1, W2, b2, out):
    qparts = nc.dram_tensor("qparts", (PARTS, PAIRS, P, S), BF16, kind="Internal").ap()
    kparts = nc.dram_tensor("kparts", (PARTS, PAIRS, P, S), BF16, kind="Internal").ap()
    vrows = nc.dram_tensor("vrows", (PAIRS, S, H // 2 * HD), F32, kind="Internal").ap()
    xz_dram = nc.dram_tensor("xz_dram", (NCH, CH, D), F32, kind="Internal").ap()
    attn_dram = nc.dram_tensor("attn_dram", (PAIRS, S, P), F32, kind="Internal").ap()
    dealt = nc.dram_tensor("dealt", (E * REGION + P, ROWW), F32, kind="Internal").ap()

    with ExitStack() as ctx:
        def sb(name, shape, dt=F32):
            return ctx.enter_context(nc.sbuf_tensor(name, shape, dt))

        def sem(name):
            return ctx.enter_context(nc.semaphore(name))

        psum = ctx.enter_context(nc.psum_tensor("psum", [P, 8, 512], F32))
        c = dict(
            ident=sb("ident", [P, P]), identb=sb("identb", [P, P], BF16),
            mask=sb("mask", [P, P], BF16), below=sb("below", [P, P], BF16), ones=sb("ones", [P, P], BF16),
            lnw=sb("lnw", [P, DK]), lnb=sb("lnb", [P, DK]), minus_half=sb("minus_half", [P, CT]),
            counts=sb("counts", [P, E]), wr=sb("wr", [P, DK, E]), wo=sb("wo_sb", [P, DK, D]),
        )
        qst = sb("qst", [P, GU, 2, GH, CH], BF16)
        kst = sb("kst", [P, GU, GH, S], BF16)
        stack_in = [sem(f"stack_in{g}") for g in range(GU)]
        wo_in = sem("wo_in")

        stacks = qparts, kparts, qst, kst, stack_in
        projections(nc, psum, c, wo_in, x, ln_w, ln_b, wq, wk, wv, wo, w_red, wg,
                    stacks, vrows, xz_dram)
        w1 = sb("w1_sb", [P, E * DK * FF])
        w2 = sb("w2_sb", [P, E * FK * D])
        b1s = sb("b1s", [P, E * FK])
        b2s = sb("b2s", [P, E * D])
        tile_row = sb("tile_row", [1, TILES], I32)
        tile_expert = sb("tile_expert", [1, TILES], I32)
        experts_in = sem("experts_in")
        attention(nc, psum, c, stacks, vrows, attn_dram, (W1, b1, W2, b2), (w1, b1s, w2, b2s), experts_in)
        routing(nc, psum, c, wo_in, attn_dram, xz_dram, dealt, tile_row, tile_expert)
        mlp(nc, psum, c["ident"], experts_in, w1, w2, b1s, b2s, tile_row, tile_expert, dealt, out)


def projections(nc, psum, c, wo_in, x, ln_w, ln_b, wq, wk, wv, wo, w_red, wg,
                stacks, vrows, xz_dram):
    qparts, kparts, qst, kst, stack_in = stacks
    with ExitStack() as ctx:
        def sb(name, shape, dt=F32):
            return ctx.enter_context(nc.sbuf_tensor(name, shape, dt))

        def sem(name):
            return ctx.enter_context(nc.semaphore(name))

        ident, identb, mask, below, ones = c["ident"], c["identb"], c["mask"], c["below"], c["ones"]
        lnw, lnb, minus_half = c["lnw"], c["lnb"], c["minus_half"]
        wqkv = sb("wqkv", [P, 3, DK, D])
        xt = sb("xt", [P, 2, CT, D])
        z = sb("z", [P, 2, CT, D])
        yn = sb("yn", [P, 2, CT, D])
        xz = sb("xz", [P, 2, CT, D])
        yT = sb("yT", [P, 2, DK, CH])
        warm = sb("warm", [P, DK])
        parts = sb("parts", [P, 2, 4, PARTS, CH], BF16)
        rest = sb("rest", [P, 4, CH])
        vsb = sb("vsb", [P, 2, CT, H * HD])
        stats = sb("stats", [P, CT, 6])
        mv = sb("mv", [P, 2, 2, CT, 2])
        ve = sb("ve", [P, 2, 2, CT])
        rstd = sb("rstd", [P, 2, 2, CT])
        wgs = sb("wgs", [E, RED])
        wgq = sb("wgq", [E, RED])
        wgn = sb("wgn", [E, 4])
        wgT = sb("wgT", [RED, E])
        wred = sb("wred", [P, DK, RED])
        wredT = sb("wredT", [RED, DK, P])

        consts_set, half_set, ln_in, wqkv_in = sem("consts_set"), sem("half_set"), sem("ln_in"), sem("wqkv_in")
        router_in, router_dve, router_other = sem("router_in"), sem("router_dve"), sem("router_other")
        x_in = [sem(f"x_in{u}") for u in range(2)]
        var_ready, rstd_ready, ve_ready = sem("var_ready"), sem("rstd_ready"), sem("ve_ready")
        stats_ready, z_ready, yn_ready = sem("stats_ready"), sem("z_ready"), sem("yn_ready")
        xz_ready = sem("xz_ready")
        xz_out = [sem(f"xz_out{u}") for u in range(2)]
        turned, yT_ready = sem("turned"), sem("yT_ready")
        qk_ready, v_ready = sem("qk_ready"), sem("v_ready")
        part1, rest_ready, part2, part3 = sem("part1"), sem("rest_ready"), sem("part2"), sem("part3")
        v_copied = sem("v_copied")
        parts_out = [sem(f"parts_out{u}") for u in range(2)]
        v_out = [sem(f"v_out{u}") for u in range(2)]

        block = ctx.enter_context(nc.Block())
        N2 = NCH // 2

        @block.sync
        def _(sp):
            def load_x(i, u):
                sp.dma_start(xt[:, u], x[bass.ds(lin(i, u, 2, 1), 1)].rearrange("o (t p) d -> p (o t) d", p=P)
                             ).then_inc(x_in[u], 16)

            passed = sem("sp_passed")

            def residual(i, u, load=True):
                wait(sp, xz_ready, lin(i, u, 2, 1, 1))
                sp.dma_start(xz_dram[bass.ds(lin(i, u, 2, 1), 1)].rearrange("o (t p) d -> p (o t) d", p=P),
                             xz[:, u]).then_inc(xz_out[u], 16)
                if load:
                    load_x(i + 1, u)

            def store(i, u, m):
                wait(sp, part3, lin(i, u, 2, 4, m + 1))
                dst = (qparts if m < 2 else kparts)[:, bass.ds(i + (m % 2) * B, 1), :, u * CH:(u + 1) * CH]
                sp.dma_start(dst.rearrange("a o p n -> p (o a) n"), parts[:, u, m]).then_inc(parts_out[u], 16)

            def store_v(i, u):
                wait_alone(sp, v_copied, lin(i, u, 2, 2, 2), passed)
                for half in range(2):
                    dst = vrows[bass.ds(i + half * B, 1), u * CH:(u + 1) * CH]
                    sp.dma_start(dst.rearrange("o (t p) n -> p (o t) n", p=P),
                                 vsb[:, u, :, half * P:half * P + P]).then_inc(v_out[u], 16)

            def chunk(i, u, ahead=True, load=True):
                store(i, u, 0)
                if ahead:
                    residual(i + 1, u, load)
                for m in range(1, 4):
                    store(i, u, m)
                store_v(i, u)

            load_x(0, 0)
            load_x(0, 1)
            for u in range(2):
                residual(0, u)
            with sp.Fori(0, N2 - 2) as i:
                for u in range(2):
                    chunk(i, u)
            for u in range(2):
                chunk(N2 - 2, u, load=False)
            for u in range(2):
                sp.wait_ge(parts_out[u], 64)
            load_stack(sp, stacks, 0, 0)
            for u in range(2):
                chunk(N2 - 1, u, ahead=False)
            load_stack(sp, stacks, 0, 1)
            for u in range(2):
                sp.wait_ge(xz_out[u], 16 * N2)
                sp.wait_ge(parts_out[u], 64 * N2)
                sp.wait_ge(v_out[u], 32 * N2)

        @block.gpsimd
        def _(pool):
            passed = sem("pool_passed")
            pool.memset(ident[:, :], 0.0).then_inc(consts_set, 1)
            pool.memset(minus_half[:, :], -0.5).then_inc(consts_set, 1)
            pool.memset(mask[:, :], 0.0).then_inc(consts_set, 1)
            pool.memset(ones[:, :], 1.0).then_inc(consts_set, 1)
            pool.memset(c["counts"][:, :], 0.0).then_inc(consts_set, 1)
            pool.wait_ge(consts_set, 5)
            pool.affine_select(out=ident[:, :], in_=ident[:, :], compare_op=ALU.not_equal, fill=1.0, base=0,
                               pattern=[[-1, P]], channel_multiplier=1).then_inc(consts_set, 1)
            pool.affine_select(out=mask[:, :], in_=mask[:, :], compare_op=ALU.is_ge, fill=MASK, base=0,
                               pattern=[[-1, P]], channel_multiplier=1).then_inc(consts_set, 1)
            pool.affine_select(out=below[:, :], in_=ones[:, :], compare_op=ALU.is_gt, fill=0.0, base=0,
                               pattern=[[1, P]], channel_multiplier=-1).then_inc(consts_set, 1)
            pool.wait_ge(consts_set, 8)
            pool.tensor_copy(identb[:, :], ident[:, :]).then_inc(consts_set, 1)

            def chunk(i, u):
                for norm in range(2):
                    wait_alone(pool, var_ready, lin(i, u, 2, 2, norm + 1), passed)
                    pool.tensor_scalar(ve[:, u, norm], mv[:, u, norm, :, 1], EPS, None, ALU.add).then_inc(ve_ready, 1)
                    wait(pool, ve_ready, lin(i, u, 2, 2, norm + 1))
                    pool.tensor_tensor(rstd[:, u, norm], ve[:, u, norm], minus_half[:, :], ALU.pow).then_inc(rstd_ready, 1)
                wait(pool, xz_out[u], lin(i, 0, 1, 16))
                wait(pool, z_ready, lin(i, u, 2, 1, 1))
                pool.tensor_tensor(xz[:, u], xt[:, u], z[:, u], ALU.add).then_inc(xz_ready, 1)

            for u in range(2):
                chunk(0, u)
            pool.wait_ge(router_dve, 1)
            pool.tensor_tensor(wgn[:, 1:2], wgn[:, 0:1], wgn[:, 3:4], ALU.pow).then_inc(router_other, 1)
            with pool.Fori(1, N2) as i:
                for u in range(2):
                    chunk(i, u)
            pool.wait_ge(xz_ready, NCH)
            pool.memset(kst[KROWS:MROWS], 1.0)

        @block.vector
        def _(dve):
            passed = sem("dve_passed")

            def router_length():
                dve.memset(wgn[:, 3:4], 0.5).then_inc(half_set, 1)
                dve.wait_ge(half_set, 1)
                dve.wait_ge(router_in, 32)
                dve.tensor_tensor_reduce(wgq[:, :], wgs[:, :], wgs[:, :], 1.0, 0.0, ALU.mult, ALU.add,
                                         wgn[:, 0:1]).then_inc(router_dve, 1)
                dve.wait_ge(router_other, 1)
                dve.tensor_scalar(wgn[:, 2:3], wgn[:, 1:2], 1e-4, None, ALU.max).then_inc(router_dve, 1)
                dve.wait_ge(router_dve, 2)
                dve.reciprocal(wgn[:, 0:1], wgn[:, 2:3]).then_inc(router_dve, 1)
                dve.wait_ge(router_dve, 3)
                dve.tensor_scalar(wgq[:, :], wgs[:, :], wgn[:, 0:1], None, ALU.mult).then_inc(router_dve, 1)

            def router_turned():
                dve.wait_ge(router_other, 2)
                dve.tensor_copy(wgT[:, :], psum[0:RED, 6, 0:E]).then_inc(router_dve, 1)
                dve.tensor_copy(wredT[:, :, :], psum[0:RED, 7, 0:DK * P].rearrange("r (k p) -> r k p", k=DK)
                                ).then_inc(router_dve, 1)

            def router_product():
                dve.wait_ge(router_other, 3)
                dve.tensor_copy(c["wr"][:, :, :], psum[:, 6, 0:DK * E].rearrange("p (k e) -> p k e", k=DK)
                                ).then_inc(router_dve, 1)

            def statistics(i, u, norm):
                src = z if norm else xt
                if norm == 0:
                    wait(dve, x_in[u], lin(i, 0, 1, 16, 16))
                for t in range(CT):
                    last = dve.bn_stats(stats[:, t], src[:, u, t])
                last.then_inc(stats_ready, 1)
                wait_alone(dve, stats_ready, lin(i, u, 2, 2, norm + 1), passed)
                for t in range(CT):
                    last = dve.bn_aggr(mv[:, u, norm, t], stats[:, t])
                last.then_inc(var_ready, 1)

            def normalised(i, u, norm):
                src, dst = ((xt, z), (z, yn))[norm]
                wait(dve, rstd_ready, lin(i, u, 2, 2, norm + 1))
                if norm:
                    wait(dve, turned, lin(i, u, 2, 1, -1))
                else:
                    wait(dve, xz_ready, lin(i, u, 2, 1, -1))
                for t in range(CT):
                    last = dve.tensor_scalar(dst[:, u, t], src[:, u, t], mv[:, u, norm, t, 0:1],
                                             rstd[:, u, norm, t:t + 1], ALU.subtract, ALU.mult)
                if norm:
                    last.then_inc(yn_ready, 1)
                else:
                    last.then_inc(z_ready, 1)
                    wait(dve, z_ready, lin(i, u, 2, 1, 1))

            def second(i, u, m):
                wait(dve, part1, lin(i, u, 2, 4, m + 1))
                dve.tensor_tensor(rest[:, m], psum[:, m], parts[:, u, m, 0], ALU.subtract).then_inc(rest_ready, 1)

            def third(i, u, m):
                wait(dve, part2, lin(i, u, 2, 4, m + 1))
                dve.tensor_tensor(parts[:, u, m, 2], rest[:, m], parts[:, u, m, 1], ALU.subtract).then_inc(part3, 1)

            def round_of(split, norms=None):
                if norms:
                    statistics(*norms, 0)
                second(*split, 0)
                second(*split, 1)
                if norms:
                    normalised(*norms, 0)
                    statistics(*norms, 1)
                third(*split, 0)
                second(*split, 2)
                third(*split, 1)
                second(*split, 3)
                if norms:
                    normalised(*norms, 1)
                third(*split, 2)
                third(*split, 3)

            for u in range(2):
                for norm in range(2):
                    statistics(0, u, norm)
                    normalised(0, u, norm)
            router_length()
            with dve.Fori(1, N2) as i:
                for u in range(2):
                    round_of((i - 1, u), (i, u))
            for u in range(2):
                round_of((N2 - 1, u))
            router_turned()
            router_product()

        @block.scalar
        def _(act):
            act.dma_start(wgs[:, :], wg).then_inc(router_in, 16)
            act.dma_start(wred[:, :, :], w_red.rearrange("(k p) r -> p k r", p=P)).then_inc(router_in, 16)
            act.dma_start(lnw[:, :], ln_w.rearrange("(k p) -> p k", p=P), allow_slow_non_contiguous=True).then_inc(ln_in, 16)
            act.dma_start(lnb[:, :], ln_b.rearrange("(k p) -> p k", p=P), allow_slow_non_contiguous=True).then_inc(ln_in, 16)
            for n, w in enumerate((wq, wk, wv)):
                for k in range(DK):
                    act.dma_start(wqkv[:, n, k].rearrange("p (h e) -> p h e", h=H),
                                  w[:, k * P:(k + 1) * P, :].rearrange("h p e -> p h e")).then_inc(wqkv_in, 16)
            act.dma_start(c["wo"][:, :, :], wo.rearrange("(k p) d -> p k d", p=P)).then_inc(wo_in, 16)

            def evacuate(i, u):
                wait(act, turned, lin(i, u, 2, 1, 1))
                for k in range(DK):
                    last = act.activation(yT[:, u, k], psum[:, 6 + k], ACT.Identity, bias=lnb[:, k:k + 1],
                                          scale=lnw[:, k:k + 1])
                last.then_inc(yT_ready, 1)

            def split(i, u, after=None):
                def first(m):
                    wait(act, qk_ready, lin(i, u, 2, 4, m + 1))
                    act.activation(parts[:, u, m, 0], psum[:, m], ACT.Copy).then_inc(part1, 1)

                def second(m):
                    wait(act, rest_ready, lin(i, u, 2, 4, m + 1))
                    act.activation(parts[:, u, m, 1], rest[:, m], ACT.Copy).then_inc(part2, 1)

                def values(half):
                    wait(act, v_ready, lin(i, u, 2, 2, half + 1))
                    if half == 0:
                        wait(act, v_out[u], lin(i, 0, 1, 32))
                    act.activation(vsb[:, u, 2 * half:2 * half + 2],
                                   psum[:, 4 + half].rearrange("p (t d) -> p t d", t=2), ACT.Copy
                                   ).then_inc(v_copied, 1)

                wait(act, parts_out[u], lin(i, 0, 1, 64))
                first(0)
                first(1)
                second(0)
                first(2)
                second(1)
                first(3)
                if after:
                    evacuate(*after)
                second(2)
                second(3)
                values(0)
                values(1)

            act.wait_ge(ln_in, 32)
            act.activation(warm[:, :], lnw[:, :], ACT.Identity)
            evacuate(0, 0)
            split(0, 0, (0, 1))
            split(0, 1, (1, 0))
            with act.Fori(1, N2 - 1) as i:
                split(i, 0, (i, 1))
                split(i, 1, (i + 1, 0))
            split(N2 - 1, 0, (N2 - 1, 1))
            split(N2 - 1, 1)

        @block.tensor
        def _(pe):
            pe.wait_ge(consts_set, 9)

            def turn_router():
                pe.wait_ge(router_dve, 4)
                pe.wait_ge(yT_ready, NCH)
                pe.transpose(psum[0:RED, 6, 0:E], wgq[:, :], ident[0:E, 0:E])
                for k in range(DK):
                    last = pe.transpose(psum[0:RED, 7, k * P:(k + 1) * P], wred[:, k], ident[:, :])
                last.then_inc(router_other, 1)

            def fold_router():
                pe.wait_ge(router_dve, 6)
                for k in range(DK):
                    last = pe.matmul(psum[:, 6, k * E:(k + 1) * E], wredT[:, k], wgT[:, :], start=True, stop=True)
                last.then_inc(router_other, 1)

            def turn(i, u):
                wait(pe, yn_ready, lin(i, u, 2, 1, 1))
                wait(pe, yT_ready, lin(i, u, 2, 1))
                for k in range(DK):
                    for t in range(CT):
                        last = pe.transpose(psum[:, 6 + k, t * P:(t + 1) * P], yn[:, u, t, k * P:(k + 1) * P],
                                            ident[:, :])
                last.then_inc(turned, 1)

            def project(i, u, after=None):
                wait(pe, yT_ready, lin(i, u, 2, 1, 1))
                for m in range(4):
                    wait(pe, rest_ready, lin(i, u, 2, 4, m - 3))
                    for k in range(DK):
                        last = pe.matmul(psum[:, m], wqkv[:, m // 2, k, (m % 2) * P:(m % 2 + 1) * P],
                                         yT[:, u, k], start=(k == 0), stop=(k == DK - 1))
                    last.then_inc(qk_ready, 1)
                if after:
                    turn(*after)
                else:
                    turn_router()
                for t in range(CT):
                    if t % 2 == 0:
                        wait(pe, v_copied, lin(i, u, 2, 2, t // 2 - 1))
                    for k in range(DK):
                        last = pe.matmul(psum[:, 4 + t // 2, (t % 2) * D:(t % 2 + 1) * D],
                                         yT[:, u, k, t * P:(t + 1) * P], wqkv[:, 2, k],
                                         start=(k == 0), stop=(k == DK - 1))
                    if t % 2:
                        last.then_inc(v_ready, 1)

            turn(0, 0)
            pe.wait_ge(wqkv_in, 96)
            project(0, 0, (0, 1))
            project(0, 1, (1, 0))
            with pe.Fori(1, N2 - 1) as i:
                project(i, 0, (i, 1))
                project(i, 1, (i + 1, 0))
            project(N2 - 1, 0, (N2 - 1, 1))
            project(N2 - 1, 1)
            fold_router()


UNITS = [(0, j) for j in range(4)] + [(1, j) for j in range(8)]
ITEMS = [(0, 0, 4), (1, 0, 4)] + [(i, h, 2) for i in (2, 3) for h in (0, 2)] + [
    (i, h, 1) for i in range(4, 8) for h in range(4)]
NU = len(UNITS)
EVACUATE = (15, 0)
SB = 3
GU = 4
NG = GROUPS // GU


def columns(c, j):
    return CH - max(0, j - 4 * c) * P


STEPS = []
for _n, _unit in enumerate(UNITS):
    _heads = {4: [1] * 4, 3: [1] * 4, 2: [2, 1, 1] if _n < 4 else [2, 2], 1: [4]}[columns(*_unit) // P]
    STEPS += [(_n, sum(_heads[:_k]), _nh) for _k, _nh in enumerate(_heads)]
NS = len(STEPS)
assert NS % SB == 0


def steps_to(n):
    return len([1 for step in STEPS if step[0] <= n])


WEIGH = [1, 7, 10, 11, 15, 19, 22, 29, 32, 35, 37, 38]

ROTATION = {0: [21], 2: [20], 4: ["o1", "m1"], 7: [0], 9: [2], 10: [4], 11: [1], 12: [3], 14: [5], 16: [6],
            18: ["o0"], 19: [9], 20: [7], 22: ["m0"], 23: [8], 24: [11], 26: [13], 28: [12], 30: [10], 31: [17],
            33: [15], 34: [16], 36: [14], 37: [19], 38: [18]}
ORDER = [(s, e) for s in sorted(ROTATION) for e in ROTATION[s]]
NAMES = [e for _, e in ORDER]
ENTRIES = len(ORDER)
OWN = NAMES.index(0)
FIRST = [e for e in NAMES[OWN:] if e != "o0"]
assert ENTRIES % 2 == 0
for _m, _items in (("m0", range(6)), ("m1", range(6, 22))):
    assert all((NAMES.index(_m) - OWN) % ENTRIES >= (NAMES.index(_k) - OWN) % ENTRIES + 2 for _k in _items)


def attention(nc, psum, c, stacks, vrows, attn_dram, experts, resident, experts_in):
    qparts, kparts, qst, kst, stack_in = stacks
    with ExitStack() as ctx:
        def sb(name, shape, dt=F32):
            return ctx.enter_context(nc.sbuf_tensor(name, shape, dt))

        def sem(name):
            return ctx.enter_context(nc.semaphore(name))

        ident, identb, mask = c["ident"], c["identb"], c["mask"]
        vraw = sb("vraw", [P, 2, ST, GH * HD])
        vst = sb("vst", [P, 2, ST, GH * VW])
        pT = sb("pT", [P, 3, GH, CH])
        oT = sb("oT", [P, 2, CH])
        mneg = sb("mneg", [P, 2, 2, GH * CT])
        mparts = sb("mparts", [GH * CT, 2, PARTS, P], BF16)
        mrest = sb("mrest", [GH * CT, P])
        rsum = sb("rsum", [P, 2, CT, GH])
        attn = sb("attn", [P, 2, ST, P])

        oT_set = sem("oT_set")
        v_in = [sem(f"v_in{g}") for g in range(2)]
        v_columns_set, v_placed = sem("v_columns_set"), sem("v_placed")
        m_in = [sem(f"m_in{half}") for half in range(2)]
        attn_out = [sem(f"attn_out{g}") for g in range(2)]
        filled, drained = sem("filled"), sem("drained")
        m_split, m_chain = sem("m_split"), sem("m_chain")
        st_ready, exp_done, masked, pv_done = sem("st_ready"), sem("exp_done"), sem("masked"), sem("pv_done")
        oT_ready, rsum_ready = sem("oT_ready"), sem("rsum_ready")


        def at(i, g, pos):
            return lin(i, g, GU, ENTRIES, len(FIRST) + pos + 1)

        def owner(entry):
            if entry == "o1":
                return -1
            return 0 if entry == "o0" or NAMES.index(entry) < OWN else 1

        END = len(FIRST) + len([e for e in NAMES if owner(e) < 1])

        block = ctx.enter_context(nc.Block())

        def over_groups(eng, group):
            for g in range(GU):
                group(0, g)
            with eng.Fori(1, NG - 1) as i:
                for g in range(GU):
                    group(i, g)
            for g in range(GU):
                group(NG - 1, g, last=(g == GU - 1))

        @block.sync
        def _(sp):
            passed = sem("sp_passed2")

            def load_v(i, g):
                i, g = i + g // GU, g % GU
                src = vrows[bass.ds(lin(i, g // 2, 2, 1), 1), :, (g % 2) * GH * HD:(g % 2 + 1) * GH * HD]
                sp.dma_start(vraw[:, g % 2], src.rearrange("o (t p) n -> p (o t) n", p=P)).then_inc(v_in[g % 2], 16)

            def load_max(i, g, half):
                wait(sp, m_split, lin(i, g, GU, 2, half + 1))
                for part in range(PARTS):
                    row = KROWS + part
                    sp.dma_start(qst[row:row + 1, g % GU, half].rearrange("o h (t n) -> o (h t) n", n=P),
                                 mparts[:, half, part]).then_inc(m_in[half], 16)

            def store(i, g, count=None):
                wait_alone(sp, drained, at(i, g, NAMES.index("o1")) if count is None else count, passed)
                pair = lin(i, g // 2, 2, 1, -1)
                buf = (g // 2 + 1) % 2
                sp.dma_start(attn_dram[bass.ds(pair, 1)].rearrange("o (t p) n -> p (o t) n", p=P),
                             attn[:, buf]).then_inc(attn_out[buf], 16)

            def group(i, g, last=False):
                wait_alone(sp, pv_done, lin(i, g, GU, NU), passed)
                if not last:
                    load_v(i, g + 1)
                load_max(i, g, 1)
                if not (isinstance(i, int) and i * GU + g + 2 >= GROUPS):
                    load_stack(sp, stacks, i, g + 2)
                if g % 2 == 0 and not (isinstance(i, int) and i * GU + g == 0):
                    store(i, g)
                if not last:
                    load_max(i, g + 1, 0)

            load_v(0, 0)
            load_max(0, 0, 0)
            over_groups(sp, group)
            store(NG, 0, at(NG - 1, GU - 1, END - len(FIRST)))
            for buf in range(2):
                sp.wait_ge(attn_out[buf], 16 * NG)

        @block.gpsimd
        def _(pool):
            passed = sem("pool_passed2")
            pool.memset(vst[:, :, :, :], 0.0).then_inc(v_columns_set, 1)
            pool.wait_ge(v_columns_set, 1)
            columns_of = vst[:, :, :, :].rearrange("p g t (h w) -> p (g t h) w", w=VW)
            pool.memset(columns_of[:, :, HD:HD + 1], 1.0).then_inc(v_columns_set, 1)
            pool.wait_ge(v_columns_set, 2)

            def place(i, g):
                i, g = i + g // GU, g % GU
                wait_alone(pool, pv_done, lin(i, g, GU, NU, -NU), passed)
                wait_alone(pool, v_in[g % 2], lin(i, g // 2, 2, 16, 16), passed)
                pool.tensor_copy(vst[:, g % 2].rearrange("p t (h w) -> p (t h) w", w=VW)[:, :, 0:HD],
                                 vraw[:, g % 2].rearrange("p t (h d) -> p (t h) d", d=HD)).then_inc(v_placed, 1)

            def group(i, g, last=False):
                for n, (half, j) in enumerate(UNITS):
                    if j >= 4 * half:
                        wait_alone(pool, exp_done, lin(i, g, GU, NS, steps_to(n)), passed)
                        part = pT[:, n % 3, :, 0:P]
                        pool.affine_select(out=part, in_=part, compare_op=ALU.is_ge, fill=0.0, base=0,
                                           pattern=[[0, GH], [1, P]], channel_multiplier=-1).then_inc(masked, 1)
                    if n == 3 and not last:
                        place(i, g + 1)

            place(0, 0)
            over_groups(pool, group)

        @block.scalar
        def _(act):
            def evacuate(i, g, half):
                wait(act, pv_done, lin(i, g, GU, NU, 4 + 8 * half))
                act.activation(oT[:, half], psum[:, 7], ACT.Copy).then_inc(oT_ready, 1)

            def load_expert(e):
                act.dma_start(w1[:, e * DK * FF:(e + 1) * DK * FF].rearrange("p (k f) -> p k f", k=DK),
                              W1[e].rearrange("(k p) f -> p k f", p=P)).then_inc(experts_in, 16)
                act.dma_start(w2[:, e * FK * D:(e + 1) * FK * D].rearrange("p (k f) -> p k f", k=FK),
                              W2[e].rearrange("(k p) f -> p k f", p=P)).then_inc(experts_in, 16)

            def group(i, g, last=False):
                for s, (n, h0, nh) in enumerate(STEPS):
                    cols = columns(*UNITS[n])
                    if h0 == 0:
                        wait(act, pv_done, lin(i, g, GU, NU, n - 2))
                    wait(act, st_ready, lin(i, g, GU, NS, s + 1))
                    act.activation(pT[:, n % 3, h0:h0 + nh, 0:cols],
                                   psum[:, 4 + s % SB, 0:nh * cols].rearrange("p (h n) -> p h n", h=nh), ACT.Exp,
                                   scale=HD ** -0.5).then_inc(exp_done, 1)
                    if s == EVACUATE[1] and not (isinstance(i, int) and i * GU + g == 0):
                        evacuate(i, g - 1, 1)
                    if s == EVACUATE[0]:
                        evacuate(i, g, 0)
                    if isinstance(i, int) and i == 0 and s == NS // 2:
                        for e in range(g * E // GU, (g + 1) * E // GU):
                            load_expert(e)

            (W1, b1, W2, b2), (w1, b1s, w2, b2s) = experts, resident
            act.dma_start(b1s[:, :], b1.rearrange("e (k p) -> p (e k)", p=P), allow_slow_non_contiguous=True
                          ).then_inc(experts_in, 16)
            act.dma_start(b2s[:, :], b2.rearrange("(o e) f -> o (e f)", o=1).broadcast_to([P, E * D])
                          ).then_inc(experts_in, 16)
            over_groups(act, group)
            evacuate(NG - 1, GU - 1, 1)

        @block.vector
        def _(dve):
            def largest(g, k, buf, count):
                tile, h0, n = ITEMS[k]
                cols = (tile + 1) * P
                wait(dve, filled, count)
                src = psum[:, 2 * buf:2 * buf + 2]
                flat = src.rearrange("p b n -> p (b n)")
                if tile < 2:
                    src = flat[:, 0:n * cols].rearrange("p (h n) -> p h n", h=n)
                elif tile < 4:
                    src = src[:, :, 0:cols]
                else:
                    src = flat[:, 0:cols]
                dst = mneg[:, g % 2, tile // CT].rearrange("p (h t) -> p h t", t=CT)[:, h0:h0 + n, tile % CT]
                dve.tensor_reduce(dst, src, X, ALU.max, negate=True).then_inc(drained, 1)

            def split_max(i, g, half, buf, count):
                wait(dve, filled, count)
                wait(dve, m_in[half], lin(i, g, GU, 16 * PARTS))
                turned = psum[0:GH * CT, 2 * buf, 0:P]
                p1, p2, p3 = (mparts[:, half, k] for k in range(PARTS))
                dve.tensor_copy(p1, turned).then_inc(m_chain, 1)
                wait(dve, m_chain, lin(i, g, GU, 4, 2 * half + 1))
                dve.tensor_tensor(mrest[:, :], turned, p1, ALU.subtract).then_inc(drained, 1)
                wait(dve, drained, count)
                dve.tensor_copy(p2, mrest[:, :]).then_inc(m_chain, 1)
                wait(dve, m_chain, lin(i, g, GU, 4, 2 * half + 2))
                dve.tensor_tensor(p3, mrest[:, :], p2, ALU.subtract).then_inc(m_split, 1)

            def normalise(i, g, half, buf, count):
                wait(dve, filled, count)
                g4 = g % GU
                if half == 0 and g4 % 2 == 0:
                    wait(dve, attn_out[(g4 // 2) % 2], lin(i, 0, 1, 16))
                src = psum[:, 2 * buf].rearrange("p (t h w) -> p t h w", t=CT, w=VW)
                dve.reciprocal(rsum[:, half], src[:, :, :, HD]).then_inc(rsum_ready, 1)
                wait(dve, rsum_ready, lin(i, g, GU, 2, half + 2))
                dst = attn[:, (g4 // 2) % 2, half * CT:(half + 1) * CT, (g4 % 2) * GH * HD:(g4 % 2 + 1) * GH * HD]
                dve.tensor_tensor(dst.rearrange("p t (h d) -> p t h d", h=GH), src[:, :, :, 0:HD],
                                  rsum[:, half].rearrange("p t (h o) -> p t h o", o=1).broadcast_to([P, CT, GH, HD]),
                                  ALU.mult).then_inc(drained, 1)

            def drain(i, g, entry, buf, count):
                if entry in ("m0", "m1"):
                    split_max(i, g, int(entry[1]), buf, count)
                elif entry in ("o0", "o1"):
                    normalise(i, g, int(entry[1]), buf, count)
                else:
                    largest(g, entry, buf, count)

            def group(i, g, last=False):
                pos = 0
                for entry in NAMES:
                    if not (last and owner(entry) > 0):
                        drain(i, g + owner(entry), entry, (len(FIRST) + pos) % 2, at(i, g, pos))
                        pos += 1

            dve.memset(oT[:, 1], 1.0).then_inc(oT_set, 1)
            for pos, entry in enumerate(FIRST):
                drain(0, 0, entry, pos % 2, pos + 1)
            over_groups(dve, group)
            normalise(NG - 1, GU - 1, 1, END % 2, at(NG - 1, GU - 1, END - len(FIRST)))

        @block.tensor
        def _(pe):
            def first_pass(g, k, buf):
                tile, h0, n = ITEMS[k]
                b = g % GU
                cols = (tile + 1) * P
                buf = psum[:, 2 * buf:2 * buf + 2].rearrange("p b n -> p (b n)")
                for a in range(n):
                    h = h0 + a
                    at0 = a * cols if tile < 2 else a * 512
                    q = qst[0:KROWS, b, tile // CT, h, (tile % CT) * P:(tile % CT + 1) * P]
                    for t0 in range(0, cols, 512):
                        t1 = min(cols, t0 + 512)
                        pe.matmul(buf[:, at0 + t0:at0 + t1], q, kst[0:KROWS, b, h, t0:t1], start=True,
                                  stop=(t1 < cols), skip_group_check=True)
                    mm = pe.matmul(buf[:, at0 + cols - P:at0 + cols], identb[:, :], mask[:, :], start=False,
                                   stop=True, skip_group_check=True)
                return mm

            def fill(i, g, entry, buf, count):
                if entry == 0:
                    wait(pe, stack_in[g % GU], lin(i + g // GU, 0, 1, 18 * 16, 18 * 16))
                if entry in ("o0", "o1"):
                    wait(pe, oT_ready, lin(i, g, GU, 2, int(entry[1]) + 1))
                wait(pe, drained, count - 2)
                if entry in ("m0", "m1"):
                    mm = pe.transpose(psum[0:GH * CT, 2 * buf, 0:P], mneg[:, g % 2, int(entry[1])], ident[:, :])
                elif entry in ("o0", "o1"):
                    for t in range(CT):
                        mm = pe.transpose(psum[:, 2 * buf, t * P:(t + 1) * P], oT[:, int(entry[1]), t * P:(t + 1) * P],
                                          ident[:, :])
                else:
                    mm = first_pass(g, entry, buf)
                mm.then_inc(filled, 1)

            def scores(i, g, s):
                n, h0, nh = STEPS[s]
                half, j = UNITS[n]
                cols = columns(half, j)
                if j == 0 and h0 == 0:
                    wait(pe, m_in[half], lin(i, g, GU, 16 * PARTS, 16 * PARTS))
                wait(pe, exp_done, lin(i, g, GU, NS, s + 1 - SB))
                for a in range(nh):
                    mm = pe.matmul(psum[:, 4 + s % SB, a * cols:(a + 1) * cols],
                                   kst[0:MROWS, g, h0 + a, j * P:(j + 1) * P],
                                   qst[0:MROWS, g, half, h0 + a, CH - cols:CH], start=True, stop=True)
                mm.then_inc(st_ready, 1)

            def weigh(i, g, n):
                half, j = UNITS[n]
                cols = columns(half, j)
                if n == 0:
                    wait(pe, v_placed, lin(i, g, GU, 1, 1))
                if j == 0:
                    wait(pe, oT_ready, lin(i, g, GU, 2, half))
                if j >= 4 * half:
                    wait(pe, masked, lin(i, g, GU, 8, j + 1))
                else:
                    wait(pe, exp_done, lin(i, g, GU, NS, steps_to(n)))
                for h in range(GH):
                    mm = pe.matmul(psum[32 * h:32 * h + 32, 7, CH - cols:CH], vst[:, g % 2, j, h * VW:(h + 1) * VW],
                                   pT[:, n % 3, h, 0:cols], start=(j == 0), stop=(j == 4 * half + 3),
                                   skip_group_check=True)
                mm.then_inc(pv_done, 1)

            def group(i, g, last=False):
                pos = 0
                for s in range(NS):
                    scores(i, g, s)
                    for entry in ROTATION.get(s, []):
                        if not (last and owner(entry) > 0):
                            fill(i, g + owner(entry), entry, (len(FIRST) + pos) % 2, at(i, g, pos))
                            pos += 1
                    if s in WEIGH:
                        n = WEIGH.index(s)
                        if n > 0:
                            weigh(i, g, n - 1)
                        elif not (isinstance(i, int) and i * GU + g == 0):
                            weigh(i, g - 1, NU - 1)

            pe.wait_ge(oT_set, 1)
            for pos, entry in enumerate(FIRST):
                fill(0, 0, entry, pos % 2, pos + 1)
            over_groups(pe, group)
            weigh(NG - 1, GU - 1, NU - 1)
            fill(NG - 1, GU - 1, "o1", END % 2, at(NG - 1, GU - 1, END - len(FIRST)))


def routing(nc, psum, c, wo_in, attn_dram, xz_dram, dealt, tile_row, tile_expert):
    with ExitStack() as ctx:
        def sb(name, shape, dt=F32):
            return ctx.enter_context(nc.sbuf_tensor(name, shape, dt))

        def sem(name):
            return ctx.enter_context(nc.semaphore(name))

        ident, below, ones, counts = c["ident"], c["below"], c["ones"], c["counts"]
        RU = 4
        at = sb("at", [P, 2, 2, CT, P])
        xz = sb("xz_r", [P, 2, CT, D])
        aT = sb("aT", [P, 2, DK, CH])
        rows = sb("rows", [P, RU, CT, ROWW])
        hn = sb("hn", [P, 2, CT, D])
        hT = sb("hT", [P, 2, DK, CH])
        stats = sb("stats_r", [P, CT, 6])
        mv = sb("mv_r", [P, 2, CT, 2])
        ve = sb("ve_r", [P, 2, CT])
        lmax = sb("lmax", [P, CT])
        shifted = sb("shifted", [P, CT, E])
        exps = sb("exps", [P, CT, E])
        expsum = sb("expsum", [P, CT])
        order = sb("order", [P, CT, E])
        first = sb("first", [P, CT, E])
        best = sb("best", [P, CT])
        chosen = sb("chosen", [P, CT, E], BF16)
        place = sb("place", [P, CT, E])
        slot = sb("slot", [P, RU, CT], I32)
        token = sb("token", [P, CT])
        nobody = sb("nobody", [P, ROWW])
        ends = sb("ends", [1, E], I32)
        start = sb("start", [1, E])
        held = sb("held", [1, E])
        grid = sb("grid", [1, E, NTOK // P])
        ntiles = sb("ntiles", [1, E])
        ones8 = sb("ones8", [1, E])
        upto = sb("upto", [1, E])
        jgrid = sb("jgrid", [1, TILES, E])
        behind = sb("behind", [1, TILES, E])
        ej = sb("ej", [1, TILES])
        cj = sb("cj", [1, TILES])
        rj = sb("rj", [1, TILES])
        rk = sb("rk", [1, TILES])

        at_in = [sem(f"at_in{u}") for u in range(2)]
        xz_in = [sem(f"xz_in{u}") for u in range(2)]
        tables_set = sem("tables_set")
        a_turned, aT_ready, wo_ready, x1_ready = sem("a_turned"), sem("aT_ready"), sem("wo_ready"), sem("x1_ready")
        stats_ready, var_ready, rstd_ready, ve_ready = (
            sem("stats_ready2"), sem("var_ready2"), sem("rstd_ready2"), sem("ve_ready2"))
        h_ready, h_turned, hT_ready = sem("h_ready"), sem("h_turned"), sem("hT_ready")
        logits_ready, shifted_ready, exp_ready = sem("logits_ready"), sem("shifted_ready"), sem("exp_ready")
        chosen_ready, rank_ready, slot_ready = sem("chosen_ready"), sem("rank_ready"), sem("slot_ready")
        step = sem("step")
        sent = [sem(f"sent{u}") for u in range(RU)]
        ends_ready, nobody_out, pads_out = sem("ends_ready"), sem("nobody_out"), sem("pads_out")

        block = ctx.enter_context(nc.Block())
        NR = NCH // RU

        def over_rounds(eng, one):
            for u in range(RU):
                one(0, u)
            with eng.Fori(1, NR - 1) as i:
                for u in range(RU):
                    one(i, u)
            for u in range(RU + 2):
                one(NR - 1, u)

        def absent(i, u):
            return isinstance(i, int) and not 0 <= i * RU + u < NCH

        @block.sync
        def _(sp):
            def load(i, u):
                n, part = lin(i, u // 2, RU // 2, 1), u % 2
                for half in range(2):
                    sp.dma_start(at[:, part, half], attn_dram[bass.ds(n + half * B, 1), part * CH:(part + 1) * CH
                                                              ].rearrange("o (t p) n -> p (o t) n", p=P)
                                 ).then_inc(at_in[part], 16)
                sp.dma_start(xz[:, part], xz_dram[bass.ds(lin(i, u, RU, 1), 1)].rearrange("o (t p) d -> p (o t) d", p=P)
                             ).then_inc(xz_in[part], 16)

            def chunk(i, u):
                if absent(i, u):
                    return
                wait(sp, a_turned, lin(i, u, RU, 1, -1))
                wait(sp, x1_ready, lin(i, u, RU, 1, -1))
                load(i, u)

            over_rounds(sp, chunk)
            sp.wait_ge(tables_set, 9)
            sp.dma_start(dealt[E * REGION:E * REGION + P, :], nobody[:, :]).then_inc(nobody_out, 16)
            sp.wait_ge(ends_ready, 1)
            for e in range(E):
                row = sp.value_load(ends[0:1, e:e + 1], min_val=0, max_val=E * REGION)
                sp.dma_start(dealt[bass.ds(row, P), :], nobody[:, :]).then_inc(pads_out, 16)
            sp.wait_ge(nobody_out, 16)
            sp.wait_ge(pads_out, 16 * E)

        @block.gpsimd
        def _(pool):
            passed = sem("pool_passed3")
            pool.iota(counts[:, :], pattern=[[REGION, E]], base=0, channel_multiplier=0,
                      allow_small_or_imprecise_dtypes=True).then_inc(tables_set, 1)
            pool.iota(start[:, :], pattern=[[REGION, E]], base=0, channel_multiplier=0,
                      allow_small_or_imprecise_dtypes=True).then_inc(tables_set, 1)
            pool.iota(order[:, :, :], pattern=[[0, CT], [-1, E]], base=E, channel_multiplier=0,
                      allow_small_or_imprecise_dtypes=True).then_inc(tables_set, 1)
            pool.iota(token[:, :], pattern=[[P, CT]], base=0, channel_multiplier=1,
                      allow_small_or_imprecise_dtypes=True).then_inc(tables_set, 1)
            pool.iota(grid[:, :, :], pattern=[[0, E], [P, NTOK // P]], base=0, channel_multiplier=0,
                      allow_small_or_imprecise_dtypes=True).then_inc(tables_set, 1)
            pool.iota(jgrid[:, :, :], pattern=[[1, TILES], [0, E]], base=0, channel_multiplier=0,
                      allow_small_or_imprecise_dtypes=True).then_inc(tables_set, 1)
            pool.memset(ones8[:, :], 1.0).then_inc(tables_set, 1)
            pool.memset(nobody[:, :], 0.0).then_inc(tables_set, 1)
            pool.wait_ge(tables_set, 8)
            pool.memset(nobody[:, D + 1:D + 2], float(NOWHERE)).then_inc(tables_set, 1)

            def deviation(i, u):
                if absent(i, u):
                    return
                wait_alone(pool, var_ready, lin(i, u, RU, 1, 1), passed)
                pool.tensor_scalar(ve[:, u % 2], mv[:, u % 2, :, 1], EPS, None, ALU.add).then_inc(ve_ready, 1)
                wait(pool, ve_ready, lin(i, u, RU, 1, 1))
                pool.tensor_tensor(rows[:, u % RU, :, D + 3], ve[:, u % 2], c["minus_half"][:, :], ALU.pow
                                   ).then_inc(rstd_ready, 1)

            def deal(i, u):
                if absent(i, u):
                    return
                wait_alone(pool, slot_ready, lin(i, u, RU, 1, 1), passed)
                for t in range(CT):
                    pool.indirect_dma_start(
                        out=dealt[:, :],
                        out_offset=bass.IndirectOffsetOnAxis(ap=slot[:, u % RU, t:t + 1].bitcast(U32), axis=0),
                        in_=rows[:, u % RU, t], in_offset=None).then_inc(sent[u % RU], 16)

            def one(i, u):
                deviation(i, u)
                deal(i, u - 2)

            over_rounds(pool, one)
            for u in range(RU):
                pool.wait_ge(sent[u], 16 * CT * NR)

        @block.scalar
        def _(act):
            def turn_attention(i, u):
                if absent(i, u):
                    return
                wait(act, a_turned, lin(i, u, RU, 1, 1))
                wait(act, wo_ready, lin(i, u, RU, 1, -1))
                act.activation(aT[:, u % 2], psum[:, 0:2], ACT.Copy).then_inc(aT_ready, 1)

            def turn_h(i, u):
                if absent(i, u):
                    return
                wait(act, h_turned, lin(i, u, RU, 1, 1))
                wait(act, logits_ready, lin(i, u, RU, 1, -1))
                act.activation(hT[:, u % 2], psum[:, 4:6], ACT.Copy).then_inc(hT_ready, 1)

            def gate(i, u):
                if absent(i, u):
                    return
                wait(act, shifted_ready, lin(i, u, RU, 1, 1))
                act.activation(exps[:, :, :], shifted[:, :, :], ACT.Exp).then_inc(exp_ready, 1)

            def one(i, u):
                gate(i, u - 2)
                turn_h(i, u - 1)
                turn_attention(i, u + 1)

            turn_attention(0, 0)
            over_rounds(act, one)

        @block.tensor
        def _(pe):
            pe.wait_ge(wo_in, 16)

            def turn_attention(i, u):
                if absent(i, u):
                    return
                wait(pe, at_in[u % 2], lin(i, u // 2, RU // 2, 32, 32))
                wait(pe, aT_ready, lin(i, u, RU, 1))
                for k in range(DK):
                    for t in range(CT):
                        mm = pe.transpose(psum[:, k, t * P:(t + 1) * P], at[:, u % 2, k, t], ident[:, :])
                mm.then_inc(a_turned, 1)

            def times_wo(i, u):
                if absent(i, u):
                    return
                wait(pe, aT_ready, lin(i, u, RU, 1, 1))
                wait(pe, x1_ready, lin(i, u, RU, 1))
                for t in range(CT):
                    for k in range(DK):
                        mm = pe.matmul(psum[:, 2 + t // 2, (t % 2) * D:(t % 2 + 1) * D],
                                       aT[:, u % 2, k, t * P:(t + 1) * P], c["wo"][:, k],
                                       start=(k == 0), stop=(k == DK - 1))
                mm.then_inc(wo_ready, 1)

            def turn_h(i, u):
                if absent(i, u):
                    return
                wait(pe, h_ready, lin(i, u, RU, 1, 1))
                wait(pe, hT_ready, lin(i, u, RU, 1))
                for k in range(DK):
                    for t in range(CT):
                        mm = pe.transpose(psum[:, 4 + k, t * P:(t + 1) * P], hn[:, u % 2, t, k * P:(k + 1) * P],
                                          ident[:, :])
                mm.then_inc(h_turned, 1)

            def logits(i, u):
                if absent(i, u):
                    return
                wait(pe, hT_ready, lin(i, u, RU, 1, 1))
                wait(pe, shifted_ready, lin(i, u, RU, 1))
                for t in range(CT):
                    for k in range(DK):
                        mm = pe.matmul(psum[:, 6, t * E:(t + 1) * E], hT[:, u % 2, k, t * P:(t + 1) * P], c["wr"][:, k],
                                       start=(k == 0), stop=(k == DK - 1))
                mm.then_inc(logits_ready, 1)

            def rank(i, u):
                if absent(i, u):
                    return
                wait(pe, chosen_ready, lin(i, u, RU, 1, 1))
                wait(pe, slot_ready, lin(i, u, RU, 1))
                flat = chosen[:, :, :].rearrange("p t e -> p (t e)")
                pe.matmul(psum[:, 7, 0:CT * E], below[:, :], flat, start=True, stop=False, skip_group_check=True)
                for t in range(1, CT):
                    for before in range(t):
                        pe.matmul(psum[:, 7, t * E:(t + 1) * E], ones[:, :], chosen[:, before], start=False,
                                  stop=True, skip_group_check=True)
                for t in range(CT):
                    mm = pe.matmul(psum[:, 7, CT * E:CT * E + E], ones[:, :], chosen[:, t], start=False,
                                   stop=(t == CT - 1), skip_group_check=True)
                mm.then_inc(rank_ready, 1)

            def one(i, u):
                times_wo(i, u)
                turn_h(i, u - 1)
                turn_attention(i, u + 1)
                rank(i, u - 2)
                logits(i, u - 1)

            turn_attention(0, 0)
            over_rounds(pe, one)

        @block.vector
        def _(dve):
            passed = sem("dve_passed3")
            dve.wait_ge(tables_set, 9)

            def normed(i, u):
                if absent(i, u):
                    return
                own = rows[:, u % RU]
                wait(dve, wo_ready, lin(i, u, RU, 1, 1))
                wait(dve, xz_in[u % 2], lin(i, u // 2, RU // 2, 16, 16))
                wait(dve, sent[u % RU], lin(i, 0, 1, 16 * CT))
                dve.tensor_tensor(own[:, :, 0:D], psum[:, 2:4].rearrange("p b (t d) -> p (b t) d", d=D), xz[:, u % 2],
                                  ALU.add).then_inc(x1_ready, 1)
                wait(dve, x1_ready, lin(i, u, RU, 1, 1))
                for t in range(CT):
                    last = dve.bn_stats(stats[:, t], own[:, t, 0:D])
                last.then_inc(stats_ready, 1)
                wait_alone(dve, stats_ready, lin(i, u, RU, 1, 1), passed)
                for t in range(CT):
                    last = dve.bn_aggr(mv[:, u % 2, t], stats[:, t])
                last.then_inc(var_ready, 1)
                wait(dve, var_ready, lin(i, u, RU, 1, 1))
                dve.tensor_copy(own[:, :, D + 2], mv[:, u % 2, :, 0])
                wait(dve, rstd_ready, lin(i, u, RU, 1, 1))
                wait(dve, h_turned, lin(i, u, RU, 1, -1))
                for t in range(CT):
                    last = dve.tensor_scalar(hn[:, u % 2, t], own[:, t, 0:D], mv[:, u % 2, t, 0:1],
                                             own[:, t, D + 3:D + 4], ALU.subtract, ALU.mult)
                last.then_inc(h_ready, 1)

            BEFORE, STEPS = 3, 7

            def stepwise(i, u, n):
                def then(ins):
                    nonlocal n
                    n += 1
                    ins.then_inc(step, 1)
                    wait(dve, step, lin(i, u, RU, STEPS, n))
                return then

            def choose(i, u):
                if absent(i, u):
                    return
                then = stepwise(i, u, 0)
                logits = psum[:, 6, 0:CT * E].rearrange("p (t e) -> p t e", e=E)

                def wide(a):
                    return a.rearrange("p (t o) -> p t o", o=1).broadcast_to([P, CT, E])

                wait(dve, logits_ready, lin(i, u, RU, 1, 1))
                then(dve.tensor_reduce(lmax[:, :], logits, X, ALU.max))
                dve.tensor_tensor(shifted[:, :, :], logits, wide(lmax[:, :]), ALU.subtract).then_inc(shifted_ready, 1)
                wait(dve, shifted_ready, lin(i, u, RU, 1, 1))
                then(dve.scalar_tensor_tensor(out=first[:, :, :], in0=shifted[:, :, :], scalar=0.0, in1=order[:, :, :],
                                              op0=ALU.is_equal, op1=ALU.mult))
                then(dve.tensor_reduce(best[:, :], first[:, :, :], X, ALU.max))
                dve.tensor_tensor(chosen[:, :, :], first[:, :, :], wide(best[:, :]), ALU.is_equal
                                  ).then_inc(chosen_ready, 1)

            def deal_out(i, u):
                if absent(i, u):
                    return
                then = stepwise(i, u, BEFORE)
                own = rows[:, u % RU]
                wait(dve, exp_ready, lin(i, u, RU, 1, 1))
                then(dve.tensor_reduce(expsum[:, :], exps[:, :, :], X, ALU.add))
                dve.reciprocal(own[:, :, D], expsum[:, :])
                dve.tensor_copy(own[:, :, D + 1], token[:, :])
                wait(dve, rank_ready, lin(i, u, RU, 1, 1))
                then(dve.tensor_tensor(place[:, :, :], psum[:, 7, 0:CT * E].rearrange("p (t e) -> p t e", e=E),
                                       counts[:, :].rearrange("p (o e) -> p o e", o=1).broadcast_to([P, CT, E]),
                                       ALU.add))
                dve.tensor_scalar(token[:, :], token[:, :], float(CH), None, ALU.add)
                then(dve.tensor_tensor(first[:, :, :], place[:, :, :], chosen[:, :, :], ALU.mult))
                dve.tensor_tensor(counts[:, :], psum[:, 7, CT * E:CT * E + E], counts[:, :], ALU.add)
                then(dve.tensor_reduce(best[:, :], first[:, :, :], X, ALU.add))
                dve.tensor_copy(slot[:, u % RU], best[:, :]).then_inc(slot_ready, 1)

            def one(i, u):
                choose(i, u - 2)
                normed(i, u)
                deal_out(i, u - 2)

            over_rounds(dve, one)

            done = STEPS * NCH

            def then(ins):
                nonlocal done
                done += 1
                ins.then_inc(step, 1)
                dve.wait_ge(step, done)

            dve.wait_ge(slot_ready, NCH)
            dve.tensor_copy(ends[:, :], counts[0:1, :]).then_inc(ends_ready, 1)
            then(dve.tensor_tensor(held[:, :], counts[0:1, :], start[:, :], ALU.subtract))
            then(dve.tensor_tensor(grid[:, :, :], held[:, :].rearrange("p (e o) -> p e o", o=1).broadcast_to(
                [1, E, NTOK // P]), grid[:, :, :], ALU.is_gt))
            then(dve.tensor_reduce(ntiles[:, :], grid[:, :, :], X, ALU.add))
            then(dve.tensor_tensor_scan(upto[:, :], ones8[:, :], ntiles[:, :], 0.0, ALU.mult, ALU.add))

            def each(a):
                return a.rearrange("p (o e) -> p o e", o=1).broadcast_to([1, TILES, E])

            then(dve.tensor_tensor(behind[:, :, :], each(upto[:, :]), jgrid[:, :, :], ALU.is_le))
            then(dve.tensor_reduce(ej[:, :], behind[:, :, :], X, ALU.add))
            then(dve.tensor_tensor(behind[:, :, :], behind[:, :, :], each(ntiles[:, :]), ALU.mult))
            then(dve.tensor_reduce(cj[:, :], behind[:, :, :], X, ALU.add))
            then(dve.tensor_tensor(rj[:, :], jgrid[:, :, 0], cj[:, :], ALU.subtract))
            then(dve.tensor_scalar(rj[:, :], rj[:, :], float(P), None, ALU.mult))
            then(dve.tensor_scalar(rk[:, :], ej[:, :], float(REGION), None, ALU.mult))
            then(dve.tensor_tensor(rj[:, :], rj[:, :], rk[:, :], ALU.add))
            then(dve.tensor_scalar(tile_row[:, :], rj[:, :], float(E * REGION), None, ALU.min))
            then(dve.tensor_scalar(tile_expert[:, :], ej[:, :], float(E - 1), None, ALU.min))


def mlp(nc, psum, ident, experts_in, w1, w2, b1s, b2s, tile_row, tile_expert, dealt, out):
    with ExitStack() as ctx:
        def sb(name, shape, dt=F32):
            return ctx.enter_context(nc.sbuf_tensor(name, shape, dt))

        def sem(name):
            return ctx.enter_context(nc.semaphore(name))

        TU = 8
        NT = TILES // TU
        rows = sb("rows_m", [P, TU, ROWW])
        hn = sb("hn_m", [P, 2, D])
        hT = sb("hT_m", [P, 2, DK, P])
        w1t = sb("w1t", [P, 2, DK * FF])
        warm = sb("warm_m", [P, 1])
        pre = sb("pre", [P, 2, FK, P])
        gT = sb("gT", [P, 2, FK, P])
        o1 = sb("o1", [P, 2, D])
        orow = sb("orow", [P, TU, D])
        token = sb("token_m", [P, TU, 1], I32)

        row_in = [sem(f"row_in{u}") for u in range(TU)]
        h_ready, h_turned, hT_ready = sem("h_ready3"), sem("h_turned3"), sem("hT_ready3")
        up_ready, pre_ready, gelu_ready = sem("up_ready"), sem("pre_ready"), sem("gelu_ready")
        down_ready, w1_ready = sem("down_ready"), sem("w1_ready")
        o1_ready, orow_ready = sem("o1_ready"), sem("orow_ready")
        sent = [sem(f"sent_m{u}") for u in range(TU)]

        block = ctx.enter_context(nc.Block())

        def over_tiles(eng, tile):
            for u in range(TU):
                tile(0, u)
            with eng.Fori(1, NT - 1) as i:
                for u in range(TU):
                    tile(i, u)
            for u in range(TU):
                tile(NT - 1, u)

        def beyond(i, u):
            return isinstance(i, int) and i * TU + u >= TILES

        def entry(eng, table, i, u, most):
            return eng.value_load(table[0:1, bass.ds(lin(i, u, TU, 1), 1)], min_val=0, max_val=most)

        @block.sync
        def _(sp):
            def tile(i, u):
                wait(sp, orow_ready, lin(i, u, TU, 1, 1 - TU))
                row = entry(sp, tile_row, i, u, E * REGION)
                sp.dma_start(rows[:, u], dealt[bass.ds(row, P), :]).then_inc(row_in[u], 16)

            over_tiles(sp, tile)

        @block.gpsimd
        def _(pool):
            passed = sem("pool_passed4")
            def tile(i, u):
                wait_alone(pool, orow_ready, lin(i, u, TU, 1, 1), passed)
                pool.indirect_dma_start(
                    out=out, out_offset=bass.IndirectOffsetOnAxis(ap=token[:, u].bitcast(U32), axis=0),
                    in_=orow[:, u], in_offset=None, bounds_check=NTOK - 1, oob_is_err=False).then_inc(sent[u], 16)

            over_tiles(pool, tile)
            for u in range(TU):
                pool.wait_ge(sent[u], 16 * NT)

        @block.vector
        def _(dve):
            dve.wait_ge(experts_in, WEIGHTS)

            def normed(i, u):
                if beyond(i, u):
                    return
                n, u4 = lin(i, u, TU, 1), u % TU
                wait(dve, row_in[u4], lin(i + u // TU, 0, 1, 16, 16))
                wait(dve, h_turned, n - 1)
                dve.tensor_scalar(hn[:, u % 2], rows[:, u4, 0:D], rows[:, u4, D + 2:D + 3], rows[:, u4, D + 3:D + 4],
                                  ALU.subtract, ALU.mult).then_inc(h_ready, 1)

            def bias(i, u):
                if beyond(i, u):
                    return
                n = lin(i, u, TU, 1)
                e = entry(dve, tile_expert, i, u, E - 1)
                wait(dve, up_ready, n + 1)
                wait(dve, gelu_ready, n - 1)
                dve.tensor_tensor(pre[:, u % 2], psum[:, 2 + u % 2].rearrange("p (k n) -> p k n", k=FK),
                                  b1s[:, bass.ds(e * FK, FK)].rearrange("p (k o) -> p k o", o=1
                                                                        ).broadcast_to([P, FK, P]), ALU.add
                                  ).then_inc(pre_ready, 1)

            def tile(i, u):
                normed(i, u + 3)
                bias(i, u + 1)
                n = lin(i, u, TU, 1)
                e = entry(dve, tile_expert, i, u, E - 1)
                wait(dve, down_ready, n + 1)
                dve.tensor_tensor(o1[:, u % 2], psum[:, 4 + u % 2, 0:D], b2s[:, bass.ds(e * D, D)], ALU.add
                                  ).then_inc(o1_ready, 1)
                wait(dve, sent[u], lin(i, 0, 1, 16))
                dve.tensor_copy(token[:, u], rows[:, u, D + 1:D + 2])
                wait(dve, o1_ready, n + 1)
                dve.scalar_tensor_tensor(out=orow[:, u], in0=o1[:, u % 2], scalar=rows[:, u, D:D + 1], in1=rows[:, u, 0:D],
                                         op0=ALU.mult, op1=ALU.add).then_inc(orow_ready, 1)

            for u in range(3):
                normed(0, u)
            bias(0, 0)
            over_tiles(dve, tile)

        @block.scalar
        def _(act):
            def turned_h(i, u):
                if beyond(i, u):
                    return
                wait(act, h_turned, lin(i, u, TU, 1, 1))
                act.activation(hT[:, u % 2], psum[:, u % 2, 0:DK * P].rearrange("p (k n) -> p k n", k=DK), ACT.Copy
                               ).then_inc(hT_ready, 1)

            def fetch(i, u):
                if beyond(i, u):
                    return
                e = entry(act, tile_expert, i, u, E - 1)
                wait(act, up_ready, lin(i, u, TU, 1, -1))
                act.activation(w1t[:, u % 2], w1[:, bass.ds(e * (DK * FF), DK * FF)], ACT.Copy).then_inc(w1_ready, 1)

            def gelu(i, u):
                if beyond(i, u):
                    return
                wait(act, pre_ready, lin(i, u, TU, 1, 1))
                wait(act, down_ready, lin(i, u, TU, 1, -1))
                act.activation(gT[:, u % 2], pre[:, u % 2], ACT.Gelu).then_inc(gelu_ready, 1)

            def tile(i, u):
                turned_h(i, u + 2)
                gelu(i, u + 1)
                fetch(i, u + 3)

            act.wait_ge(experts_in, WEIGHTS)
            act.activation(warm[:, :], b1s[:, 0:1], ACT.Gelu)
            fetch(0, 0)
            fetch(0, 1)
            turned_h(0, 0)
            turned_h(0, 1)
            gelu(0, 0)
            fetch(0, 2)
            over_tiles(act, tile)

        @block.tensor
        def _(pe):
            def turn_h(i, u):
                if beyond(i, u):
                    return
                n = lin(i, u, TU, 1)
                wait(pe, h_ready, n + 1)
                wait(pe, hT_ready, n - 1)
                for k in range(DK):
                    mm = pe.transpose(psum[:, u % 2, k * P:(k + 1) * P], hn[:, u % 2, k * P:(k + 1) * P], ident[:, :])
                mm.then_inc(h_turned, 1)

            def up(i, u):
                if beyond(i, u):
                    return
                n = lin(i, u, TU, 1)
                wait(pe, w1_ready, n + 1)
                wait(pe, hT_ready, n + 1)
                wait(pe, pre_ready, n - 1)
                for f in range(FK):
                    for k in range(DK):
                        mm = pe.matmul(psum[:, 2 + u % 2, f * P:(f + 1) * P],
                                       w1t[:, u % 2, k * FF + f * P:k * FF + (f + 1) * P], hT[:, u % 2, k],
                                       start=(k == 0), stop=(k == DK - 1))
                mm.then_inc(up_ready, 1)

            def tile(i, u):
                n = lin(i, u, TU, 1)
                turn_h(i, u + 2)
                up(i, u + 1)
                e = entry(pe, tile_expert, i, u, E - 1)
                wait(pe, gelu_ready, n + 1)
                wait(pe, o1_ready, n - 1)
                for k in range(FK):
                    mm = pe.matmul(psum[:, 4 + u % 2, 0:D], gT[:, u % 2, k], w2[:, bass.ds(e * (FK * D) + k * D, D)],
                                   start=(k == 0), stop=(k == FK - 1))
                mm.then_inc(down_ready, 1)

            pe.wait_ge(experts_in, WEIGHTS)
            turn_h(0, 0)
            turn_h(0, 1)
            up(0, 0)
            over_tiles(pe, tile)


_INS = ["L0_attn_x", "L0_attn_ln_w", "L0_attn_ln_b", "L0_attn_wq", "L0_attn_wk", "L0_attn_wv", "L0_attn_wo",
        "L0_ffn_w_red", "L0_ffn_wg", "L0_ffn_W1", "L0_ffn_b1", "L0_ffn_W2", "L0_ffn_b2"]


def kernel(**inputs):
    import numpy as np
    import concourse.bacc as bacc
    from concourse.bass_utils import run_bass_kernel_spmd

    nc = bacc.Bacc("TRN2", target_bir_lowering=False, num_devices=1)
    arrays, args = {}, []
    for name in _INS:
        a = np.ascontiguousarray(inputs[name])
        if name == "L0_attn_x":
            a = a.reshape(NCH, CH, D)
        arrays[name + "_in"] = a
        args.append(nc.dram_tensor(name + "_in", a.shape, mybir.dt.from_np(a.dtype), kind="ExternalInput").ap())
    args.append(nc.dram_tensor("out", (NTOK, D), F32, kind="ExternalOutput").ap())
    build(nc, *args)
    r = run_bass_kernel_spmd(nc, [arrays], core_ids=[0])
    return r.results[0]["out"].reshape(B, S, D)
```
